# Optimizing a Trainium2 kernel written in Bass

```python
import numpy as np
import jax
import jax.numpy as jnp

def _softmax(x, axis=-1):
    return jax.nn.softmax(x, axis=axis)

def _gelu(x):
    return jax.nn.gelu(x, approximate=True)

def _silu(x):
    return jax.nn.silu(x)

def _sigmoid(x):
    return jax.nn.sigmoid(x)

def _layernorm(x, axis=-1, eps=1e-05):
    m = jnp.mean(x, axis=axis, keepdims=True)
    v = jnp.var(x, axis=axis, keepdims=True)
    return (x - m) / jnp.sqrt(v + eps)

def _scatter_add(tgt, idx, src, axis=0):
    return tgt.at[idx].add(src)

def _segment_sum(src, seg, n):
    return jax.ops.segment_sum(src, seg, n)
kernel_name = 'mk_flamingo_gated_d4_seqx_r4_2fc1f2'

def setup_inputs(seed: int=0):
    np.random.seed(seed)
    _w = jnp.asarray

    def _rec_inputs():
        import jax
        import jax.numpy as jnp
        _rk = jax.random.key(seed)
        x = -0.000125 + 0.9999 * jax.random.normal(jax.random.fold_in(_rk, 1), (8, 512, 256), jnp.float32)
        _lenS = 512 - jax.random.randint(jax.random.fold_in(_rk, 7), (8,), 0, max(1, 512 // 4) + 1, jnp.int32)
        _lenS2 = 512 - jax.random.randint(jax.random.fold_in(_rk, 8), (8,), 0, max(1, 512 // 4) + 1, jnp.int32)
        _ctx_1024P = jax.random.normal(jax.random.fold_in(_rk, 11), (8, 16, 256), jnp.float32)
        _ctx_1024c = jax.random.dirichlet(jax.random.fold_in(_rk, 511), 0.3 * jnp.ones((16,), jnp.float32), (8, 512))
        _ctx_1024t = jnp.einsum('bsk,bkd->bsd', _ctx_1024c, _ctx_1024P)
        _ctx_1024t = _ctx_1024t * jax.lax.rsqrt(jnp.mean(jnp.square(_ctx_1024t)) + 1e-12) * 0.953939
        ctx_1024 = -1.52775e-05 + 0.999936 * (_ctx_1024t + 0.3 * jax.random.normal(jax.random.fold_in(_rk, 611), (8, 512, 256), jnp.float32))
        _g = jax.random.normal(jax.random.fold_in(_rk, 9001), (2, 4), jnp.float32)
        _g = jnp.sign(_g) * jnp.maximum(jnp.abs(_g), 1.0) + (_g == 0) * 1.0
        g_xattn = _g[0]
        g_ffn = _g[1]
        return (x, ctx_1024, g_xattn, g_ffn)
    x, ctx_1024, g_xattn, g_ffn = _rec_inputs()

    def _L0_xattn_setup():
        import jax, jax.numpy as jnp
        import numpy as np
        N_HEADS = 4
        IN_FEATURES = 256

        def _channel_attention(qm, km, vm, scale):
            b, n, c = qm.shape
            d = c // N_HEADS
            qh = qm.reshape(b, n, N_HEADS, d).transpose(0, 2, 3, 1)
            kh = km.reshape(b, n, N_HEADS, d).transpose(0, 2, 3, 1)
            vh = vm.reshape(b, n, N_HEADS, d).transpose(0, 2, 3, 1)
            scores = jnp.einsum('bhdn,bhen->bhde', qh, kh) * scale
            attn = jax.nn.softmax(scores, axis=-1)
            out = jnp.einsum('bhde,bhen->bhdn', attn, vh)
            return out.transpose(0, 3, 1, 2).reshape(b, n, c)
        key = jax.random.key(seed)
        ks = jax.random.split(key, 20)
        B, HW, C = (2, 4096, 256)
        inp = {'q': jax.random.normal(ks[0], (B, HW, C), dtype=jnp.float32), 'k': jax.random.normal(ks[1], (B, HW, C), dtype=jnp.float32), 'v': jax.random.normal(ks[2], (B, HW, C), dtype=jnp.float32)}
        names = ['wqg', 'bqg', 'wkg', 'bkg', 'wvg', 'bvg', 'wql', 'bql', 'wkl', 'bkl', 'wvl', 'bvl', 'wp', 'bp']
        for i, n in enumerate(names):
            inp[n] = jax.random.normal(ks[3 + i], (C,), dtype=jnp.float32)
        return inp
    _L0_xattn_all = _L0_xattn_setup()
    _L0_xattn_in = {k: v for k, v in _L0_xattn_all.items() if k in ('wqg', 'bqg', 'wkg', 'bkg', 'wvg', 'bvg', 'wql', 'bql', 'wkl', 'bkl', 'wvl', 'bvl', 'wp', 'bp')}
    del _L0_xattn_all

    def _L0_ffn_setup():
        import jax, jax.numpy as jnp
        import numpy as np
        D = 256
        H = 16
        DH = D // H
        DC = D // 4
        HID = 512
        G = 2
        EPG = 4
        E = G * EPG
        TOPK = 2
        EPS = 1e-06
        B, T = (2, 512)

        def _rope_sincos(t, dh):
            inv_freq = 1.0 / 10000.0 ** (jnp.arange(0, dh, 2, dtype=jnp.float32) / dh)
            ang = jnp.arange(t, dtype=jnp.float32)[:, None] * inv_freq[None, :]
            return (jnp.sin(ang), jnp.cos(ang))

        def _apply_rope(x, sin, cos):
            x1 = x[..., ::2]
            x2 = x[..., 1::2]
            r = jnp.stack([x1 * cos - x2 * sin, x1 * sin + x2 * cos], axis=-1)
            return r.reshape(x.shape)

        def _swiglu(x):
            a, b = jnp.split(x, 2, axis=-1)
            return jax.nn.silu(a) * b

        def _rmsnorm(x, w):
            return x * jax.lax.rsqrt(jnp.mean(x * x, axis=-1, keepdims=True) + EPS) * w
        key = jax.random.key(seed)
        ks = jax.random.split(key, 14)
        s = 0.02
        return {'src': jax.random.normal(ks[0], (B, T, D), jnp.float32), 'Wq': jax.random.normal(ks[1], (D, D), jnp.float32) * s, 'Wk_c': jax.random.normal(ks[2], (D, DC), jnp.float32) * s, 'Wv_c': jax.random.normal(ks[3], (D, DC), jnp.float32) * s, 'Wk': jax.random.normal(ks[4], (DC, D), jnp.float32) * s, 'Wv': jax.random.normal(ks[5], (DC, D), jnp.float32) * s, 'Wo': jax.random.normal(ks[6], (D, D), jnp.float32) * s, 'W_shared_in': jax.random.normal(ks[7], (D, 2 * HID), jnp.float32) * s, 'W_shared_out': jax.random.normal(ks[8], (HID, D), jnp.float32) * s, 'W1_shared': jax.random.normal(ks[9], (D, 2 * HID), jnp.float32) * s, 'W2_experts': jax.random.normal(ks[10], (E, HID, D), jnp.float32) * s, 'Wg_gate': jax.random.normal(ks[11], (D, G), jnp.float32) * s, 'We_gate': jax.random.normal(ks[12], (D, E), jnp.float32) * s, 'group_bias': jnp.zeros((G,), jnp.float32), 'expert_bias': jnp.zeros((E,), jnp.float32), 'norm1_w': jnp.ones((D,), jnp.float32), 'norm2_w': jnp.ones((D,), jnp.float32)}
    _L0_ffn_all = _L0_ffn_setup()
    _L0_ffn_in = {k: v for k, v in _L0_ffn_all.items() if k in ('Wq', 'Wk_c', 'Wv_c', 'Wk', 'Wv', 'Wo', 'W_shared_in', 'W_shared_out', 'W1_shared', 'W2_experts', 'Wg_gate', 'We_gate', 'group_bias', 'expert_bias', 'norm1_w', 'norm2_w')}
    del _L0_ffn_all

    def _L1_xattn_setup():
        import jax, jax.numpy as jnp
        import numpy as np
        import math
        B, S, DM, H = (2, 512, 256, 16)
        HD = DM // H
        key = jax.random.key(seed)
        ks = jax.random.split(key, 7)
        mk = lambda k, shp, s=1.0: jax.random.normal(k, shp, dtype=jnp.float32) * s
        return {'q': mk(ks[0], (B, S, DM)), 'k': mk(ks[1], (B, S, DM)), 'v': mk(ks[2], (B, S, DM)), 'wq': mk(ks[3], (DM, DM), 0.02), 'wk': mk(ks[4], (DM, DM), 0.02), 'wv': mk(ks[5], (DM, DM), 0.02), 'wo': mk(ks[6], (DM, DM), 0.02)}
    _L1_xattn_all = _L1_xattn_setup()
    _L1_xattn_in = {k: v for k, v in _L1_xattn_all.items() if k in ('wq', 'wk', 'wv', 'wo')}
    del _L1_xattn_all

    def _L1_ffn_setup():
        import jax, jax.numpy as jnp
        import numpy as np
        N_EXPERT_CAPACITY = 2
        key = jax.random.key(seed)
        k1, k2, k3, k4 = jax.random.split(key, 4)
        B, S, D, E, F = (8, 256, 256, 8, 512)
        x = jax.random.normal(k1, (B, S, D), dtype=jnp.float32)
        choice_w = jax.random.uniform(k2, (E, D), dtype=jnp.float32, minval=-1.0, maxval=1.0) * (1.0 / np.sqrt(D))
        w1 = jax.random.uniform(k3, (E, D, F), dtype=jnp.float32, minval=-1.0, maxval=1.0) * (1.0 / np.sqrt(D))
        w2 = jax.random.uniform(k4, (E, F, D), dtype=jnp.float32, minval=-1.0, maxval=1.0) * (1.0 / np.sqrt(F))
        return {'x': x, 'choice_w': choice_w, 'w1': w1, 'w2': w2}
    _L1_ffn_all = _L1_ffn_setup()
    _L1_ffn_in = {k: v for k, v in _L1_ffn_all.items() if k in ('choice_w', 'w1', 'w2')}
    del _L1_ffn_all

    def _L2_xattn_setup():
        import jax, jax.numpy as jnp
        import numpy as np
        B, T, S, D = (4, 512, 1024, 256)
        TOP_K = 32

        def _read(query, mem_state, top_k, Wq, bq, Wk, bk, Wv, bv, Wo, bo):
            b, t, d = query.shape
            s = mem_state.shape[1]
            scale = 1.0 / np.sqrt(d)
            q = query @ Wq.T + bq
            k = mem_state @ Wk.T + bk
            v = mem_state @ Wv.T + bv
            scores = jnp.einsum('btd,bsd->bts', q, k) * scale
            if top_k < s:
                vals, idx = jax.lax.top_k(scores, top_k)
                b_ix = jnp.arange(b)[:, None, None]
                t_ix = jnp.arange(t)[None, :, None]
                masked = jnp.full_like(scores, -jnp.inf)
                scores = masked.at[b_ix, t_ix, idx].set(vals)
            attn = jax.nn.softmax(scores, axis=-1)
            ctx = jnp.einsum('bts,bsd->btd', attn, v)
            return ctx @ Wo.T + bo
        key = jax.random.key(seed)
        ks = jax.random.split(key, 12)
        std = 0.02
        inp = {'query': jax.random.normal(ks[0], (B, T, D), dtype=jnp.float32), 'mem_state': jax.random.normal(ks[1], (B, S, D), dtype=jnp.float32), 'top_k': TOP_K, 'Wq': jax.random.normal(ks[2], (D, D), dtype=jnp.float32) * std, 'bq': jnp.zeros((D,), dtype=jnp.float32), 'Wk': jax.random.normal(ks[3], (D, D), dtype=jnp.float32) * std, 'bk': jnp.zeros((D,), dtype=jnp.float32), 'Wv': jax.random.normal(ks[4], (D, D), dtype=jnp.float32) * std, 'bv': jnp.zeros((D,), dtype=jnp.float32), 'Wo': jax.random.normal(ks[5], (D, D), dtype=jnp.float32) * std, 'bo': jnp.zeros((D,), dtype=jnp.float32)}
        return inp
    _L2_xattn_all = _L2_xattn_setup()
    _L2_xattn_in = {k: v for k, v in _L2_xattn_all.items() if k in ('Wq', 'bq', 'Wk', 'bk', 'Wv', 'bv', 'Wo', 'bo')}
    del _L2_xattn_all

    def _L2_ffn_setup():
        import jax, jax.numpy as jnp
        import numpy as np
        D = 256
        F = 256
        E = 8
        K = 2
        B, T = (2, 512)

        def _moe_forward(x, router_w, w1, w2, shared_gate_up, shared_down, shared_gate_w):
            b, t, d = x.shape
            xf = x.reshape(-1, d)
            n = xf.shape[0]
            logits = xf @ router_w
            probs = jax.nn.softmax(logits, axis=-1)
            topw, topi = jax.lax.top_k(probs, K)
            combine = jnp.zeros((n, E), dtype=probs.dtype).at[jnp.arange(n)[:, None], topi].add(topw)
            h = jax.nn.silu(jnp.einsum('nd,edf->nef', xf, w1))
            ye = jnp.einsum('nef,efd->ned', h, w2)
            routed = jnp.einsum('ne,ned->nd', combine, ye)
            gu = xf @ shared_gate_up
            gate, up = (gu[:, :F], gu[:, F:])
            shared = jax.nn.silu(gate) * up @ shared_down
            shared = jax.nn.sigmoid(xf @ shared_gate_w) * shared
            return (routed + shared).reshape(b, t, d)
        key = jax.random.key(seed)
        ks = jax.random.split(key, 7)
        std = 0.02
        x = jax.random.normal(ks[0], (B, T, D), dtype=jnp.float32)
        router_w = jax.random.normal(ks[1], (D, E), dtype=jnp.float32) * std
        w1 = jax.random.normal(ks[2], (E, D, F), dtype=jnp.float32) * std
        w2 = jax.random.normal(ks[3], (E, F, D), dtype=jnp.float32) * std
        shared_gate_up = jax.random.normal(ks[4], (D, 2 * F), dtype=jnp.float32) * std
        shared_down = jax.random.normal(ks[5], (F, D), dtype=jnp.float32) * std
        shared_gate_w = jax.random.normal(ks[6], (D, 1), dtype=jnp.float32) * std
        return {'x': x, 'router_w': router_w, 'w1': w1, 'w2': w2, 'shared_gate_up': shared_gate_up, 'shared_down': shared_down, 'shared_gate_w': shared_gate_w}
    _L2_ffn_all = _L2_ffn_setup()
    _L2_ffn_in = {k: v for k, v in _L2_ffn_all.items() if k in ('router_w', 'w1', 'w2', 'shared_gate_up', 'shared_down', 'shared_gate_w')}
    del _L2_ffn_all

    def _L3_xattn_setup():
        import jax, jax.numpy as jnp
        import numpy as np
        HEADS = 16
        D_MODEL = 256
        D_K = D_MODEL // HEADS
        B, S = (2, 512)
        key = jax.random.key(seed)
        ks = jax.random.split(key, 8)
        scale = 1.0 / np.sqrt(D_MODEL)
        return {'q': jax.random.normal(ks[0], (B, S, D_MODEL), jnp.float32), 'k': jax.random.normal(ks[1], (B, S, D_MODEL), jnp.float32), 'v': jax.random.normal(ks[2], (B, S, D_MODEL), jnp.float32), 'Wq': jax.random.normal(ks[3], (D_MODEL, D_MODEL), jnp.float32) * scale, 'bq': jnp.zeros((D_MODEL,), jnp.float32), 'Wk': jax.random.normal(ks[4], (D_MODEL, D_MODEL), jnp.float32) * scale, 'bk': jnp.zeros((D_MODEL,), jnp.float32), 'Wv': jax.random.normal(ks[5], (D_MODEL, D_MODEL), jnp.float32) * scale, 'bv': jnp.zeros((D_MODEL,), jnp.float32), 'Wo': jax.random.normal(ks[6], (D_MODEL, D_MODEL), jnp.float32) * scale, 'bo': jnp.zeros((D_MODEL,), jnp.float32)}
    _L3_xattn_all = _L3_xattn_setup()
    _L3_xattn_in = {k: v for k, v in _L3_xattn_all.items() if k in ('Wq', 'bq', 'Wk', 'bk', 'Wv', 'bv', 'Wo', 'bo')}
    del _L3_xattn_all

    def _L3_ffn_setup():
        import jax, jax.numpy as jnp
        import numpy as np
        N_EXPERTS = 16
        TOP_K = 4
        HIDDEN = 256
        INTER = 128
        B, S = (2, 256)
        key = jax.random.key(seed)
        k1, k2, k3, k4, k5 = jax.random.split(key, 5)
        return {'hidden_states': jax.random.normal(k1, (B, S, HIDDEN), dtype=jnp.float32), 'gate_w': jax.random.normal(k2, (N_EXPERTS, HIDDEN), dtype=jnp.float32) * 0.02, 'w1': jax.random.normal(k3, (N_EXPERTS, HIDDEN, INTER), dtype=jnp.float32) * 0.02, 'w3': jax.random.normal(k4, (N_EXPERTS, HIDDEN, INTER), dtype=jnp.float32) * 0.02, 'w2': jax.random.normal(k5, (N_EXPERTS, INTER, HIDDEN), dtype=jnp.float32) * 0.02}
    _L3_ffn_all = _L3_ffn_setup()
    _L3_ffn_in = {k: v for k, v in _L3_ffn_all.items() if k in ('gate_w', 'w1', 'w3', 'w2')}
    del _L3_ffn_all
    return {'x': x, 'ctx_1024': ctx_1024, 'g_xattn': g_xattn, 'g_ffn': g_ffn, 'L0_xattn_wqg': _L0_xattn_in['wqg'], 'L0_xattn_bqg': _L0_xattn_in['bqg'], 'L0_xattn_wkg': _L0_xattn_in['wkg'], 'L0_xattn_bkg': _L0_xattn_in['bkg'], 'L0_xattn_wvg': _L0_xattn_in['wvg'], 'L0_xattn_bvg': _L0_xattn_in['bvg'], 'L0_xattn_wql': _L0_xattn_in['wql'], 'L0_xattn_bql': _L0_xattn_in['bql'], 'L0_xattn_wkl': _L0_xattn_in['wkl'], 'L0_xattn_bkl': _L0_xattn_in['bkl'], 'L0_xattn_wvl': _L0_xattn_in['wvl'], 'L0_xattn_bvl': _L0_xattn_in['bvl'], 'L0_xattn_wp': _L0_xattn_in['wp'], 'L0_xattn_bp': _L0_xattn_in['bp'], 'L0_ffn_Wq': _L0_ffn_in['Wq'], 'L0_ffn_Wk_c': _L0_ffn_in['Wk_c'], 'L0_ffn_Wv_c': _L0_ffn_in['Wv_c'], 'L0_ffn_Wk': _L0_ffn_in['Wk'], 'L0_ffn_Wv': _L0_ffn_in['Wv'], 'L0_ffn_Wo': _L0_ffn_in['Wo'], 'L0_ffn_W_shared_in': _L0_ffn_in['W_shared_in'], 'L0_ffn_W_shared_out': _L0_ffn_in['W_shared_out'], 'L0_ffn_W1_shared': _L0_ffn_in['W1_shared'], 'L0_ffn_W2_experts': _L0_ffn_in['W2_experts'], 'L0_ffn_Wg_gate': _L0_ffn_in['Wg_gate'], 'L0_ffn_We_gate': _L0_ffn_in['We_gate'], 'L0_ffn_group_bias': _L0_ffn_in['group_bias'], 'L0_ffn_expert_bias': _L0_ffn_in['expert_bias'], 'L0_ffn_norm1_w': _L0_ffn_in['norm1_w'], 'L0_ffn_norm2_w': _L0_ffn_in['norm2_w'], 'L1_xattn_wq': _L1_xattn_in['wq'], 'L1_xattn_wk': _L1_xattn_in['wk'], 'L1_xattn_wv': _L1_xattn_in['wv'], 'L1_xattn_wo': _L1_xattn_in['wo'], 'L1_ffn_choice_w': _L1_ffn_in['choice_w'], 'L1_ffn_w1': _L1_ffn_in['w1'], 'L1_ffn_w2': _L1_ffn_in['w2'], 'L2_xattn_Wq': _L2_xattn_in['Wq'], 'L2_xattn_bq': _L2_xattn_in['bq'], 'L2_xattn_Wk': _L2_xattn_in['Wk'], 'L2_xattn_bk': _L2_xattn_in['bk'], 'L2_xattn_Wv': _L2_xattn_in['Wv'], 'L2_xattn_bv': _L2_xattn_in['bv'], 'L2_xattn_Wo': _L2_xattn_in['Wo'], 'L2_xattn_bo': _L2_xattn_in['bo'], 'L2_ffn_router_w': _L2_ffn_in['router_w'], 'L2_ffn_w1': _L2_ffn_in['w1'], 'L2_ffn_w2': _L2_ffn_in['w2'], 'L2_ffn_shared_gate_up': _L2_ffn_in['shared_gate_up'], 'L2_ffn_shared_down': _L2_ffn_in['shared_down'], 'L2_ffn_shared_gate_w': _L2_ffn_in['shared_gate_w'], 'L3_xattn_Wq': _L3_xattn_in['Wq'], 'L3_xattn_bq': _L3_xattn_in['bq'], 'L3_xattn_Wk': _L3_xattn_in['Wk'], 'L3_xattn_bk': _L3_xattn_in['bk'], 'L3_xattn_Wv': _L3_xattn_in['Wv'], 'L3_xattn_bv': _L3_xattn_in['bv'], 'L3_xattn_Wo': _L3_xattn_in['Wo'], 'L3_xattn_bo': _L3_xattn_in['bo'], 'L3_ffn_gate_w': _L3_ffn_in['gate_w'], 'L3_ffn_w1': _L3_ffn_in['w1'], 'L3_ffn_w3': _L3_ffn_in['w3'], 'L3_ffn_w2': _L3_ffn_in['w2']}

def reference(x, ctx_1024, g_xattn, g_ffn, L0_xattn_wqg, L0_xattn_bqg, L0_xattn_wkg, L0_xattn_bkg, L0_xattn_wvg, L0_xattn_bvg, L0_xattn_wql, L0_xattn_bql, L0_xattn_wkl, L0_xattn_bkl, L0_xattn_wvl, L0_xattn_bvl, L0_xattn_wp, L0_xattn_bp, L0_ffn_Wq, L0_ffn_Wk_c, L0_ffn_Wv_c, L0_ffn_Wk, L0_ffn_Wv, L0_ffn_Wo, L0_ffn_W_shared_in, L0_ffn_W_shared_out, L0_ffn_W1_shared, L0_ffn_W2_experts, L0_ffn_Wg_gate, L0_ffn_We_gate, L0_ffn_group_bias, L0_ffn_expert_bias, L0_ffn_norm1_w, L0_ffn_norm2_w, L1_xattn_wq, L1_xattn_wk, L1_xattn_wv, L1_xattn_wo, L1_ffn_choice_w, L1_ffn_w1, L1_ffn_w2, L2_xattn_Wq, L2_xattn_bq, L2_xattn_Wk, L2_xattn_bk, L2_xattn_Wv, L2_xattn_bv, L2_xattn_Wo, L2_xattn_bo, L2_ffn_router_w, L2_ffn_w1, L2_ffn_w2, L2_ffn_shared_gate_up, L2_ffn_shared_down, L2_ffn_shared_gate_w, L3_xattn_Wq, L3_xattn_bq, L3_xattn_Wk, L3_xattn_bk, L3_xattn_Wv, L3_xattn_bv, L3_xattn_Wo, L3_xattn_bo, L3_ffn_gate_w, L3_ffn_w1, L3_ffn_w3, L3_ffn_w2):
    import jax
    import jax.numpy as jnp

    def _L0_xattn_ref(q, k, v, wqg, bqg, wkg, bkg, wvg, bvg, wql, bql, wkl, bkl, wvl, bvl, wp, bp):
        import jax, jax.numpy as jnp
        import numpy as np
        N_HEADS = 4
        IN_FEATURES = 256

        def _channel_attention(qm, km, vm, scale):
            b, n, c = qm.shape
            d = c // N_HEADS
            qh = qm.reshape(b, n, N_HEADS, d).transpose(0, 2, 3, 1)
            kh = km.reshape(b, n, N_HEADS, d).transpose(0, 2, 3, 1)
            vh = vm.reshape(b, n, N_HEADS, d).transpose(0, 2, 3, 1)
            scores = jnp.einsum('bhdn,bhen->bhde', qh, kh) * scale
            attn = jax.nn.softmax(scores, axis=-1)
            out = jnp.einsum('bhde,bhen->bhdn', attn, vh)
            return out.transpose(0, 3, 1, 2).reshape(b, n, c)
        scale = IN_FEATURES ** (-0.5)
        att_global = _channel_attention(q * wqg + bqg, k * wkg + bkg, v * wvg + bvg, scale)
        att_local = _channel_attention(q * wql + bql, k * wkl + bkl, v * wvl + bvl, scale)
        att = att_global + att_local
        return 2.0 * att * wp + bp

    def _L0_ffn_ref(src, Wq, Wk_c, Wv_c, Wk, Wv, Wo, W_shared_in, W_shared_out, W1_shared, W2_experts, Wg_gate, We_gate, group_bias, expert_bias, norm1_w, norm2_w):
        import jax, jax.numpy as jnp
        import numpy as np
        D = 256
        H = 16
        DH = D // H
        DC = D // 4
        HID = 512
        G = 2
        EPG = 4
        E = G * EPG
        TOPK = 2
        EPS = 1e-06
        B, T = (2, 512)

        def _rope_sincos(t, dh):
            inv_freq = 1.0 / 10000.0 ** (jnp.arange(0, dh, 2, dtype=jnp.float32) / dh)
            ang = jnp.arange(t, dtype=jnp.float32)[:, None] * inv_freq[None, :]
            return (jnp.sin(ang), jnp.cos(ang))

        def _apply_rope(x, sin, cos):
            x1 = x[..., ::2]
            x2 = x[..., 1::2]
            r = jnp.stack([x1 * cos - x2 * sin, x1 * sin + x2 * cos], axis=-1)
            return r.reshape(x.shape)

        def _swiglu(x):
            a, b = jnp.split(x, 2, axis=-1)
            return jax.nn.silu(a) * b

        def _rmsnorm(x, w):
            return x * jax.lax.rsqrt(jnp.mean(x * x, axis=-1, keepdims=True) + EPS) * w
        Bb, Tt, C = src.shape
        q = (src @ Wq).reshape(Bb, Tt, H, DH).transpose(0, 2, 1, 3)
        k = (src @ Wk_c @ Wk).reshape(Bb, Tt, H, DH).transpose(0, 2, 1, 3)
        v = (src @ Wv_c @ Wv).reshape(Bb, Tt, H, DH).transpose(0, 2, 1, 3)
        sin, cos = _rope_sincos(Tt, DH)
        q = _apply_rope(q, sin, cos)
        k = _apply_rope(k, sin, cos)
        attn = jnp.einsum('bhqd,bhkd->bhqk', q, k) / np.sqrt(DH).astype(np.float32)
        attn = jax.nn.softmax(attn, axis=-1)
        sa = jnp.einsum('bhqk,bhkd->bhqd', attn, v)
        sa = sa.transpose(0, 2, 1, 3).reshape(Bb, Tt, C) @ Wo
        x = _rmsnorm(src + sa, norm1_w)
        S = Bb * Tt
        flat = x.reshape(S, C)
        shared = _swiglu(flat @ W_shared_in) @ W_shared_out
        g_probs = jax.nn.softmax(flat @ Wg_gate + group_bias, -1)
        g_idx = jnp.argmax(g_probs, axis=-1)
        e_logits = flat @ We_gate + expert_bias
        e_group = jnp.arange(E) // EPG
        in_group = e_group[None, :] == g_idx[:, None]
        e_probs = jax.nn.softmax(jnp.where(in_group, e_logits, -jnp.inf), -1)
        g_prob = jnp.take_along_axis(g_probs, g_idx[:, None], axis=1)
        p_expert = e_probs * g_prob
        topv, topi = jax.lax.top_k(p_expert, TOPK)
        w = jnp.zeros((S, E), flat.dtype).at[jnp.arange(S)[:, None], topi].set(topv)
        h = _swiglu(flat @ W1_shared)
        routed = jnp.zeros_like(shared)
        for e in range(E):
            routed = routed + h @ W2_experts[e] * w[:, e:e + 1]
        out = x + (shared + routed).reshape(Bb, Tt, C)
        return _rmsnorm(out, norm2_w)

    def _L1_xattn_ref(q, k, v, wq, wk, wv, wo):
        import jax, jax.numpy as jnp
        import numpy as np
        import math
        B, S, DM, H = (2, 512, 256, 16)
        HD = DM // H
        bsz, seqlen, _ = q.shape

        def proj(x, w):
            y = jnp.einsum('bsd,ed->bse', x, w)
            return y.reshape(bsz, seqlen, H, HD).transpose(0, 2, 1, 3)
        xq, xk, xv = (proj(q, wq), proj(k, wk), proj(v, wv))
        scores = jnp.einsum('bhqd,bhkd->bhqk', xq, xk) / math.sqrt(HD)
        causal = jnp.tril(jnp.ones((seqlen, seqlen), dtype=bool))
        scores = jnp.where(causal[None, None], scores, -jnp.inf)
        probs = jax.nn.softmax(scores.astype(jnp.float32), axis=-1).astype(xq.dtype)
        out = jnp.einsum('bhqk,bhkd->bhqd', probs, xv)
        out = out.transpose(0, 2, 1, 3).reshape(bsz, seqlen, DM)
        return jnp.einsum('bsd,ed->bse', out, wo)

    def _L1_ffn_ref(x, choice_w, w1, w2):
        import jax, jax.numpy as jnp
        import numpy as np
        N_EXPERT_CAPACITY = 2
        B, S, D = x.shape
        E = choice_w.shape[0]
        k = S * N_EXPERT_CAPACITY // E
        probs = jax.nn.softmax(jnp.einsum('bsd,ed->bse', x, choice_w), axis=-1)
        G, I = jax.lax.top_k(jnp.swapaxes(probs, -1, -2), k)
        x_in = jnp.take_along_axis(x[:, None, :, :], I[..., None], axis=2)
        h = jax.nn.silu(jnp.einsum('bekd,edf->bekf', x_in, w1))
        x_mlp = jnp.einsum('bekf,efd->bekd', h, w2)
        b_idx = jnp.arange(B)[:, None, None]
        out = jnp.zeros_like(x).at[b_idx, I].add(G[..., None] * x_mlp)
        return out

    def _L2_xattn_ref(query, mem_state, top_k, Wq, bq, Wk, bk, Wv, bv, Wo, bo):
        import jax, jax.numpy as jnp
        import numpy as np
        B, T, S, D = (4, 512, 1024, 256)
        TOP_K = 32

        def _read(query, mem_state, top_k, Wq, bq, Wk, bk, Wv, bv, Wo, bo):
            b, t, d = query.shape
            s = mem_state.shape[1]
            scale = 1.0 / np.sqrt(d)
            q = query @ Wq.T + bq
            k = mem_state @ Wk.T + bk
            v = mem_state @ Wv.T + bv
            scores = jnp.einsum('btd,bsd->bts', q, k) * scale
            if top_k < s:
                vals, idx = jax.lax.top_k(scores, top_k)
                b_ix = jnp.arange(b)[:, None, None]
                t_ix = jnp.arange(t)[None, :, None]
                masked = jnp.full_like(scores, -jnp.inf)
                scores = masked.at[b_ix, t_ix, idx].set(vals)
            attn = jax.nn.softmax(scores, axis=-1)
            ctx = jnp.einsum('bts,bsd->btd', attn, v)
            return ctx @ Wo.T + bo
        return _read(query, mem_state, top_k, Wq, bq, Wk, bk, Wv, bv, Wo, bo)

    def _L2_ffn_ref(x, router_w, w1, w2, shared_gate_up, shared_down, shared_gate_w):
        import jax, jax.numpy as jnp
        import numpy as np
        D = 256
        F = 256
        E = 8
        K = 2
        B, T = (2, 512)

        def _moe_forward(x, router_w, w1, w2, shared_gate_up, shared_down, shared_gate_w):
            b, t, d = x.shape
            xf = x.reshape(-1, d)
            n = xf.shape[0]
            logits = xf @ router_w
            probs = jax.nn.softmax(logits, axis=-1)
            topw, topi = jax.lax.top_k(probs, K)
            combine = jnp.zeros((n, E), dtype=probs.dtype).at[jnp.arange(n)[:, None], topi].add(topw)
            h = jax.nn.silu(jnp.einsum('nd,edf->nef', xf, w1))
            ye = jnp.einsum('nef,efd->ned', h, w2)
            routed = jnp.einsum('ne,ned->nd', combine, ye)
            gu = xf @ shared_gate_up
            gate, up = (gu[:, :F], gu[:, F:])
            shared = jax.nn.silu(gate) * up @ shared_down
            shared = jax.nn.sigmoid(xf @ shared_gate_w) * shared
            return (routed + shared).reshape(b, t, d)
        return _moe_forward(x, router_w, w1, w2, shared_gate_up, shared_down, shared_gate_w)

    def _L3_xattn_ref(q, k, v, Wq, bq, Wk, bk, Wv, bv, Wo, bo):
        import jax, jax.numpy as jnp
        import numpy as np
        HEADS = 16
        D_MODEL = 256
        D_K = D_MODEL // HEADS
        B, S = (2, 512)
        bs = q.shape[0]

        def proj(x, W, b):
            return (x @ W.T + b).reshape(bs, -1, HEADS, D_K).transpose(0, 2, 1, 3)
        qh = proj(q, Wq, bq)
        kh = proj(k, Wk, bk)
        vh = proj(v, Wv, bv)
        scores = jnp.einsum('bhqd,bhkd->bhqk', qh, kh) / jnp.sqrt(jnp.float32(D_K))
        attn = jax.nn.softmax(scores, axis=-1)
        out = jnp.einsum('bhqk,bhkd->bhqd', attn, vh)
        out = out.transpose(0, 2, 1, 3).reshape(bs, -1, D_MODEL)
        return out @ Wo.T + bo

    def _L3_ffn_ref(hidden_states, gate_w, w1, w3, w2):
        import jax, jax.numpy as jnp
        import numpy as np
        N_EXPERTS = 16
        TOP_K = 4
        HIDDEN = 256
        INTER = 128
        B, S = (2, 256)
        'DeepseekV3 MoE adapter forward: router -> sparse scores -> expert GLU MLP -> combine.'
        b, s, h = hidden_states.shape
        x = hidden_states.reshape(-1, h)
        logits = jnp.einsum('th,eh->te', x, gate_w)
        probs = jax.nn.softmax(logits, axis=-1)
        topk_w, topk_idx = jax.lax.top_k(probs, TOP_K)
        topk_w = topk_w / jnp.sum(topk_w, axis=-1, keepdims=True)
        one_hot = (topk_idx[..., None] == jnp.arange(N_EXPERTS)).astype(topk_w.dtype)
        scores = jnp.einsum('tk,tke->te', topk_w, one_hot)
        g = jnp.einsum('th,ehi->tei', x, w1)
        u = jnp.einsum('th,ehi->tei', x, w3)
        act = jax.nn.silu(g) * u
        expert_out = jnp.einsum('tei,eih->teh', act, w2)
        out = jnp.einsum('teh,te->th', expert_out, scores)
        return out.reshape(b, s, h)
    x = x + jnp.tanh(g_xattn[0]) * _L0_xattn_ref(_layernorm(x, axis=-1), ctx_1024, ctx_1024, L0_xattn_wqg, L0_xattn_bqg, L0_xattn_wkg, L0_xattn_bkg, L0_xattn_wvg, L0_xattn_bvg, L0_xattn_wql, L0_xattn_bql, L0_xattn_wkl, L0_xattn_bkl, L0_xattn_wvl, L0_xattn_bvl, L0_xattn_wp, L0_xattn_bp)
    x = x + jnp.tanh(g_ffn[0]) * _L0_ffn_ref(_layernorm(x, axis=-1), L0_ffn_Wq, L0_ffn_Wk_c, L0_ffn_Wv_c, L0_ffn_Wk, L0_ffn_Wv, L0_ffn_Wo, L0_ffn_W_shared_in, L0_ffn_W_shared_out, L0_ffn_W1_shared, L0_ffn_W2_experts, L0_ffn_Wg_gate, L0_ffn_We_gate, L0_ffn_group_bias, L0_ffn_expert_bias, L0_ffn_norm1_w, L0_ffn_norm2_w)
    x = x + jnp.tanh(g_xattn[1]) * _L1_xattn_ref(_layernorm(x, axis=-1), ctx_1024, ctx_1024, L1_xattn_wq, L1_xattn_wk, L1_xattn_wv, L1_xattn_wo)
    x = x + jnp.tanh(g_ffn[1]) * _L1_ffn_ref(_layernorm(x, axis=-1), L1_ffn_choice_w, L1_ffn_w1, L1_ffn_w2)
    x = x + jnp.tanh(g_xattn[2]) * _L2_xattn_ref(_layernorm(x, axis=-1), ctx_1024, 32, L2_xattn_Wq, L2_xattn_bq, L2_xattn_Wk, L2_xattn_bk, L2_xattn_Wv, L2_xattn_bv, L2_xattn_Wo, L2_xattn_bo)
    x = x + jnp.tanh(g_ffn[2]) * _L2_ffn_ref(_layernorm(x, axis=-1), L2_ffn_router_w, L2_ffn_w1, L2_ffn_w2, L2_ffn_shared_gate_up, L2_ffn_shared_down, L2_ffn_shared_gate_w)
    x = x + jnp.tanh(g_xattn[3]) * _L3_xattn_ref(_layernorm(x, axis=-1), ctx_1024, ctx_1024, L3_xattn_Wq, L3_xattn_bq, L3_xattn_Wk, L3_xattn_bk, L3_xattn_Wv, L3_xattn_bv, L3_xattn_Wo, L3_xattn_bo)
    x = x + jnp.tanh(g_ffn[3]) * _L3_ffn_ref(_layernorm(x, axis=-1), L3_ffn_gate_w, L3_ffn_w1, L3_ffn_w3, L3_ffn_w2)
    return x

_drawn_inputs = setup_inputs


def setup_inputs(seed=0):
    import zlib

    import numpy as np

    out = dict(_drawn_inputs(seed))
    spreads = {'L0_ffn_group_bias': (0.0, 0.8),
     'L0_ffn_expert_bias': (0.0, 0.8),
     'L0_ffn_norm1_w': (1.0, 0.2),
     'L0_ffn_norm2_w': (1.0, 0.2),
     'L2_xattn_bq': (0.0, 0.8),
     'L2_xattn_bk': (0.0, 2.0),
     'L2_xattn_bv': (0.0, 0.8),
     'L2_xattn_bo': (0.0, 0.302),
     'L3_xattn_bq': (0.0, 2.0),
     'L3_xattn_bk': (0.0, 2.0),
     'L3_xattn_bv': (0.0, 0.337),
     'L3_xattn_bo': (0.0, 0.309)}
    factors = {'g_ffn': 8.0,
     'L0_ffn_Wq': 8.0,
     'L0_ffn_Wk_c': 8.0,
     'L0_ffn_Wv_c': 8.0,
     'L0_ffn_Wk': 8.0,
     'L0_ffn_Wv': 8.0,
     'L0_ffn_Wo': 8.0,
     'L0_ffn_W_shared_in': 7.781,
     'L0_ffn_W_shared_out': 7.921,
     'L0_ffn_W1_shared': 8.0,
     'L0_ffn_W2_experts': 8.0,
     'L0_ffn_Wg_gate': 8.0,
     'L0_ffn_We_gate': 8.0,
     'L1_xattn_wq': 8.0,
     'L1_xattn_wk': 8.0,
     'L1_xattn_wv': 3.332,
     'L1_xattn_wo': 3.287,
     'L1_ffn_choice_w': 3.708,
     'L1_ffn_w1': 3.572,
     'L1_ffn_w2': 3.408,
     'L2_xattn_Wq': 4.975,
     'L2_xattn_Wk': 4.38,
     'L2_xattn_Wv': 2.993,
     'L2_xattn_Wo': 2.77,
     'L2_ffn_router_w': 8.0,
     'L2_ffn_w1': 8.0,
     'L2_ffn_w2': 8.0,
     'L2_ffn_shared_gate_up': 8.0,
     'L2_ffn_shared_down': 8.0,
     'L2_ffn_shared_gate_w': 8.0,
     'L3_ffn_gate_w': 8.0,
     'L3_ffn_w1': 8.0,
     'L3_ffn_w3': 8.0,
     'L3_ffn_w2': 8.0}
    for name, (base, spread) in spreads.items():
        noise = np.random.default_rng([zlib.crc32(name.encode()), seed]).standard_normal(out[name].shape)
        drawn = base * np.exp(spread * noise) if base else spread * noise
        out[name] = jnp.asarray(drawn.astype(out[name].dtype))
    for name, factor in factors.items():
        out[name] = (out[name] * factor).astype(out[name].dtype)
    return out
```

```python
from collections import namedtuple
from contextlib import ExitStack, contextmanager

import concourse.bass as bass
from concourse import mybir

ALU = mybir.AluOpType
ACT = mybir.ActivationFunctionType
AX = mybir.AxisListType
F32 = mybir.dt.float32
BF16 = mybir.dt.bfloat16
I32 = mybir.dt.int32

P = 128
B, S, D = 8, 512, 256
NT = S // P
NC = D // P
NH, DH = 16, 16
HG = NH // 4
RSQRT_SEED = 0x5F3759DF
MASKED = -1.0e30
LN_EPS = 1e-5
RMS_EPS = 1e-6


NormScratch = namedtuple("NormScratch", "stats mean var rstd seed tmp")
Job = namedtuple("Job", "glu nf win outs first last out0")


class Shared:
    pass


class Steps:

    def __init__(self, eng, sem, base=0):
        self.eng, self.sem, self.base, self.n = eng, sem, base, 0

    def __call__(self, ins):
        self.n += 1
        ins.then_inc(self.sem, 1)
        self.eng.wait_ge(self.sem, self.base + self.n)


def rsqrt(nc, step, out, seed, tmp, val):
    step(nc.vector.tensor_scalar(seed.bitcast(I32), val.bitcast(I32), 1, None, ALU.logical_shift_right))
    step(nc.vector.tensor_scalar(out.bitcast(I32), seed.bitcast(I32), -1.0, float(RSQRT_SEED), ALU.mult, ALU.add))
    for _ in range(4):
        step(nc.vector.tensor_tensor(tmp, out, out, ALU.mult))
        step(nc.vector.scalar_tensor_tensor(out=seed, in0=tmp, scalar=-0.5, in1=val, op0=ALU.mult, op1=ALU.mult))
        step(nc.vector.scalar_tensor_tensor(out=out, in0=seed, scalar=1.5, in1=out, op0=ALU.add, op1=ALU.mult))


RSQRT_STEPS = 14
LN_STEPS = 4 + RSQRT_STEPS


def layernorm(nc, step, w, xn, x):
    for t in range(NT):
        last = nc.vector.bn_stats(w.stats[:, t, :], x[:, t, :])
    step(last)
    st = w.stats
    nc.vector.tensor_tensor(w.mean[:], st[:, :, 1], st[:, :, 4], ALU.add)
    nc.vector.tensor_tensor(w.tmp[:], st[:, :, 1], st[:, :, 4], ALU.subtract)
    step(nc.vector.tensor_tensor(w.var[:], st[:, :, 2], st[:, :, 5], ALU.add))
    nc.vector.tensor_scalar(w.mean[:], w.mean[:], 0.5, None, ALU.mult)
    nc.vector.tensor_scalar(w.var[:], w.var[:], 1.0 / D, LN_EPS, ALU.mult, ALU.add)
    step(nc.vector.scalar_tensor_tensor(out=w.tmp[:], in0=w.tmp[:], scalar=0.25, in1=w.tmp[:], op0=ALU.mult,
                                        op1=ALU.mult))
    step(nc.vector.tensor_tensor(w.var[:], w.var[:], w.tmp[:], ALU.add))
    rsqrt(nc, step, w.rstd[:], w.seed[:], w.tmp[:], w.var[:])
    for t in range(NT):
        last = nc.vector.tensor_scalar(xn[:, t, :], x[:, t, :], w.mean[:, t:t + 1], w.rstd[:, t:t + 1],
                                       ALU.subtract, ALU.mult)
    return last


def norm_scratch(sb, name):
    return NormScratch(
        stats=sb(name + "_stats", [P, NT, 6]), mean=sb(name + "_mean", [P, NT]), var=sb(name + "_var", [P, NT]),
        rstd=sb(name + "_rstd", [P, NT]), seed=sb(name + "_seed", [P, NT]), tmp=sb(name + "_tmp", [P, NT]))


def rms_rstd(nc, step, w, x):
    for t in range(NT):
        last = nc.vector.bn_stats(w.stats[:, t, :], x[:, t, :])
    step(last)
    st = w.stats
    nc.vector.tensor_tensor(w.mean[:], st[:, :, 1], st[:, :, 4], ALU.add)
    nc.vector.tensor_tensor(w.tmp[:], st[:, :, 1], st[:, :, 4], ALU.subtract)
    step(nc.vector.tensor_tensor(w.var[:], st[:, :, 2], st[:, :, 5], ALU.add))
    nc.vector.scalar_tensor_tensor(out=w.mean[:], in0=w.mean[:], scalar=0.25, in1=w.mean[:], op0=ALU.mult,
                                   op1=ALU.mult)
    nc.vector.tensor_scalar(w.var[:], w.var[:], 1.0 / D, RMS_EPS, ALU.mult, ALU.add)
    step(nc.vector.scalar_tensor_tensor(out=w.tmp[:], in0=w.tmp[:], scalar=0.25, in1=w.tmp[:], op0=ALU.mult,
                                        op1=ALU.mult))
    step(nc.vector.tensor_tensor(w.var[:], w.var[:], w.tmp[:], ALU.add))
    step(nc.vector.tensor_tensor(w.var[:], w.var[:], w.mean[:], ALU.add))
    rsqrt(nc, step, w.rstd[:], w.seed[:], w.tmp[:], w.var[:])


def allocators(nc, ctx):
    def sb(name, shape, dt=F32):
        return ctx.enter_context(nc.sbuf_tensor(name, shape, dt))

    def ps(name, shape, dt=F32):
        return ctx.enter_context(nc.psum_tensor(name, shape, dt))
    return sb, ps


def batch(t, i):
    return t[:, bass.ds(i * NT, NT), :]


def prepare(nc, g, sem):
    s_x, s_gate, s_zero, s_one, s_tanh = (sem("prep_" + n) for n in ("x", "gate", "zero", "one", "tanh"))
    with nc.Block() as block:
        @block.sync
        def _(sp):
            for h in range(2):
                b = slice(h * (B // 2) * NT, (h + 1) * (B // 2) * NT)
                r = slice(h * (B // 2), (h + 1) * (B // 2))
                sp.dma_start(g.x[:, b, :], g.dram["x"][r].rearrange("b (t p) d -> p (b t) d", p=P)).then_inc(s_x, 16)
            for k, name in enumerate(("g_xattn", "g_ffn")):
                sp.dma_start(g.gates[:, k, :], g.dram[name].rearrange("(o n) -> o n", o=1).broadcast_to([P, 4])
                             ).then_inc(s_gate, 16)
            sp.wait_ge(s_x, 32)

        @block.gpsimd
        def _(pool):
            nc.gpsimd.memset(g.ident[:], 0.0).then_inc(s_zero, 1)
            nc.gpsimd.memset(g.ones[:], 1.0).then_inc(s_one, 1)
            pool.wait_ge(s_zero, 1)
            nc.gpsimd.affine_select(out=g.ident[:], in_=g.ident[:], compare_op=ALU.not_equal, fill=1.0, base=0,
                                    pattern=[[-1, P]], channel_multiplier=1).then_inc(s_one, 1)

        @block.scalar
        def _(act):
            act.wait_ge(s_gate, 32)
            nc.scalar.activation(g.tg[:], g.gates[:], ACT.Tanh).then_inc(s_tanh, 1)
            act.wait_ge(s_tanh, 1)

        @block.vector
        def _(dve):
            dve.wait_ge(s_one, 2)
            nc.vector.tensor_copy(g.identb[:], g.ident[:]).then_inc(s_zero, 1)
            dve.wait_ge(s_zero, 2)


def channel_attention(nc, g, sem):
    names = ("load", "ctx", "free", "xn", "gram", "ctxT", "ctxTc", "exp_in", "exp", "m", "mT", "mTc", "y", "x",
             "dve", "const", "all")
    Sems = namedtuple("Sems", names)
    s = Sems(*(sem("ca_" + n) for n in names))
    HW = 64
    with ExitStack() as ctx:
        sb, ps = allocators(nc, ctx)
        ctx_all = sb("ca_ctx_all", [P, B * NT, D])
        ctx_fix = sb("ca_ctx", [P, NT, D])
        ctxT = sb("ca_ctxT", [P, NC, S])
        xn = sb("ca_xn", [P, NT, D])
        w = norm_scratch(sb, "ca")
        col = {n: sb("ca_c" + n, [P, 2, NC]) for n in ("wq", "bq")}
        row = {n: sb("ca_r" + n, [P, 2, NC, HW]) for n in ("wk", "bk", "wv", "bv")}
        wp, bp, wp2 = (sb("ca_" + n, [P, NC]) for n in ("wp", "bp", "wp2"))
        gs = sb("ca_gs", [P, 320])
        T, U = sb("ca_T", [P, 2, NC, HW]), sb("ca_U", [P, 2, NC, HW])
        A, mx, sm, rc, cs = (sb("ca_" + n, [P, 2, NC]) for n in ("A", "mx", "sm", "rc", "cs"))
        cst = sb("ca_cst", [P, NC])
        Mbd, MT, Dg = (sb("ca_" + n, [P, NC, P]) for n in ("Mbd", "MT", "Dg"))
        pG = ps("ca_pG", [P, 512])
        pT = ps("ca_pT", [P, NC, S])
        pM = ps("ca_pM", [P, 512])
        pY = ps("ca_pY", [P, NT, D])
        G = gs[:, 0:128].rearrange("p (c e) -> p c e", c=NC)
        sx = gs[:, 128:130]
        sc = gs[:, 192:320].rearrange("p (c e) -> p c e", c=NC)
        NLOAD = 2 + 4 + 2 + 16
        K = LN_STEPS + 18
        with nc.Block() as block:
            @block.sync
            def _(sp):
                for h in range(2):
                    b = slice(h * (B // 2) * NT, (h + 1) * (B // 2) * NT)
                    r = slice(h * (B // 2), (h + 1) * (B // 2))
                    sp.dma_start(ctx_all[:, b, :], g.dram["ctx_1024"][r].rearrange("b (t p) d -> p (b t) d", p=P)
                                 ).then_inc(s.load, 16)
                for k, kind in enumerate("gl"):
                    for n in ("wq", "bq"):
                        sp.dma_start(col[n][:, k, :], g.dram[f"L0_xattn_{n}{kind}"].rearrange("(c p) -> p c", p=P),
                                     allow_slow_non_contiguous=True).then_inc(s.load, 16)
                sp.dma_start(wp[:], g.dram["L0_xattn_wp"].rearrange("(c p) -> p c", p=P),
                             allow_slow_non_contiguous=True).then_inc(s.load, 16)
                sp.dma_start(bp[:], g.dram["L0_xattn_bp"].rearrange("(c p) -> p c", p=P),
                             allow_slow_non_contiguous=True).then_inc(s.load, 16)
                for k, kind in enumerate("gl"):
                    for n in ("wk", "bk", "wv", "bv"):
                        v = g.dram[f"L0_xattn_{n}{kind}"].rearrange("(c j e) -> j c e", j=2, e=HW)
                        for j in range(2):
                            sp.dma_start(row[n][HW * j:HW * j + HW, k, :, :],
                                         v[j:j + 1].broadcast_to([HW, NC, HW])).then_inc(s.load, 16)

            @block.gpsimd
            def _(pool):
                nc.gpsimd.memset(Mbd[:], 0.0).then_inc(s.const, 1)
                pool.wait_ge(s.load, 16 * NLOAD)
                pool.sem_inc(s.free, 1)
                with pool.Fori(0, B) as i:
                    pool.wait_ge(s.free, i + 1)
                    nc.gpsimd.tensor_copy(ctx_fix[:], batch(ctx_all, i)).then_inc(s.ctx, 1)

            @block.tensor
            def _(pe):
                with pe.Fori(0, B) as i:
                    pe.wait_ge(s.ctx, i + 1)
                    for c in range(NC):
                        for t in range(NT):
                            last = nc.tensor.transpose(pT[:, c, t * P:(t + 1) * P], ctx_fix[:, t, c * P:(c + 1) * P],
                                                       g.ident[:])
                    last.then_inc(s.ctxT, 1)
                    pe.wait_ge(s.xn, i + 1)
                    for c in range(NC):
                        for j in range(2):
                            h = slice((2 * c + j) * HW, (2 * c + j + 1) * HW)
                            o = slice(HW * j, HW * j + HW)
                            for t in range(NT):
                                nc.tensor.matmul(pG[o, c * HW:c * HW + HW], xn[:, t, h], ctx_fix[:, t, h],
                                                 start=t == 0, stop=t == NT - 1)
                            for t in range(NT):
                                nc.tensor.matmul(pG[o, 128 + c:129 + c], xn[:, t, h], g.ones[:, 0:1],
                                                 start=t == 0, stop=t == NT - 1)
                            for t in range(NT):
                                last = nc.tensor.matmul(pG[o, 192 + c * HW:192 + c * HW + HW], g.ones[:, 0:HW],
                                                        ctx_fix[:, t, h], start=t == 0, stop=t == NT - 1)
                    last.then_inc(s.gram, 1)
                    pe.wait_ge(s.ctxT, i + 1)
                    pe.wait_ge(s.m, i + 1)
                    for c in range(NC):
                        last = nc.tensor.transpose(pM[:, c * P:(c + 1) * P], Mbd[:, c, :], g.ident[:])
                    last.then_inc(s.mT, 1)
                    pe.wait_ge(s.mTc, i + 1)
                    pe.wait_ge(s.ctxTc, 2 * i + 2)
                    for t in range(NT):
                        for c in range(NC):
                            o = pY[:, t, c * P:(c + 1) * P]
                            nc.tensor.matmul(o, ctxT[:, c, t * P:(t + 1) * P], MT[:, c, :], start=True, stop=False)
                            last = nc.tensor.matmul(o, g.ones[:], Dg[:, c, :], start=False, stop=True)
                    last.then_inc(s.y, 1)

            @block.scalar
            def _(act):
                with act.Fori(0, B) as i:
                    act.wait_ge(s.ctxT, i + 1)
                    nc.scalar.copy(ctxT[:], pT[:]).then_inc(s.ctxTc, 1)
                    nc.scalar.copy(g.ctxT[:, :, bass.ds(i * S, S)], pT[:]).then_inc(s.ctxTc, 1)
                    act.wait_ge(s.exp_in, i + 1)
                    nc.scalar.activation(T[:], T[:], ACT.Exp, scale=float(D) ** -0.5).then_inc(s.exp, 1)
                    act.wait_ge(s.mT, i + 1)
                    nc.scalar.copy(MT[:], pM[:, 0:NC * P].rearrange("p (c n) -> p c n", c=NC)).then_inc(s.mTc, 1)
                act.wait_ge(s.ctxTc, 2 * B)

            @block.vector
            def _(dve):
                dve.wait_ge(s.load, 16 * NLOAD)
                dve.wait_ge(s.const, 1)
                first = Steps(dve, s.const, 1)
                first(nc.vector.tensor_scalar(wp2[:], wp[:], g.tg[:, 0, 0:1], 2.0, ALU.mult, ALU.mult))
                first(nc.vector.tensor_scalar(bp[:], bp[:], g.tg[:, 0, 0:1], None, ALU.mult))
                four = [P, 2, NC, HW]
                with dve.Fori(0, B) as i:
                    step = Steps(dve, s.dve, i * K)
                    layernorm(nc, step, w, xn, batch(g.x, i)).then_inc(s.xn, 1)
                    dve.wait_ge(s.gram, i + 1)
                    step(nc.vector.tensor_copy(gs[:, 0:130], pG[:, 0:130]))
                    step(nc.vector.tensor_copy(gs[:, 192:320], pG[:, 192:320]))
                    nc.vector.tensor_tensor(A[:], col["wq"][:], sx.unsqueeze(1).broadcast_to([P, 2, NC]), ALU.mult)
                    step(nc.vector.tensor_tensor(T[:], G.unsqueeze(1).broadcast_to(four),
                                                 col["wq"][:].unsqueeze(3).broadcast_to(four), ALU.mult))
                    step(nc.vector.scalar_tensor_tensor(out=A[:], in0=col["bq"][:], scalar=float(S), in1=A[:],
                                                        op0=ALU.mult, op1=ALU.add))
                    nc.vector.tensor_tensor(T[:], T[:], row["wk"][:], ALU.mult)
                    step(nc.vector.tensor_tensor(U[:], row["bk"][:], A[:].unsqueeze(3).broadcast_to(four), ALU.mult))
                    step(nc.vector.tensor_tensor(T[:], T[:], U[:], ALU.add))
                    step(nc.vector.tensor_tensor(U[:], row["wk"][:], sc.unsqueeze(1).broadcast_to(four), ALU.mult))
                    step(nc.vector.tensor_tensor(U[:], U[:], col["bq"][:].unsqueeze(3).broadcast_to(four), ALU.mult))
                    step(nc.vector.tensor_tensor(T[:], T[:], U[:], ALU.add))
                    step(nc.vector.tensor_reduce(mx[:], T[:], AX.X, ALU.max))
                    nc.vector.tensor_tensor(T[:], T[:], mx[:].unsqueeze(3).broadcast_to(four), ALU.subtract
                                            ).then_inc(s.exp_in, 1)
                    dve.wait_ge(s.exp, i + 1)
                    step(nc.vector.tensor_reduce(sm[:], T[:], AX.X, ALU.add))
                    step(nc.vector.reciprocal(rc[:], sm[:]))
                    step(nc.vector.tensor_tensor(rc[:], rc[:], wp2[:].unsqueeze(1).broadcast_to([P, 2, NC]), ALU.mult))
                    step(nc.vector.tensor_tensor(T[:], T[:], rc[:].unsqueeze(3).broadcast_to(four), ALU.mult))
                    step(nc.vector.tensor_tensor(U[:], T[:], row["bv"][:], ALU.mult))
                    nc.vector.tensor_tensor(T[:], T[:], row["wv"][:], ALU.mult)
                    step(nc.vector.tensor_reduce(cs[:], U[:], AX.X, ALU.add))
                    nc.vector.tensor_tensor(cst[:], cs[:, 0, :], bp[:], ALU.add)
                    for j in range(2):
                        q = slice(HW * j, HW * j + HW)
                        last = nc.vector.tensor_tensor(Mbd[q, :, HW * j:HW * j + HW], T[q, 0], T[q, 1], ALU.add)
                    step(last)
                    step(nc.vector.tensor_tensor(cst[:], cst[:], cs[:, 1, :], ALU.add))
                    for c in range(NC):
                        last = nc.vector.tensor_scalar(Dg[:, c, :], g.ident[:], cst[:, c:c + 1], None, ALU.mult)
                    last.then_inc(s.m, 1)
                    assert step.n == K, step.n
                    dve.wait_ge(s.y, i + 1)
                    x = batch(g.x, i)
                    nc.vector.tensor_tensor(x, pY[:], x, ALU.add).then_inc(s.x, 1)
                    dve.sem_inc(s.free, 1)
                dve.wait_ge(s.x, B)


PAIRS = ((0, 0), (0, 1), (1, 0), (1, 1), (0, 2), (2, 0))
KS = DH * len(PAIRS)
KM = KS + 3


def load_transposed(nc, g, sb, ps, sem, tag, weights):
    s_in, s_t, s_c = sem(tag + "_w_in"), sem(tag + "_w_t"), sem(tag + "_w_c")
    turned = [sb(f"{tag}_wT{n}", [P, NC, D]) for n in range(len(weights))]
    with ExitStack() as ctx:
        sb2, ps2 = allocators(nc, ctx)
        raw = [sb2(f"{tag}_raw{n}", [P, NC, D]) for n in range(len(weights))]
        pW = ps2(tag + "_pW", [P, 2, NC, D])
        with nc.Block() as block:
            @block.sync
            def _(sp):
                for n, wt in enumerate(weights):
                    sp.dma_start(raw[n][:], wt.rearrange("(c p) k -> p c k", p=P)).then_inc(s_in, 16)

            @block.tensor
            def _(pe):
                pe.wait_ge(s_in, 16 * len(weights))
                for n in range(len(weights)):
                    if n >= 2:
                        pe.wait_ge(s_c, n - 1)
                    for c in range(NC):
                        for k in range(NC):
                            last = nc.tensor.transpose(pW[:, n % 2, k, c * P:(c + 1) * P],
                                                       raw[n][:, c, k * P:(k + 1) * P], g.ident[:])
                    last.then_inc(s_t, 1)

            @block.scalar
            def _(act):
                for n in range(len(weights)):
                    act.wait_ge(s_t, n + 1)
                    nc.scalar.copy(turned[n][:], pW[:, n % 2]).then_inc(s_c, 1)
                act.wait_ge(s_c, len(weights))
    return turned


def head_attention(nc, g, sem, tag, kind, wts, gate):
    self_attn, causal, biased = kind == "self", kind == "causal", kind == "biased"
    names = ("load", "wo", "woc", "const", "dve", "xn", "xT", "xTc", "kv", "cT", "cTc", "q", "qsw", "k", "ksw", "v",
             "qf", "kf", "qr", "kr", "vc", "qp", "kp", "pool", "qw", "kw", "qs", "ks", "S", "max", "mm", "mT", "mTc",
             "mw", "mrow", "ST", "exp", "pv", "oev", "den", "rd", "on", "y", "x")
    Sems = namedtuple("Sems", names)
    s = Sems(*(sem(f"{tag}_{n}") for n in names))
    NS = NH * NT
    NW = HG * NT
    with ExitStack() as ctx:
        sb, ps = allocators(nc, ctx)
        if self_attn:
            Wq, Wk = sb(tag + "_Wq", [P, NC, D]), sb(tag + "_Wk", [64, D])
            Wqs, Wks = sb(tag + "_Wqs", [P, NC, D]), sb(tag + "_Wks", [64, D])
            Wc, Wv = sb(tag + "_Wc", [P, 2, NC, 64]), sb(tag + "_Wv", [64, D])
            kvc = sb(tag + "_kvc", [64, 2, S])
            cos, sin = sb(tag + "_cos", [P, S]), sb(tag + "_sin", [P, S])
            normw = sb(tag + "_normw", [P, D])
        else:
            WqT, WkT, WvT, WoT = load_transposed(nc, g, sb, ps, sem, tag, [wts[n] for n in ("Wq", "Wk", "Wv", "Wo")])
            kvT = sb(tag + "_kvT", [P, NC, S])
        Wo = sb(tag + "_Wo", [P, HG, D])
        if biased:
            bq, bk = sb(tag + "_bq", [P, NC]), sb(tag + "_bk", [P, NC])
            bv, bo = sb(tag + "_bv", [P, D]), sb(tag + "_bo", [P, D])
        if causal:
            mask_q, mask_k = sb(tag + "_mask_q", [P, P], BF16), sb(tag + "_mask_k", [P, P], BF16)
        xn, xnT = sb(tag + "_xn", [P, NT, D]), sb(tag + "_xnT", [P, NC, S])
        w = norm_scratch(sb, tag)
        Pb = sb(tag + "_P", [P, 2, 4, S])
        (qf, qr), (kf, kr) = ((Pb[:, n, 0:NC], Pb[:, n, NC:2 * NC]) for n in range(2))
        parts = sb(tag + "_parts", [P, 6, NC, S], BF16)
        qp, kp = parts[:, 0:3], parts[:, 3:6]
        qs, ks = sb(tag + "_qs", [P, NH, S], BF16), sb(tag + "_ks", [P, NH, S], BF16)
        V = sb(tag + "_V", [P, NT, NH, 32])
        nm, nr = sb(tag + "_nm", [P, NT, NH]), sb(tag + "_nr", [P, NT, NH])
        mm, mTb = sb(tag + "_mm", [P, NT, 3, NH], BF16), sb(tag + "_mTb", [3 * NH, S], BF16)
        Osb, rD = xnT, sb(tag + "_rD", [P, S])
        On = parts[:, 0:4].rearrange("p a c n -> p (a c n)").bitcast(F32).rearrange("p (g n) -> p g n", g=HG)
        sel = sb(tag + "_sel", [P, P])
        pST, pS = ps(tag + "_pST", [P, 2, 2, S]), ps(tag + "_pS", [P, 2, S])
        pO, pM = ps(tag + "_pO", [P, S]), ps(tag + "_pM", [P, S])
        pQ, pK = pST[:, 0], pST[:, 1]
        pV = (pST[:, 0] if self_attn else pS[:]).rearrange("p a n -> p (a n)").rearrange("p (t n) -> p t n", t=NT)
        pY = pST[:, 0].rearrange("p a n -> p (a n)").rearrange("p (t n) -> p t n", t=NT)
        d_parts = {n: nc.dram_tensor(f"{tag}_d{n}", (3, D, S), BF16, kind="Internal").ap() for n in "qk"}
        d_max = nc.dram_tensor(f"{tag}_dm", (3 * NH, S), BF16, kind="Internal").ap()
        if not self_attn:
            d_wo = nc.dram_tensor(f"{tag}_dwo", (D, D), F32, kind="Internal").ap()
        NLOAD = {"self": 8 + 4, "causal": 4, "biased": 4 + 4}[kind]
        NDVE = {"self": LN_STEPS + 1 + 3 + 1 + 5 + RSQRT_STEPS, "causal": LN_STEPS + 3,
                "biased": LN_STEPS + 3 + 1}[kind] + 3
        NCONST = {"self": 4 + 4, "causal": 4 + 2, "biased": 4}[kind]
        with nc.Block() as block:
            @block.sync
            def _(sp):
                wo = wts["Wo"]
                if self_attn:
                    sp.dma_start(Wq[:], wts["Wq"].rearrange("(c p) n -> p c n", p=P)).then_inc(s.load, 16)
                    sp.dma_start(Wk[:], wts["Wk"]).then_inc(s.load, 16)
                    sp.dma_start(Wv[:], wts["Wv"]).then_inc(s.load, 16)
                    for n, m in enumerate(("Wk_c", "Wv_c")):
                        sp.dma_start(Wc[:, n], wts[m].rearrange("(c p) n -> p c n", p=P)).then_inc(s.load, 16)
                    for j in range(2):
                        sp.dma_start((cos, sin)[j][:], wts[("cos", "sin")[j]]).then_inc(s.load, 16)
                    sp.dma_start(normw[:], wts["norm1_w"].rearrange("(o n) -> o n", o=1).broadcast_to([P, D])
                                 ).then_inc(s.load, 16)
                else:
                    wo = d_wo
                    sp.dma_start(wo.rearrange("(c p) n -> p c n", p=P), WoT[:]).then_inc(s.wo, 16)
                    sp.wait_ge(s.wo, 16)
                if biased:
                    for t, n in ((bq, "bq"), (bk, "bk")):
                        sp.dma_start(t[:], wts[n].rearrange("(c p) -> p c", p=P),
                                     allow_slow_non_contiguous=True).then_inc(s.load, 16)
                    for t, n in ((bv, "bv"), (bo, "bo")):
                        sp.dma_start(t[:], wts[n].rearrange("(o n) -> o n", o=1).broadcast_to([P, D])
                                     ).then_inc(s.load, 16)
                sp.wait_ge(s.const, 1)
                for j in range(4):
                    sp.dma_start(Wo[32 * j:32 * j + DH], wo.rearrange("(g j d) n -> j d g n", j=4, d=DH)[j]
                                 ).then_inc(s.load, 16)
                with sp.Fori(0, B) as i:
                    for src, dram, dst, ready, wrote, there in (
                            (qp, d_parts["q"], qs, s.qp, s.qw, s.qs), (kp, d_parts["k"], ks, s.kp, s.kw, s.ks)):
                        sp.wait_ge(ready, i + 1)
                        for r in range(3):
                            sp.dma_start(dram[r].rearrange("(c p) t -> p c t", p=P), src[:, r]).then_inc(wrote, 16)
                        sp.wait_ge(wrote, i * 48 + 48)
                        for n, pair in enumerate(PAIRS):
                            r = pair[0] if dst is qs else pair[1]
                            sp.dma_start(dst[DH * n:DH * n + DH], dram[r].rearrange("(h d) t -> d h t", d=DH)
                                         ).then_inc(there, 16)
                    sp.wait_ge(s.mTc, i + 1)
                    sp.dma_start(d_max, mTb[:]).then_inc(s.mw, 16)
                    sp.wait_ge(s.mw, i * 16 + 16)
                    sp.dma_start(qs[KS:KM], d_max.rearrange("(r h) t -> r h t", h=NH)).then_inc(s.mrow, 16)

            @block.gpsimd
            def _(pool):
                nc.gpsimd.memset(Wo[:], 0.0).then_inc(s.const, 1)
                pre = Steps(pool, s.pool)
                nc.gpsimd.memset(V[:], 0.0).then_inc(s.const, 1)
                pool.wait_ge(s.const, 2)
                nc.gpsimd.memset(V[:, :, :, DH:DH + 1], 1.0).then_inc(s.const, 1)
                pool.wait_ge(s.const, 3)
                pre(nc.gpsimd.memset(ks[KS:P], 1.0))
                pre(nc.gpsimd.memset(sel[:], 0.0))
                nc.gpsimd.affine_select(out=sel[:].rearrange("p (j m) -> p j m", j=4),
                                        in_=sel[:].rearrange("p (j m) -> p j m", j=4),
                                        compare_op=ALU.not_equal, fill=1.0, base=-DH,
                                        pattern=[[-32, 4], [0, 32]], channel_multiplier=1).then_inc(s.const, 1)
                if causal:
                    pre(nc.gpsimd.memset(mask_q[:], 0.0))
                    pre(nc.gpsimd.memset(mask_k[:], 0.0))
                    nc.gpsimd.affine_select(out=mask_q[:], in_=mask_q[:], compare_op=ALU.is_ge, fill=MASKED, base=0,
                                            pattern=[[-1, P]], channel_multiplier=1).then_inc(s.const, 1)
                    nc.gpsimd.affine_select(out=mask_k[:], in_=mask_k[:], compare_op=ALU.is_ge, fill=MASKED, base=0,
                                            pattern=[[1, P]], channel_multiplier=-1).then_inc(s.const, 1)
                if self_attn:
                    pool.wait_ge(s.load, 16 * NLOAD)
                    for dst, src in ((Wqs, Wq), (Wks, Wk)):
                        for e in range(2):
                            dv, sv = (x[:].rearrange("p c (n e) -> p c n e", e=2)[:, :, :, k] if x in (Wq, Wqs) else
                                      x[:].rearrange("p (n e) -> p n e", e=2)[:, :, k]
                                      for x, k in ((dst, e), (src, 1 - e)))
                            nc.gpsimd.tensor_copy(dv, sv).then_inc(s.const, 1)
                npre = pre.n
                one = g.ones[:, 0:1].unsqueeze(2).broadcast_to([P, NC, S])
                with pool.Fori(0, B) as i:
                    step = Steps(pool, s.pool, i * 3 + npre)
                    if not self_attn:
                        pool.wait_ge(s.xn, i + 1)
                        nc.gpsimd.tensor_copy(kvT[:], g.ctxT[:, :, bass.ds(i * S, S)]).then_inc(s.kv, 1)
                    pool.wait_ge(s.kf, i + 1)
                    step(nc.gpsimd.tensor_tensor(kp[:, 0], kf, one, ALU.mult))
                    step(nc.gpsimd.tensor_tensor(kr, kf, kp[:, 0], ALU.subtract))
                    step(nc.gpsimd.tensor_tensor(kp[:, 1], kr, one, ALU.mult))
                    nc.gpsimd.tensor_tensor(kp[:, 2], kr, kp[:, 1], ALU.subtract).then_inc(s.kp, 1)

            @block.tensor
            def _(pe):
                pe.wait_ge(s.load, 16 * NLOAD)
                pe.wait_ge(s.const, NCONST)
                pe.wait_ge(s.woc, 1)

                def project(out, lhsT, rhs, chunks=NC):
                    for m in range(NC):
                        for c in range(chunks):
                            last = nc.tensor.matmul(out[:, m, :], lhsT(c)[:, m * P:(m + 1) * P], rhs(c),
                                                    start=c == 0, stop=c == chunks - 1)
                    return last

                with pe.Fori(0, B) as i:
                    pe.wait_ge(s.xn, i + 1)
                    for c in range(NC):
                        for t in range(NT):
                            last = nc.tensor.transpose(pS[:, c, t * P:(t + 1) * P], xn[:, t, c * P:(c + 1) * P],
                                                       g.ident[:])
                    last.then_inc(s.xT, 1)
                    pe.wait_ge(s.xTc, i + 1)
                    if self_attn:
                        for n, bank in enumerate((pO, pM)):
                            for c in range(NC):
                                last = nc.tensor.matmul(bank[0:64], Wc[:, n, c, :], xnT[:, c, :],
                                                        start=c == 0, stop=c == NC - 1)
                        last.then_inc(s.cT, 1)
                        project(pQ, lambda c: Wq[:, c, :], lambda c: xnT[:, c, :]).then_inc(s.q, 1)
                        project(pS, lambda c: Wqs[:, c, :], lambda c: xnT[:, c, :]).then_inc(s.qsw, 1)
                        pe.wait_ge(s.cTc, i + 1)
                        project(pK, lambda c: Wk[:], lambda c: kvc[:, 0, :], 1).then_inc(s.k, 1)
                        pe.wait_ge(s.qr, i + 1)
                        project(pS, lambda c: Wks[:], lambda c: kvc[:, 0, :], 1).then_inc(s.ksw, 1)
                        for t in range(NT):
                            last = nc.tensor.matmul(pV[:, t, :], kvc[:, 1, t * P:(t + 1) * P], Wv[:],
                                                    start=True, stop=True)
                        last.then_inc(s.v, 1)
                    else:
                        project(pQ, lambda c: WqT[:, c, :], lambda c: xnT[:, c, :]).then_inc(s.q, 1)
                        pe.wait_ge(s.kv, i + 1)
                        project(pK, lambda c: WkT[:, c, :], lambda c: kvT[:, c, :]).then_inc(s.k, 1)
                        for t in range(NT):
                            for c in range(NC):
                                last = nc.tensor.matmul(pV[:, t, :], kvT[:, c, t * P:(t + 1) * P], WvT[:, c, :],
                                                        start=c == 0, stop=c == NC - 1)
                        last.then_inc(s.v, 1)
                    pe.wait_ge(s.kr if self_attn else s.vc, i + 1)
                    pe.wait_ge(s.qs, i * 96 + 96)
                    pe.wait_ge(s.ks, i * 96 + 96)
                    for n in range(NS):
                        h, t = divmod(n, NT)
                        if n >= 2:
                            pe.wait_ge(s.max, i * NS + n - 1)
                        keys = (t + 1) * P if causal else S
                        last = nc.tensor.matmul(pS[:, n % 2, 0:keys], qs[0:KS, h, t * P:(t + 1) * P],
                                                ks[0:KS, h, 0:keys], start=True, stop=not causal)
                        if causal:
                            last = nc.tensor.matmul(pS[:, n % 2, t * P:keys], g.identb[:], mask_q[:],
                                                    start=False, stop=True)
                        last.then_inc(s.S, 1)
                    pe.wait_ge(s.mm, i + 1)
                    for t in range(NT):
                        last = nc.tensor.matmul(pM[0:3 * NH, t * P:(t + 1) * P],
                                                mm[:, t].rearrange("p r h -> p (r h)"), g.identb[:],
                                                start=True, stop=True)
                    last.then_inc(s.mT, 1)
                    pe.wait_ge(s.mrow, i * 16 + 16)
                    pe.wait_ge(s.vc, i + 1)

                    def spread(h):
                        pe.wait_ge(s.oev, i * HG + h + 1)
                        if h >= 1:
                            pe.wait_ge(s.rd, i * HG + h)
                        nc.tensor.matmul(pM[:], sel[:], Osb[:, h % 2, :], start=True, stop=True).then_inc(s.den, 1)

                    for n in range(NW + 1):
                        if n < NW:
                            hg, kt = divmod(n, NT)
                            lo = kt * P if causal else 0
                            for pair in range(2):
                                if n >= 1:
                                    pe.wait_ge(s.exp, i * 2 * NW + 2 * n + pair - 1)
                                for j in range(2):
                                    h = 4 * hg + 2 * pair + j
                                    o = pST[:, pair, j]
                                    last = nc.tensor.matmul(o[:, lo:S], ks[0:KM, h, kt * P:(kt + 1) * P],
                                                            qs[0:KM, h, lo:S], start=True, stop=not causal)
                                    if causal:
                                        last = nc.tensor.matmul(o[:, lo:lo + P], g.identb[:], mask_k[:],
                                                                start=False, stop=True)
                                last.then_inc(s.ST, 1)
                        if n >= 1:
                            hg, kt = divmod(n - 1, NT)
                            lo = kt * P if causal else 0
                            if kt == 0 and hg >= 1:
                                spread(hg - 1)
                            pe.wait_ge(s.exp, i * 2 * NW + 2 * n)
                            for j in range(4):
                                last = nc.tensor.matmul(pO[32 * j:32 * j + 32, lo:S], V[:, kt, 4 * hg + j, :],
                                                        Pb[:, (n - 1) % 2, j, lo:S], start=kt == 0, stop=kt == NT - 1)
                            last.then_inc(s.pv, 1)
                    spread(HG - 1)
                    pe.wait_ge(s.on, i * HG + HG)
                    for t in range(NT):
                        for h in range(HG):
                            last = nc.tensor.matmul(pY[:, t, :], On[:, h, t * P:(t + 1) * P], Wo[:, h, :],
                                                    start=h == 0, stop=h == HG - 1)
                    last.then_inc(s.y, 1)

            @block.scalar
            def _(act):
                if biased:
                    act.wait_ge(s.load, 16 * NLOAD)
                act.wait_ge(s.const, NCONST)
                vv = V[:, :, :, 0:DH]
                pv = pV.rearrange("p t (h d) -> p t h d", d=DH)
                with act.Fori(0, B) as i:
                    act.wait_ge(s.xT, i + 1)
                    nc.scalar.copy(xnT[:], pS[:]).then_inc(s.xTc, 1)
                    if self_attn:
                        act.wait_ge(s.cT, i + 1)
                        nc.scalar.copy(kvc[:, 0], pO[0:64])
                        nc.scalar.copy(kvc[:, 1], pM[0:64]).then_inc(s.cTc, 1)
                    else:
                        act.wait_ge(s.q, i + 1)
                        if biased:
                            for c in range(NC):
                                last = nc.scalar.activation(qf[:, c], pQ[:, c], ACT.Identity, bias=bq[:, c:c + 1])
                        else:
                            last = nc.scalar.copy(qf, pQ)
                        last.then_inc(s.qf, 1)
                        act.wait_ge(s.k, i + 1)
                        if biased:
                            for c in range(NC):
                                last = nc.scalar.activation(kf[:, c], pK[:, c], ACT.Identity, bias=bk[:, c:c + 1])
                        else:
                            last = nc.scalar.copy(kf, pK)
                        last.then_inc(s.kf, 1)
                    if not biased:
                        act.wait_ge(s.v, i + 1)
                        nc.scalar.copy(vv, pv).then_inc(s.vc, 1)
                    act.wait_ge(s.mT, i + 1)
                    nc.scalar.copy(mTb[:], pM[0:3 * NH]).then_inc(s.mTc, 1)
                    for n in range(NW):
                        lo = (n % NT) * P if causal else 0
                        if n >= 2:
                            act.wait_ge(s.pv, i * NW + n - 1)
                        for pair in range(2):
                            act.wait_ge(s.ST, i * 2 * NW + 2 * n + pair + 1)
                            nc.scalar.activation(Pb[:, n % 2, 2 * pair:2 * pair + 2, lo:S], pST[:, pair, :, lo:S],
                                                 ACT.Exp, scale=float(DH) ** -0.5).then_inc(s.exp, 1)

            @block.vector
            def _(dve):
                dve.wait_ge(s.load, 16 * NLOAD)
                dve.wait_ge(s.const, NCONST)
                if self_attn:
                    dve.sem_inc(s.woc, 1)
                else:
                    if biased:
                        nc.vector.tensor_scalar(bo[:], bo[:], g.tg[:, 0, gate:gate + 1], None, ALU.mult)
                    nc.vector.tensor_scalar(Wo[:], Wo[:], g.tg[:, 0, gate:gate + 1], None, ALU.mult).then_inc(s.woc, 1)
                    dve.wait_ge(s.woc, 1)
                with dve.Fori(0, B) as i:
                    step = Steps(dve, s.dve, i * NDVE)
                    layernorm(nc, step, w, xn, batch(g.x, i)).then_inc(s.xn, 1)
                    if self_attn:
                        wide = [P, NC, S]
                        for f, r, pf, psw, a, b, done in ((qf, qr, pQ, pS, s.q, s.qsw, s.qr),
                                                          (kf, kr, pK, pS, s.k, s.ksw, s.kr)):
                            dve.wait_ge(a, i + 1)
                            nc.vector.tensor_tensor(f, pf, cos[:].unsqueeze(1).broadcast_to(wide), ALU.mult)
                            dve.wait_ge(b, i + 1)
                            nc.vector.tensor_tensor(r, psw[:], sin[:].unsqueeze(1).broadcast_to(wide),
                                                    ALU.mult).then_inc(done, 1)
                            dve.wait_ge(done, i + 1)
                            if f is qf:
                                step(nc.vector.tensor_tensor(f, f, r, ALU.add))
                            else:
                                nc.vector.tensor_tensor(f, f, r, ALU.add).then_inc(s.kf, 1)
                    else:
                        dve.wait_ge(s.qf, i + 1)
                    step(nc.vector.tensor_copy(qp[:, 0], qf))
                    step(nc.vector.tensor_tensor(qr, qf, qp[:, 0], ALU.subtract))
                    step(nc.vector.tensor_copy(qp[:, 1], qr))
                    nc.vector.tensor_tensor(qp[:, 2], qr, qp[:, 1], ALU.subtract).then_inc(s.qp, 1)
                    if biased:
                        dve.wait_ge(s.v, i + 1)
                        for t in range(NT):
                            last = nc.vector.tensor_tensor(V[:, t, :, 0:DH], pV[:, t].rearrange("p (h d) -> p h d", d=DH),
                                                           bv[:].rearrange("p (h d) -> p h d", d=DH), ALU.add)
                        last.then_inc(s.vc, 1)
                    for n in range(NS):
                        h, t = divmod(n, NT)
                        dve.wait_ge(s.S, i * NS + n + 1)
                        keys = (t + 1) * P if causal else S
                        nc.vector.tensor_reduce(nm[:, t, h:h + 1], pS[:, n % 2, 0:keys], AX.X, ALU.max,
                                                negate=True).then_inc(s.max, 1)
                    dve.wait_ge(s.max, i * NS + NS)
                    step(nc.vector.tensor_copy(mm[:, :, 0], nm[:]))
                    step(nc.vector.tensor_tensor(nr[:], nm[:], mm[:, :, 0], ALU.subtract))
                    step(nc.vector.tensor_copy(mm[:, :, 1], nr[:]))
                    nc.vector.tensor_tensor(mm[:, :, 2], nr[:], mm[:, :, 1], ALU.subtract).then_inc(s.mm, 1)
                    for h in range(HG):
                        dve.wait_ge(s.pv, i * NW + NT * h + NT)
                        nc.vector.tensor_copy(Osb[:, h % 2], pO[:]).then_inc(s.oev, 1)
                        dve.wait_ge(s.den, i * HG + h + 1)
                        nc.vector.reciprocal(rD[:], pM[:]).then_inc(s.rd, 1)
                        dve.wait_ge(s.rd, i * HG + h + 1)
                        nc.vector.tensor_tensor(On[:, h], Osb[:, h % 2], rD[:], ALU.mult).then_inc(s.on, 1)
                    dve.wait_ge(s.y, i + 1)
                    if self_attn:
                        step(nc.vector.tensor_tensor(xn[:], pY, xn[:], ALU.add))
                        rms_rstd(nc, step, w, xn)
                        x2 = batch(g.x2, i)
                        for t in range(NT):
                            last = nc.vector.scalar_tensor_tensor(out=x2[:, t, :], in0=xn[:, t, :],
                                                                  scalar=w.rstd[:, t:t + 1], in1=normw[:],
                                                                  op0=ALU.mult, op1=ALU.mult)
                        last.then_inc(s.x, 1)
                    else:
                        x = batch(g.x, i)
                        if biased:
                            step(nc.vector.tensor_tensor(x, pY, x, ALU.add))
                            nc.vector.tensor_tensor(x, x, bo[:].unsqueeze(1).broadcast_to([P, NT, D]), ALU.add
                                                    ).then_inc(s.x, 1)
                        else:
                            nc.vector.tensor_tensor(x, pY, x, ALU.add).then_inc(s.x, 1)
                    dve.wait_ge(s.x, i + 1)
                    assert step.n == NDVE, (step.n, NDVE)


def top_attention(nc, g, sem):
    TOP, ROUND, TAKEN = 32, 8, -3.0e38
    NR = TOP // ROUND
    SCALE = float(D) ** -0.5
    d = {k[9:]: v for k, v in g.dram.items() if k.startswith("L2_xattn_")}
    names = ("load", "bo", "dve", "xn", "kv", "xT", "xTc", "q", "k", "v", "qf", "kf", "vc", "sc", "top", "bias", "exp",
             "read", "p", "pT", "pTc", "o", "oc", "y", "x",
             "passed")
    Sems = namedtuple("Sems", names)
    s = Sems(*(sem("t2_" + n) for n in names))
    with ExitStack() as ctx:
        sb, ps = allocators(nc, ctx)
        WqT, WkT, WvT, WoT = load_transposed(nc, g, sb, ps, sem, "t2", [d["W" + n] for n in "qkvo"])
        bq, bk = sb("t2_bq", [P, NC]), sb("t2_bk", [P, NC])
        bv, bo = sb("t2_bv", [P, D]), sb("t2_bo", [P, D])
        w = norm_scratch(sb, "t2")
        xn, xnT, kvT = sb("t2_xn", [P, NT, D]), sb("t2_xnT", [P, NC, S]), sb("t2_kvT", [P, NC, S])
        qf, kf, V = sb("t2_qf", [P, NC, S]), sb("t2_kf", [P, NC, S]), sb("t2_V", [P, NT, D])
        best, work = sb("t2_best", [P, NR, ROUND]), sb("t2_work", [P, 2, S])
        nb = sb("t2_nb", [P, NT])
        E, Pm = sb("t2_E", [P, 2, S]), sb("t2_Pm", [P, 2, S])
        PT, oT = sb("t2_PT", [P, NT, S]), sb("t2_oT", [P, NC, S])
        rsum, rinv = sb("t2_rsum", [P, NT]), sb("t2_rinv", [P, NT])
        pA, pB = ps("t2_pA", [P, NC, S]), ps("t2_pB", [P, NC, S])
        pS, pT = ps("t2_pS", [P, 2, S]), ps("t2_pT", [P, 2, S])
        pV = pS[:].rearrange("p a n -> p (a n)").rearrange("p (t n) -> p t n", t=NT)
        pY = pA[:].rearrange("p a n -> p (a n)").rearrange("p (t n) -> p t n", t=NT)
        NLOAD = 4
        NDVE = LN_STEPS + 1 + NT * (2 * NR - 1) + 2
        with nc.Block() as block:
            @block.sync
            def _(sp):
                for t, n in ((bq, "bq"), (bk, "bk")):
                    sp.dma_start(t[:], d[n].rearrange("(c p) -> p c", p=P),
                                 allow_slow_non_contiguous=True).then_inc(s.load, 16)
                for t, n in ((bv, "bv"), (bo, "bo")):
                    sp.dma_start(t[:], d[n].rearrange("(o n) -> o n", o=1).broadcast_to([P, D])).then_inc(s.load, 16)

            @block.gpsimd
            def _(pool):
                with pool.Fori(0, B) as i:
                    pool.wait_ge(s.xn, i + 1)
                    nc.gpsimd.tensor_copy(kvT[:], g.ctxT[:, :, bass.ds(i * S, S)]).then_inc(s.kv, 1)

            @block.tensor
            def _(pe):
                def project(out, W, src):
                    for m in range(NC):
                        for c in range(NC):
                            last = nc.tensor.matmul(out[:, m, :], W[:, c, m * P:(m + 1) * P], src[:, c, :],
                                                    start=c == 0, stop=c == NC - 1)
                    return last

                with pe.Fori(0, B) as i:
                    pe.wait_ge(s.xn, i + 1)
                    for c in range(NC):
                        for t in range(NT):
                            last = nc.tensor.transpose(pA[:, c, t * P:(t + 1) * P], xn[:, t, c * P:(c + 1) * P],
                                                       g.ident[:])
                    last.then_inc(s.xT, 1)
                    pe.wait_ge(s.kv, i + 1)
                    project(pB, WkT, kvT).then_inc(s.k, 1)
                    for t in range(NT):
                        for c in range(NC):
                            last = nc.tensor.matmul(pV[:, t, :], kvT[:, c, t * P:(t + 1) * P], WvT[:, c, :],
                                                    start=c == 0, stop=c == NC - 1)
                    last.then_inc(s.v, 1)
                    pe.wait_ge(s.xTc, i + 1)
                    project(pA, WqT, xnT).then_inc(s.q, 1)
                    pe.wait_ge(s.qf, i + 1)
                    pe.wait_ge(s.kf, i + 1)
                    pe.wait_ge(s.vc, i + 1)
                    for n in range(NT + 1):
                        if n < NT:
                            if n >= 2:
                                pe.wait_ge(s.exp, i * NT + n - 1)
                                pe.wait_ge(s.read, i * NT + n - 1)
                            for c in range(NC):
                                last = nc.tensor.matmul(pS[:, n % 2], qf[:, c, n * P:(n + 1) * P], kf[:, c, :],
                                                        start=c == 0, stop=c == NC - 1)
                            last.then_inc(s.sc, 1)
                        if n >= 1:
                            t = n - 1
                            pe.wait_ge(s.p, i * NT + t + 1)
                            if t >= 2:
                                pe.wait_ge(s.pTc, i * NT + t - 1)
                            for k in range(NT):
                                last = nc.tensor.transpose(pT[:, t % 2, k * P:(k + 1) * P],
                                                           Pm[:, t % 2, k * P:(k + 1) * P], g.ident[:])
                            last.then_inc(s.pT, 1)
                    pe.wait_ge(s.pTc, i * NT + NT)
                    for m in range(NC):
                        for k in range(NT):
                            last = nc.tensor.matmul(pB[:, m, :], V[:, k, m * P:(m + 1) * P], PT[:, k, :],
                                                    start=k == 0, stop=k == NT - 1)
                    last.then_inc(s.o, 1)
                    pe.wait_ge(s.oc, i + 1)
                    for t in range(NT):
                        for c in range(NC):
                            last = nc.tensor.matmul(pY[:, t, :], oT[:, c, t * P:(t + 1) * P], WoT[:, c, :],
                                                    start=c == 0, stop=c == NC - 1)
                    last.then_inc(s.y, 1)

            @block.scalar
            def _(act):
                act.wait_ge(s.load, 16 * NLOAD)
                with act.Fori(0, B) as i:
                    act.wait_ge(s.xT, i + 1)
                    nc.scalar.copy(xnT[:], pA[:]).then_inc(s.xTc, 1)
                    for src, dst, bias, ready, done in ((pB, kf, bk, s.k, s.kf), (pA, qf, bq, s.q, s.qf)):
                        act.wait_ge(ready, i + 1)
                        for c in range(NC):
                            last = nc.scalar.activation(dst[:, c], src[:, c], ACT.Identity, bias=bias[:, c:c + 1])
                        last.then_inc(done, 1)
                    for t in range(NT + 1):
                        if t < NT:
                            act.wait_ge(s.bias, i * NT + t + 1)
                            act.wait_ge(s.read, i * NT + t + 1)
                            if t >= 2:
                                act.wait_ge(s.p, i * NT + t - 1)
                            nc.scalar.activation(E[:, t % 2], pS[:, t % 2], ACT.Exp, bias=nb[:, t:t + 1], scale=SCALE
                                                 ).then_inc(s.exp, 1)
                        if t >= 1:
                            act.wait_ge(s.pT, i * NT + t)
                            nc.scalar.copy(PT[:, :, (t - 1) * P:t * P],
                                           pT[:, (t - 1) % 2].rearrange("p (k n) -> p k n", k=NT)).then_inc(s.pTc, 1)
                    act.wait_ge(s.o, i + 1)
                    nc.scalar.copy(oT[:], pB[:]).then_inc(s.oc, 1)

            @block.vector
            def _(dve):
                dve.wait_ge(s.load, 16 * NLOAD)
                nc.vector.tensor_scalar(bo[:], bo[:], g.tg[:, 0, 2:3], None, ALU.mult).then_inc(s.bo, 1)
                dve.wait_ge(s.bo, 1)

                def pass_wait():
                    dve.sem_inc(s.passed, 1)
                with dve.Fori(0, B) as i:
                    step = Steps(dve, s.dve, i * NDVE)
                    x = batch(g.x, i)
                    layernorm(nc, step, w, xn, x).then_inc(s.xn, 1)
                    dve.wait_ge(s.xn, i + 1)
                    step(nc.vector.tensor_tensor(x, x, bo[:].unsqueeze(1).broadcast_to([P, NT, D]), ALU.add))
                    dve.wait_ge(s.v, i + 1)
                    nc.vector.tensor_tensor(V[:], pV, bv[:].unsqueeze(1).broadcast_to([P, NT, D]), ALU.add
                                            ).then_inc(s.vc, 1)
                    for t in range(NT):
                        dve.wait_ge(s.sc, i * NT + t + 1)
                        if t >= 2:
                            dve.wait_ge(s.pT, i * NT + t - 1)
                        pass_wait()
                        src = pS[:, t % 2]
                        for k in range(NR):
                            step(nc.vector.max(best[:, k], src))
                            if k == 0:
                                nc.vector.tensor_scalar(nb[:, t:t + 1], best[:, 0, 0:1], -SCALE, None, ALU.mult
                                                        ).then_inc(s.bias, 1)
                            else:
                                pass_wait()
                            ins = nc.vector.match_replace(work[:, k % 2], best[:, k], src, TAKEN)
                            if k == 0:
                                ins.then_inc(s.read, 1)
                                dve.wait_ge(s.read, i * NT + t + 1)
                            else:
                                step(ins)
                            if k < NR - 1:
                                pass_wait()
                            src = work[:, k % 2]
                        dve.wait_ge(s.exp, i * NT + t + 1)
                        nc.vector.scalar_tensor_tensor(out=Pm[:, t % 2], in0=src, scalar=TAKEN, in1=E[:, t % 2],
                                                       op0=ALU.is_equal, op1=ALU.mult, accum_out=rsum[:, t:t + 1]
                                                       ).then_inc(s.p, 1)
                    dve.wait_ge(s.p, i * NT + NT)
                    step(nc.vector.reciprocal(rinv[:], rsum[:]))
                    step(nc.vector.tensor_scalar(rinv[:], rinv[:], g.tg[:, 0, 2:3], None, ALU.mult))
                    dve.wait_ge(s.y, i + 1)
                    for t in range(NT):
                        last = nc.vector.scalar_tensor_tensor(out=x[:, t, :], in0=pY[:, t, :], scalar=rinv[:, t:t + 1],
                                                              in1=x[:, t, :], op0=ALU.mult, op1=ALU.add)
                    last.then_inc(s.x, 1)
                    dve.wait_ge(s.x, i + 1)
                    assert step.n == NDVE, (step.n, NDVE)


def top_k(nc, step, k, E, prob, gt, eq, rank, tri, out):
    four = [P, NT, E, E]
    other, own = prob.unsqueeze(2).broadcast_to(four), prob.unsqueeze(3).broadcast_to(four)
    nc.vector.tensor_tensor(gt, other, own, ALU.is_gt)
    step(nc.vector.tensor_tensor(eq, other, own, ALU.is_equal))
    step(nc.vector.tensor_tensor(eq, eq, tri.unsqueeze(1).broadcast_to(four), ALU.mult))
    step(nc.vector.tensor_tensor(gt, gt, eq, ALU.add))
    step(nc.vector.tensor_reduce(rank, gt, AX.X, ALU.add))
    step(nc.vector.scalar_tensor_tensor(out=out, in0=rank, scalar=float(k), in1=prob, op0=ALU.is_lt, op1=ALU.mult))


def routing(nc, g, sem, r):
    tag, E, EL = r.tag, r.E, r.EL
    names = ("load", "const", "dve", "xn", "xT", "xTc", "logit", "ein", "exp", "w", "tp", "tpc", "tb", "sel")
    Sems = namedtuple("Sems", names)
    s = Sems(*(sem(f"{tag}r_{n}") for n in names))
    with ExitStack() as ctx:
        sb, ps = allocators(nc, ctx)
        w = norm_scratch(sb, tag + "r")
        xn, xnT = sb(tag + "r_xn", [P, NT, D]), sb(tag + "r_xnT", [P, NC, S])
        Wr = sb(tag + "r_Wr", [P, NC, EL])
        L = sb(tag + "r_L", [P, NT, EL])
        pr = sb(tag + "r_pr", [P, NT, E])
        a, b, c2 = (sb(f"{tag}r_{n}", [P, NT, 4]) for n in "abc")
        gt, eq = sb(tag + "r_gt", [P, NT, E, E]), sb(tag + "r_eq", [P, NT, E, E])
        rank, tri = sb(tag + "r_rank", [P, NT, E]), sb(tag + "r_tri", [P, E, E])
        bias = sb(tag + "r_bias", [P, EL])
        if r.kind == "expert_choice":
            R = B * E
            pt, work, best = sb(tag + "r_pt", [R, S]), sb(tag + "r_work", [R, S]), sb(tag + "r_best", [R, 8])
            chosen = sb(tag + "r_chosen", [R, S])
        pT, pL, pX = ps(tag + "r_pT", [P, NC, S]), ps(tag + "r_pL", [P, NT, EL]), ps(tag + "r_pX", [P, S])
        NLOAD = len(r.router) + (2 if r.kind == "grouped" else 0)
        NDVE = {"grouped": 2 + 7 + 5, "expert_choice": LN_STEPS + 1 + 2,
                "top": LN_STEPS + 1 + 3 + 5 + (2 if r.shared_gate else 0) + (3 if r.renorm else 0)}[r.kind]
        tgate = g.tg[:, 1, r.gate:r.gate + 1]
        with nc.Block() as block:
            @block.sync
            def _(sp):
                for dst, src in r.router:
                    sp.dma_start(Wr[:, :, dst], src, allow_slow_non_contiguous=True).then_inc(s.load, 16)
                if r.kind == "grouped":
                    sp.dma_start(bias[:, 0:2], r.biases[0].rearrange("(o n) -> o n", o=1).broadcast_to([P, 2])
                                 ).then_inc(s.load, 16)
                    sp.dma_start(bias[:, 2:10], r.biases[1].rearrange("(o n) -> o n", o=1).broadcast_to([P, 8])
                                 ).then_inc(s.load, 16)
                for dst, src in r.loads:
                    sp.dma_start(dst, src).then_inc(r.s_weights, 16)

            @block.gpsimd
            def _(pool):
                nc.gpsimd.memset(tri[:], 0.0).then_inc(s.const, 1)
                pool.wait_ge(s.const, 1)
                nc.gpsimd.affine_select(out=tri[:], in_=tri[:], compare_op=ALU.is_ge, fill=1.0, base=0,
                                        pattern=[[-1, E], [1, E]], channel_multiplier=0).then_inc(s.const, 1)

            @block.tensor
            def _(pe):
                pe.wait_ge(s.load, 16 * NLOAD)
                with pe.Fori(0, B) as i:
                    pe.wait_ge(s.xn, i + 1)
                    for c in range(NC):
                        for t in range(NT):
                            last = nc.tensor.transpose(pT[:, c, t * P:(t + 1) * P], xn[:, t, c * P:(c + 1) * P],
                                                       g.ident[:])
                    last.then_inc(s.xT, 1)
                    pe.wait_ge(s.xTc, 2 * i + 2)
                    for t in range(NT):
                        for c in range(NC):
                            last = nc.tensor.matmul(pL[:, t, :], xnT[:, c, t * P:(t + 1) * P], Wr[:, c, :],
                                                    start=c == 0, stop=c == NC - 1)
                    last.then_inc(s.logit, 1)
                if r.kind == "expert_choice":
                    pe.wait_ge(s.w, B)
                    for t in range(NT):
                        last = nc.tensor.transpose(pX[0:R, t * P:(t + 1) * P], r.weights[:, t, :], g.ident[:])
                    last.then_inc(s.tp, 1)
                    pe.wait_ge(s.sel, 1)
                    for t in range(NT):
                        last = nc.tensor.transpose(pX[:, t * R:(t + 1) * R], chosen[:, t * P:(t + 1) * P],
                                                   g.ident[0:R, 0:R])
                    last.then_inc(s.tb, 1)

            @block.scalar
            def _(act):
                with act.Fori(0, B) as i:
                    act.wait_ge(s.xT, i + 1)
                    nc.scalar.copy(xnT[:], pT[:]).then_inc(s.xTc, 1)
                    nc.scalar.copy(g.xT[:, :, bass.ds(i * S, S)], pT[:]).then_inc(s.xTc, 1)
                    act.wait_ge(s.ein, i + 1)
                    nc.scalar.activation(L[:], L[:], ACT.Exp).then_inc(s.exp, 1)

            @block.vector
            def _(dve):
                dve.wait_ge(s.load, 16 * NLOAD)
                dve.wait_ge(s.const, 2)

                def wide(x, n=E):
                    return x.unsqueeze(2).broadcast_to([P, NT, n])
                with dve.Fori(0, B) as i:
                    step = Steps(dve, s.dve, i * NDVE)
                    if r.kind == "grouped":
                        nc.vector.tensor_scalar(xn[:], batch(g.x2, i), 1.0, None, ALU.mult).then_inc(s.xn, 1)
                    else:
                        layernorm(nc, step, w, xn, batch(g.x, i)).then_inc(s.xn, 1)
                    dve.wait_ge(s.logit, i + 1)
                    if r.kind == "grouped":
                        eight = [P, NT, 2, 4]
                        Lg, Le = L[:, :, 0:2], L[:, :, 2:10].rearrange("p t (g e) -> p t g e", g=2)
                        step(nc.vector.tensor_tensor(L[:], pL[:], bias[:].unsqueeze(1).broadcast_to([P, NT, EL]),
                                                     ALU.add))
                        nc.vector.tensor_reduce(a[:, :, 0:1], Lg, AX.X, ALU.max)
                        step(nc.vector.tensor_reduce(b[:, :, 0:2], Le, AX.X, ALU.max))
                        nc.vector.tensor_tensor(Lg, Lg, a[:, :, 0:1].broadcast_to([P, NT, 2]), ALU.subtract)
                        nc.vector.tensor_tensor(Le, Le, b[:, :, 0:2].unsqueeze(3).broadcast_to(eight), ALU.subtract
                                                ).then_inc(s.ein, 1)
                        dve.wait_ge(s.exp, i + 1)
                        nc.vector.tensor_reduce(a[:, :, 0:1], Lg, AX.X, ALU.add)
                        step(nc.vector.tensor_reduce(a[:, :, 1:3], Le, AX.X, ALU.add))
                        step(nc.vector.reciprocal(b[:, :, 0:3], a[:, :, 0:3]))
                        step(nc.vector.tensor_tensor(Lg, Lg, b[:, :, 0:1].broadcast_to([P, NT, 2]), ALU.mult))
                        nc.vector.tensor_tensor(c2[:, :, 0:1], Lg[:, :, 0:1], Lg[:, :, 1:2], ALU.is_ge)
                        step(nc.vector.tensor_tensor(c2[:, :, 1:2], Lg[:, :, 0:1], Lg[:, :, 1:2], ALU.is_lt))
                        step(nc.vector.tensor_tensor(c2[:, :, 0:2], c2[:, :, 0:2], Lg, ALU.mult))
                        step(nc.vector.tensor_tensor(c2[:, :, 0:2], c2[:, :, 0:2], b[:, :, 1:3], ALU.mult))
                        step(nc.vector.tensor_tensor(pr[:].rearrange("p t (g e) -> p t g e", g=2), Le,
                                                     c2[:, :, 0:2].unsqueeze(3).broadcast_to(eight), ALU.mult))
                    else:
                        step(nc.vector.tensor_reduce(a[:, :, 0:1], pL[:, :, 0:E], AX.X, ALU.max))
                        if r.shared_gate:
                            nc.vector.tensor_scalar(L[:, :, E:E + 1], pL[:, :, E:E + 1], -1.0, None, ALU.mult)
                        nc.vector.tensor_tensor(L[:, :, 0:E], pL[:, :, 0:E], wide(a[:, :, 0]), ALU.subtract
                                                ).then_inc(s.ein, 1)
                        dve.wait_ge(s.exp, i + 1)
                        step(nc.vector.tensor_reduce(a[:, :, 0:1], L[:, :, 0:E], AX.X, ALU.add))
                        step(nc.vector.reciprocal(b[:, :, 0:1], a[:, :, 0:1]))
                    out = r.weights[:, :, bass.ds(i * r.EW, E)]
                    if r.kind == "expert_choice":
                        nc.vector.tensor_tensor(out, L[:, :, 0:E], wide(b[:, :, 0]), ALU.mult).then_inc(s.w, 1)
                    else:
                        if r.kind == "top":
                            step(nc.vector.tensor_tensor(pr[:], L[:, :, 0:E], wide(b[:, :, 0]), ALU.mult))
                        top_k(nc, step, r.k, E, pr[:], gt[:], eq[:], rank[:], tri[:], pr[:])
                        if r.renorm:
                            step(nc.vector.tensor_reduce(a[:, :, 0:1], pr[:], AX.X, ALU.add))
                            step(nc.vector.reciprocal(b[:, :, 0:1], a[:, :, 0:1]))
                            step(nc.vector.tensor_tensor(pr[:], pr[:], wide(b[:, :, 0]), ALU.mult))
                        if r.shared_gate:
                            step(nc.vector.tensor_scalar(a[:, :, 0:1], L[:, :, E:E + 1], 1.0, None, ALU.add))
                            step(nc.vector.reciprocal(b[:, :, 0:1], a[:, :, 0:1]))
                            nc.vector.tensor_scalar(r.weights[:, :, bass.ds(i * r.EW + E, 1)], b[:, :, 0:1], tgate,
                                                    None, ALU.mult)
                        if r.kind == "grouped":
                            nc.vector.tensor_scalar(out, pr[:], 1.0, None, ALU.mult).then_inc(s.w, 1)
                        else:
                            nc.vector.tensor_scalar(out, pr[:], tgate, None, ALU.mult).then_inc(s.w, 1)
                    dve.wait_ge(s.w, i + 1)
                    assert step.n == NDVE, (step.n, NDVE)
                if r.kind == "expert_choice":
                    dve.wait_ge(s.tp, 1)
                    nc.vector.tensor_copy(work[:], pX[0:R, :]).then_inc(s.tpc, 1)
                    nc.vector.tensor_copy(pt[:], pX[0:R, :]).then_inc(s.tpc, 1)
                    dve.wait_ge(s.tpc, 2)
                    for n in range(r.capacity // 8):
                        nc.vector.max(best[:], work[:]).then_inc(s.tpc, 1)
                        dve.wait_ge(s.tpc, 2 * n + 3)
                        nc.vector.match_replace(work[:], best[:], work[:], -1.0).then_inc(s.tpc, 1)
                        dve.wait_ge(s.tpc, 2 * n + 4)
                    nc.vector.scalar_tensor_tensor(out=chosen[:], in0=work[:], scalar=0.0, in1=pt[:],
                                                   op0=ALU.is_lt, op1=ALU.mult).then_inc(s.sel, 1)
                    dve.wait_ge(s.tb, 1)
                    nc.vector.tensor_scalar(r.weights[:], pX[:, 0:NT * R].rearrange("p (t r) -> p t r", t=NT), tgate,
                                            None, ALU.mult).then_inc(s.sel, 1)
                    dve.wait_ge(s.sel, 2)


def experts(nc, g, sem, r):
    tag = r.tag
    names = ("H", "sg", "ha", "hm", "Y", "acc", "fin", "dve", "x")
    Sems = namedtuple("Sems", names)
    s = Sems(*(sem(f"{tag}e_{n}") for n in names))
    units, outs = [], []
    for j, job in enumerate(r.jobs):
        for q in range(job.nf if job.glu else job.nf // 2):
            units.append((j, q))
        outs += [(j, n) for n in range(len(job.outs))]
    NU, NY = len(units), len(outs)
    glu = [r.jobs[j].glu for j, _ in units]
    NG, NA = sum(glu), NU - sum(glu)
    assert NU % 2 == 0
    FMAX = max(job.nf for job in r.jobs)
    with ExitStack() as ctx:
        sb, ps = allocators(nc, ctx)
        hT = sb(tag + "e_hT", [P, 2, FMAX, S])
        sg = sb(tag + "e_sg", [P, 2, S])
        acc = sb(tag + "e_acc", [P, NT, D])
        wf = sb(tag + "e_wf", [P, NT, r.EW])
        if r.final_norm is not None:
            nw, w = sb(tag + "e_nw", [P, D]), norm_scratch(sb, tag + "e")
        pH, pY = ps(tag + "e_pH", [P, 2, 2, S]), ps(tag + "e_pY", [P, 2, NT, D])

        def consumed(eng, u, i):
            ahead = 1 if u >= 0 else 0
            u %= NU
            if glu[u]:
                eng.wait_ge(s.hm, (i + ahead) * NG + sum(glu[:u + 1]))
            else:
                eng.wait_ge(s.ha, (i + ahead) * NA + u + 1 - sum(glu[:u + 1]))

        def hidden_free(eng, j, i):
            ahead = 1 if j >= 2 else 0
            before = j - 2 if j >= 2 else max(k for k in range(len(r.jobs)) if k % 2 == j % 2)
            eng.wait_ge(s.Y, (i + ahead) * NY + r.jobs[before].out0 + len(r.jobs[before].outs))

        def out_free(eng, y, i):
            ahead = 1 if y >= 2 else 0
            before = y - 2 if y >= 2 else max(k for k in range(NY) if k % 2 == y % 2)
            eng.wait_ge(s.acc, (i + ahead) * NY + before + 1)

        with nc.Block() as block:
            if r.final_norm is not None:
                @block.sync
                def _(sp):
                    sp.dma_start(nw[:], r.final_norm.rearrange("(o n) -> o n", o=1).broadcast_to([P, D])
                                 ).then_inc(s.fin, 16)

            @block.tensor
            def _(pe):
                pe.wait_ge(r.s_weights, 16 * len(r.loads))
                pe.sem_inc(s.Y, NY)
                with pe.Fori(0, B) as i:
                    def rhs(c):
                        return g.xT[:, c, bass.ds(i * S, S)]

                    def outputs(j):
                        job = r.jobs[j]
                        consumed(pe, job.last, i)
                        for n, (w2, _) in enumerate(job.outs):
                            y = job.out0 + n
                            out_free(pe, y, i)
                            for t in range(NT):
                                for f in range(job.nf):
                                    last = nc.tensor.matmul(pY[:, y % 2, t, :], hT[:, j % 2, f, t * P:(t + 1) * P],
                                                            w2(f), start=f == 0, stop=f == job.nf - 1)
                            last.then_inc(s.Y, 1)
                    for j, job in enumerate(r.jobs):
                        for u in range(job.first, job.last + 1):
                            q = u - job.first
                            consumed(pe, u - 2, i)
                            for k in range(2):
                                for c in range(NC):
                                    w1 = job.win(k, q, c) if job.glu else job.win(0, 2 * q + k, c)
                                    last = nc.tensor.matmul(pH[:, u % 2, k], w1, rhs(c),
                                                            start=c == 0, stop=c == NC - 1)
                            last.then_inc(s.H, 1)
                        if j >= 1:
                            outputs(j - 1)
                    outputs(len(r.jobs) - 1)

            @block.scalar
            def _(act):
                if NA:
                    act.sem_inc(s.ha, NA)
                with act.Fori(0, B) as i:
                    for u, (j, q) in enumerate(units):
                        if not glu[u] and q == 0:
                            hidden_free(act, j, i)
                        act.wait_ge(s.H, i * NU + u + 1)
                        if glu[u]:
                            nc.scalar.activation(sg[:, u % 2], pH[:, u % 2, 0], ACT.Silu).then_inc(s.sg, 1)
                        else:
                            nc.scalar.activation(hT[:, j % 2, 2 * q:2 * q + 2], pH[:, u % 2], ACT.Silu
                                                 ).then_inc(s.ha, 1)

            @block.vector
            def _(dve):
                if NG:
                    dve.sem_inc(s.hm, NG)
                dve.sem_inc(s.acc, NY)
                if r.final_norm is not None:
                    dve.wait_ge(s.fin, 16)
                with dve.Fori(0, B) as i:
                    x = batch(g.x, i)
                    nc.vector.tensor_scalar(acc[:], batch(g.x2, i) if r.final_norm is not None else x, 1.0, None,
                                            ALU.mult).then_inc(s.x, 1)
                    nc.vector.tensor_scalar(wf[:], r.weights[:, :, bass.ds(i * r.EW, r.EW)], 1.0, None, ALU.mult).then_inc(s.x, 1)
                    NX = 3
                    dve.wait_ge(s.x, i * NX + 2)

                    def add(j):
                        job = r.jobs[j]
                        for n, (_, col) in enumerate(job.outs):
                            y = job.out0 + n
                            dve.wait_ge(s.Y, (i + 1) * NY + y + 1)
                            if y >= 1:
                                dve.wait_ge(s.acc, (i + 1) * NY + y)
                            for t in range(NT):
                                scale = 1.0 if col is None else wf[:, t, col:col + 1]
                                last = nc.vector.scalar_tensor_tensor(out=acc[:, t, :], in0=pY[:, y % 2, t, :],
                                                                      scalar=scale, in1=acc[:, t, :],
                                                                      op0=ALU.mult, op1=ALU.add)
                            last.then_inc(s.acc, 1)
                    for j, job in enumerate(r.jobs):
                        for u in range(job.first, job.last + 1):
                            if glu[u]:
                                if u == job.first:
                                    hidden_free(dve, j, i)
                                dve.wait_ge(s.sg, i * NG + sum(glu[:u + 1]))
                                nc.vector.tensor_tensor(hT[:, j % 2, u - job.first], pH[:, u % 2, 1], sg[:, u % 2],
                                                        ALU.mult).then_inc(s.hm, 1)
                        if j >= 1:
                            add(j - 1)
                    add(len(r.jobs) - 1)
                    dve.wait_ge(s.acc, (i + 2) * NY)
                    if r.final_norm is not None:
                        step = Steps(dve, s.dve, i * (5 + RSQRT_STEPS + 1))
                        rms_rstd(nc, step, w, acc)
                        for t in range(NT):
                            last = nc.vector.scalar_tensor_tensor(out=acc[:, t, :], in0=acc[:, t, :],
                                                                  scalar=w.rstd[:, t:t + 1], in1=nw[:],
                                                                  op0=ALU.mult, op1=ALU.mult)
                        step(last)
                        nc.vector.scalar_tensor_tensor(out=x, in0=acc[:], scalar=g.tg[:, 1, r.gate:r.gate + 1],
                                                       in1=x, op0=ALU.mult, op1=ALU.add).then_inc(s.x, 1)
                        assert step.n == 5 + RSQRT_STEPS + 1, step.n
                    else:
                        nc.vector.tensor_scalar(x, acc[:], 1.0, None, ALU.mult).then_inc(s.x, 1)
                    dve.wait_ge(s.x, i * NX + 3)


def by_rows(w):
    return w.rearrange("(c p) n -> p c n", p=P)


def moe_layer(nc, g, sem, layer):
    with ExitStack() as ctx:
        sb, _ = allocators(nc, ctx)
        tag = f"m{layer}"
        d = {k[len(f"L{layer}_ffn_"):]: v for k, v in g.dram.items() if k.startswith(f"L{layer}_ffn_")}
        r = Shared()
        r.tag, r.gate, r.shared_gate, r.renorm, r.final_norm, r.biases = tag, layer, False, False, None, None
        r.s_weights, r.loads, r.jobs = sem(tag + "_weights"), [], []
        g.xT = sb(tag + "_xT", [P, NC, B * S])

        def job(glu, nf, win, outs):
            first = r.jobs[-1].last + 1 if r.jobs else 0
            out0 = r.jobs[-1].out0 + len(r.jobs[-1].outs) if r.jobs else 0
            r.jobs.append(Job(glu, nf, win, outs, first, first + (nf if glu else nf // 2) - 1, out0))

        def chunk(w, off=0):
            return lambda k, f, c: w[:, c, off + f * P:off + (f + 1) * P]
        if layer == 0:
            E, F = d["W2_experts"].shape[0], d["W2_experts"].shape[1]
            r.kind, r.E, r.EL, r.EW, r.k = "grouped", E, E + 2, E, 2
            r.router = [(slice(0, 2), by_rows(d["Wg_gate"])), (slice(2, 10), by_rows(d["We_gate"]))]
            r.biases = (d["group_bias"], d["expert_bias"])
            r.final_norm = d["norm2_w"]
            Wsi, Wso = sb(tag + "_Wsi", [P, NC, 2 * F]), sb(tag + "_Wso", [P, F // P, D])
            W1, W2 = sb(tag + "_W1", [P, NC, 2 * F]), sb(tag + "_W2", [P, E, F // P, D])
            r.loads = [(Wsi[:], by_rows(d["W_shared_in"])), (Wso[:], by_rows(d["W_shared_out"])),
                       (W1[:], by_rows(d["W1_shared"]))]
            r.loads += [(W2[:, e], by_rows(d["W2_experts"][e])) for e in range(E)]
            job(True, F // P, lambda k, f, c: Wsi[:, c, k * F + f * P:k * F + (f + 1) * P],
                [(lambda f: Wso[:, f, :], None)])
            job(True, F // P, lambda k, f, c: W1[:, c, k * F + f * P:k * F + (f + 1) * P],
                [((lambda f, e=e: W2[:, e, f, :]), e) for e in range(E)])
        elif layer == 1:
            E, _, F = d["w1"].shape
            r.kind, r.E, r.EL, r.EW = "expert_choice", E, E, E
            r.capacity = S * 2 // E
            r.router = [(e, d["choice_w"][e].rearrange("(c p) -> p c", p=P)) for e in range(E)]
            W1, W2 = sb(tag + "_W1", [P, E, NC, F]), sb(tag + "_W2", [P, E, F // P, D])
            for e in range(E):
                r.loads += [(W1[:, e], by_rows(d["w1"][e])), (W2[:, e], by_rows(d["w2"][e]))]
                job(False, F // P, (lambda k, f, c, e=e: W1[:, e, c, f * P:(f + 1) * P]),
                    [((lambda f, e=e: W2[:, e, f, :]), e)])
        elif layer == 2:
            E, _, F = d["w1"].shape
            r.kind, r.E, r.EL, r.EW, r.k, r.shared_gate = "top", E, E + 1, E + 1, 2, True
            r.router = [(slice(0, E), by_rows(d["router_w"])), (slice(E, E + 1), by_rows(d["shared_gate_w"]))]
            W1, W2 = sb(tag + "_W1", [P, E, NC, F]), sb(tag + "_W2", [P, E, F // P, D])
            Wg, Wd = sb(tag + "_Wg", [P, NC, 2 * F]), sb(tag + "_Wd", [P, F // P, D])
            r.loads = [(Wg[:], by_rows(d["shared_gate_up"])), (Wd[:], by_rows(d["shared_down"]))]
            for e in range(E):
                r.loads += [(W1[:, e], by_rows(d["w1"][e])), (W2[:, e], by_rows(d["w2"][e]))]
            job(True, F // P, lambda k, f, c: Wg[:, c, k * F + f * P:k * F + (f + 1) * P],
                [(lambda f: Wd[:, f, :], E)])
            for e in range(E):
                job(False, F // P, (lambda k, f, c, e=e: W1[:, e, c, f * P:(f + 1) * P]),
                    [((lambda f, e=e: W2[:, e, f, :]), e)])
        else:
            E, _, F = d["w1"].shape
            r.kind, r.E, r.EL, r.EW, r.k, r.renorm = "top", E, E, E, 4, True
            r.router = [(e, d["gate_w"][e].rearrange("(c p) -> p c", p=P)) for e in range(E)]
            W1, W3, W2 = (sb(f"{tag}_W{n}", shape) for n, shape in
                          (("1", [P, E, NC, F]), ("3", [P, E, NC, F]), ("2", [P, E, D])))
            for e in range(E):
                r.loads += [(W1[:, e], by_rows(d["w1"][e])), (W3[:, e], by_rows(d["w3"][e])), (W2[:, e], d["w2"][e])]
                job(True, 1, (lambda k, f, c, e=e: (W1, W3)[k][:, e, c, :]), [((lambda f, e=e: W2[:, e, :]), e)])
        r.weights = sb(tag + "_weights", [P, NT, B * r.EW])
        routing(nc, g, sem, r)
        experts(nc, g, sem, r)


@contextmanager
def stage(nc):
    with ExitStack() as ctx:
        taken = []

        def sem(name):
            taken.append(ctx.enter_context(nc.semaphore(name)))
            return taken[-1]
        yield sem
        with nc.Block() as block:
            @block.sync
            def _(sp):
                for one in taken:
                    sp.sem_clear(one)


def build(nc, dram, out):
    with ExitStack() as ctx:
        sb, _ = allocators(nc, ctx)

        def sem_kept(name):
            return ctx.enter_context(nc.semaphore(name))

        g = Shared()
        g.dram = dram
        g.x = sb("x_all", [P, B * NT, D])
        g.ctxT = sb("ctxT_all", [P, NC, B * S])
        g.gates, g.tg = sb("gates", [P, 2, 4]), sb("tanh_gates", [P, 2, 4])
        g.ident, g.ones, g.identb = sb("ident", [P, P]), sb("ones", [P, P]), sb("identb", [P, P], BF16)
        prepare(nc, g, sem_kept)
        with stage(nc) as sem:
            channel_attention(nc, g, sem)
        with ExitStack() as l0:
            g.x2 = l0.enter_context(nc.sbuf_tensor("x2_all", [P, B * NT, D], F32))
            d = {k[7:]: v for k, v in dram.items() if k.startswith("L0_ffn_")}
            d.update(cos=dram["rope_cos"], sin=dram["rope_sin"])
            with stage(nc) as sem:
                head_attention(nc, g, sem, "a0", "self", d, 0)
            with stage(nc) as sem:
                moe_layer(nc, g, sem, 0)
        with stage(nc) as sem:
            head_attention(nc, g, sem, "a1", "causal",
                           {"W" + n: dram["L1_xattn_w" + n] for n in "qkvo"}, 1)
        with stage(nc) as sem:
            moe_layer(nc, g, sem, 1)
        with stage(nc) as sem:
            top_attention(nc, g, sem)
        with stage(nc) as sem:
            moe_layer(nc, g, sem, 2)
        with stage(nc) as sem:
            head_attention(nc, g, sem, "a3", "biased",
                           {k[9:]: v for k, v in dram.items() if k.startswith("L3_xattn_")}, 3)
        with stage(nc) as sem:
            moe_layer(nc, g, sem, 3)
        s_out = sem_kept("out_stored")
        with nc.Block() as block:
            @block.sync
            def _(sp):
                sp.dma_start(out.rearrange("b (t p) d -> p (b t) d", p=P), g.x[:]).then_inc(s_out, 16)
                sp.wait_ge(s_out, 16)


def kernel(**inputs):
    import numpy as _np
    import concourse.bacc as _bacc
    from concourse import mybir as _mybir
    from concourse.bass_utils import run_bass_kernel_spmd as _run
    nc = _bacc.Bacc("TRN2", target_bir_lowering=False, num_devices=1)
    arrays, dram = {}, {}
    for name, a in inputs.items():
        a = _np.ascontiguousarray(a)
        arrays["in_" + name] = a
        dram[name] = nc.dram_tensor("in_" + name, a.shape, _mybir.dt.from_np(a.dtype), kind="ExternalInput").ap()
    freq = (1.0 / 10000.0 ** (_np.arange(0, DH, 2, dtype=_np.float32) / DH)).astype(_np.float32)
    angle = _np.arange(S, dtype=_np.float32)[:, None] * freq[None, :]
    sign = _np.tile(_np.array([-1, 1], _np.float32), DH // 2)
    for name, t in (("rope_cos", _np.repeat(_np.cos(angle), 2, 1)), ("rope_sin", _np.repeat(_np.sin(angle), 2, 1) * sign)):
        arrays["in_" + name] = _np.ascontiguousarray(_np.tile(t.T, (P // DH, 1)), dtype=_np.float32)
        dram[name] = nc.dram_tensor("in_" + name, (P, S), F32, kind="ExternalInput").ap()
    out = nc.dram_tensor("out_0", (B, S, D), F32, kind="ExternalOutput").ap()
    build(nc, dram, out)
    r = _run(nc, [arrays], core_ids=[0])
    return r.results[0]["out_0"]
```

```python
from collections import namedtuple
from contextlib import ExitStack, contextmanager

import concourse.bass as bass
from concourse import mybir

ALU = mybir.AluOpType
ACT = mybir.ActivationFunctionType
AX = mybir.AxisListType
F32 = mybir.dt.float32
BF16 = mybir.dt.bfloat16
I32 = mybir.dt.int32

P = 128
B, S, D = 8, 512, 256
NT = S // P
NC = D // P
NH, DH = 16, 16
HG = NH // 4
RSQRT_SEED = 0x5F3759DF
MASKED = -1.0e30
LN_EPS = 1e-5
RMS_EPS = 1e-6


NormScratch = namedtuple("NormScratch", "stats mean var rstd seed tmp")
Job = namedtuple("Job", "glu nf win outs first last out0")


class Shared:
    pass


class Steps:

    def __init__(self, eng, sem, base=0):
        self.eng, self.sem, self.base, self.n = eng, sem, base, 0
        self.between = None

    def __call__(self, ins):
        self.n += 1
        ins.then_inc(self.sem, 1)
        if self.between:
            self.between()
        self.eng.wait_ge(self.sem, self.base + self.n)


def rsqrt(nc, step, out, seed, tmp, val):
    step(nc.vector.tensor_scalar(seed.bitcast(I32), val.bitcast(I32), 1, None, ALU.logical_shift_right))
    step(nc.vector.tensor_scalar(out.bitcast(I32), seed.bitcast(I32), -1.0, float(RSQRT_SEED), ALU.mult, ALU.add))
    for _ in range(4):
        step(nc.vector.tensor_tensor(tmp, out, out, ALU.mult))
        step(nc.vector.scalar_tensor_tensor(out=seed, in0=tmp, scalar=-0.5, in1=val, op0=ALU.mult, op1=ALU.mult))
        step(nc.vector.scalar_tensor_tensor(out=out, in0=seed, scalar=1.5, in1=out, op0=ALU.add, op1=ALU.mult))


RSQRT_STEPS = 14
LN_STEPS = 4 + RSQRT_STEPS


def layernorm(nc, step, w, xn, x):
    for t in range(NT):
        last = nc.vector.bn_stats(w.stats[:, t, :], x[:, t, :])
    step(last)
    mean_rstd(nc, step, w)
    for t in range(NT):
        last = nc.vector.tensor_scalar(xn[:, t, :], x[:, t, :], w.mean[:, t:t + 1], w.rstd[:, t:t + 1],
                                       ALU.subtract, ALU.mult)
    return last


def mean_rstd(nc, step, w):
    st = w.stats
    nc.vector.tensor_tensor(w.mean[:], st[:, :, 1], st[:, :, 4], ALU.add)
    nc.vector.tensor_tensor(w.tmp[:], st[:, :, 1], st[:, :, 4], ALU.subtract)
    step(nc.vector.tensor_tensor(w.var[:], st[:, :, 2], st[:, :, 5], ALU.add))
    nc.vector.tensor_scalar(w.mean[:], w.mean[:], 0.5, None, ALU.mult)
    nc.vector.tensor_scalar(w.var[:], w.var[:], 1.0 / D, LN_EPS, ALU.mult, ALU.add)
    step(nc.vector.scalar_tensor_tensor(out=w.tmp[:], in0=w.tmp[:], scalar=0.25, in1=w.tmp[:], op0=ALU.mult,
                                        op1=ALU.mult))
    step(nc.vector.tensor_tensor(w.var[:], w.var[:], w.tmp[:], ALU.add))
    rsqrt(nc, step, w.rstd[:], w.seed[:], w.tmp[:], w.var[:])


def norm_scratch(sb, name, tiles=NT):
    return NormScratch(stats=sb(name + "_stats", [P, tiles, 6]),
                       **{n: sb(f"{name}_{n}", [P, tiles]) for n in ("mean", "var", "rstd", "seed", "tmp")})


def rms_rstd(nc, step, w, x):
    for t in range(NT):
        last = nc.vector.bn_stats(w.stats[:, t, :], x[:, t, :])
    step(last)
    st = w.stats
    nc.vector.tensor_tensor(w.mean[:], st[:, :, 1], st[:, :, 4], ALU.add)
    nc.vector.tensor_tensor(w.tmp[:], st[:, :, 1], st[:, :, 4], ALU.subtract)
    step(nc.vector.tensor_tensor(w.var[:], st[:, :, 2], st[:, :, 5], ALU.add))
    nc.vector.scalar_tensor_tensor(out=w.mean[:], in0=w.mean[:], scalar=0.25, in1=w.mean[:], op0=ALU.mult,
                                   op1=ALU.mult)
    nc.vector.tensor_scalar(w.var[:], w.var[:], 1.0 / D, RMS_EPS, ALU.mult, ALU.add)
    step(nc.vector.scalar_tensor_tensor(out=w.tmp[:], in0=w.tmp[:], scalar=0.25, in1=w.tmp[:], op0=ALU.mult,
                                        op1=ALU.mult))
    step(nc.vector.tensor_tensor(w.var[:], w.var[:], w.tmp[:], ALU.add))
    step(nc.vector.tensor_tensor(w.var[:], w.var[:], w.mean[:], ALU.add))
    rsqrt(nc, step, w.rstd[:], w.seed[:], w.tmp[:], w.var[:])


def allocators(nc, ctx):
    def sb(name, shape, dt=F32):
        return ctx.enter_context(nc.sbuf_tensor(name, shape, dt))

    def ps(name, shape, dt=F32):
        return ctx.enter_context(nc.psum_tensor(name, shape, dt))
    return sb, ps


def by_rows(w):
    return w.rearrange("(c p) n -> p c n", p=P)


def row_of(v):
    return v.rearrange("(o n) -> o n", o=1).broadcast_to([P, v.shape[0]])


def batch_of(t, i):
    return t[bass.ds(i, 1)].rearrange("o p c n -> (o p) c n")


def batch(t, i):
    return t[:, bass.ds(i * NT, NT), :]


def prepare(nc, g, sem):
    s_x, s_gate, s_zero, s_one, s_tanh = (sem("prep_" + n) for n in ("x", "gate", "zero", "one", "tanh"))
    with nc.Block() as block:
        @block.sync
        def _(sp):
            for h in range(2):
                b = slice(h * (B // 2) * NT, (h + 1) * (B // 2) * NT)
                r = slice(h * (B // 2), (h + 1) * (B // 2))
                sp.dma_start(g.x[:, b, :], g.dram["x"][r].rearrange("b (t p) d -> p (b t) d", p=P)).then_inc(s_x, 16)
            for k, name in enumerate(("g_xattn", "g_ffn")):
                sp.dma_start(g.gates[:, k, :], g.dram[name].rearrange("(o n) -> o n", o=1).broadcast_to([P, 4])
                             ).then_inc(s_gate, 16)
            sp.wait_ge(s_x, 32)

        @block.gpsimd
        def _(pool):
            nc.gpsimd.memset(g.ident[:], 0.0).then_inc(s_zero, 1)
            nc.gpsimd.memset(g.ones[:], 1.0).then_inc(s_one, 1)
            pool.wait_ge(s_zero, 1)
            nc.gpsimd.affine_select(out=g.ident[:], in_=g.ident[:], compare_op=ALU.not_equal, fill=1.0, base=0,
                                    pattern=[[-1, P]], channel_multiplier=1).then_inc(s_one, 1)

        @block.scalar
        def _(act):
            act.wait_ge(s_gate, 32)
            nc.scalar.activation(g.tg[:], g.gates[:], ACT.Tanh).then_inc(s_tanh, 1)
            act.wait_ge(s_tanh, 1)

        @block.vector
        def _(dve):
            dve.wait_ge(s_one, 2)
            nc.vector.tensor_copy(g.identb[:], g.ident[:]).then_inc(s_zero, 1)
            dve.wait_ge(s_zero, 2)


def channel_attention(nc, g, sem):
    names = ("load", "ctx", "free", "xn", "gram", "ctxT", "ctxTc", "exp_in", "exp", "m", "mT", "mTc", "y", "x",
             "dve", "const", "kept", "passed")
    Sems = namedtuple("Sems", names)
    s = Sems(*(sem("ca_" + n) for n in names))
    HW = 64
    with ExitStack() as ctx:
        sb, ps = allocators(nc, ctx)
        ctx_all = sb("ca_ctx_all", [P, B * NT, D])
        ctx_fix = sb("ca_ctx", [P, NT, D])
        ctxT = sb("ca_ctxT", [P, NC, S])
        xn = sb("ca_xn", [P, NT, D])
        w = norm_scratch(sb, "ca")
        col = {n: sb("ca_c" + n, [P, 2, NC]) for n in ("wq", "bq")}
        row = {n: sb("ca_r" + n, [P, 2, NC, HW]) for n in ("wk", "bk", "wv", "bv")}
        wp, bp, wp2 = (sb("ca_" + n, [P, NC]) for n in ("wp", "bp", "wp2"))
        gs = sb("ca_gs", [P, 320])
        T, U = sb("ca_T", [P, 2, NC, HW]), sb("ca_U", [P, 2, NC, HW])
        A, mx, sm, rc, cs = (sb("ca_" + n, [P, 2, NC]) for n in ("A", "mx", "sm", "rc", "cs"))
        cst = sb("ca_cst", [P, NC])
        Mbd, MT, Dg = (sb("ca_" + n, [P, NC, P]) for n in ("Mbd", "MT", "Dg"))
        pG = ps("ca_pG", [P, 512])
        pT = ps("ca_pT", [P, NC, S])
        pM = ps("ca_pM", [P, 512])
        pY = ps("ca_pY", [P, NT, D])
        G = gs[:, 0:128].rearrange("p (c e) -> p c e", c=NC)
        sx = gs[:, 128:130]
        sc = gs[:, 192:320].rearrange("p (c e) -> p c e", c=NC)
        NLOAD = 2 + 4 + 2 + 16
        K = LN_STEPS + 18
        with nc.Block() as block:
            @block.sync
            def _(sp):
                for h in range(2):
                    b = slice(h * (B // 2) * NT, (h + 1) * (B // 2) * NT)
                    r = slice(h * (B // 2), (h + 1) * (B // 2))
                    sp.dma_start(ctx_all[:, b, :], g.dram["ctx_1024"][r].rearrange("b (t p) d -> p (b t) d", p=P)
                                 ).then_inc(s.load, 16)
                for k, kind in enumerate("gl"):
                    for n in ("wq", "bq"):
                        sp.dma_start(col[n][:, k, :], g.dram[f"L0_xattn_{n}{kind}"].rearrange("(c p) -> p c", p=P),
                                     allow_slow_non_contiguous=True).then_inc(s.load, 16)
                sp.dma_start(wp[:], g.dram["L0_xattn_wp"].rearrange("(c p) -> p c", p=P),
                             allow_slow_non_contiguous=True).then_inc(s.load, 16)
                sp.dma_start(bp[:], g.dram["L0_xattn_bp"].rearrange("(c p) -> p c", p=P),
                             allow_slow_non_contiguous=True).then_inc(s.load, 16)
                for k, kind in enumerate("gl"):
                    for n in ("wk", "bk", "wv", "bv"):
                        v = g.dram[f"L0_xattn_{n}{kind}"].rearrange("(c j e) -> j c e", j=2, e=HW)
                        for j in range(2):
                            sp.dma_start(row[n][HW * j:HW * j + HW, k, :, :],
                                         v[j:j + 1].broadcast_to([HW, NC, HW])).then_inc(s.load, 16)
                sp.sem_inc(s.kept, 16)
                with sp.Fori(0, B) as i:
                    sp.wait_ge(s.ctxTc, i + 1)
                    sp.sem_inc(s.passed, 1)
                    sp.dma_start(batch_of(g.d_ctxT, i), ctxT[:]).then_inc(s.kept, 16)
                sp.wait_ge(s.kept, 16 + 16 * B)

            @block.gpsimd
            def _(pool):
                nc.gpsimd.memset(Mbd[:], 0.0).then_inc(s.const, 1)
                pool.wait_ge(s.load, 16 * NLOAD)
                pool.sem_inc(s.free, 1)
                with pool.Fori(0, B) as i:
                    pool.wait_ge(s.free, i + 1)
                    nc.gpsimd.tensor_copy(ctx_fix[:], batch(ctx_all, i)).then_inc(s.ctx, 1)

            @block.tensor
            def _(pe):
                with pe.Fori(0, B) as i:
                    pe.wait_ge(s.ctx, i + 1)
                    for c in range(NC):
                        for t in range(NT):
                            last = nc.tensor.transpose(pT[:, c, t * P:(t + 1) * P], ctx_fix[:, t, c * P:(c + 1) * P],
                                                       g.ident[:])
                    last.then_inc(s.ctxT, 1)
                    pe.wait_ge(s.xn, i + 1)
                    for c in range(NC):
                        for j in range(2):
                            h = slice((2 * c + j) * HW, (2 * c + j + 1) * HW)
                            o = slice(HW * j, HW * j + HW)
                            for t in range(NT):
                                nc.tensor.matmul(pG[o, c * HW:c * HW + HW], xn[:, t, h], ctx_fix[:, t, h],
                                                 start=t == 0, stop=t == NT - 1)
                            for t in range(NT):
                                nc.tensor.matmul(pG[o, 128 + c:129 + c], xn[:, t, h], g.ones[:, 0:1],
                                                 start=t == 0, stop=t == NT - 1)
                            for t in range(NT):
                                last = nc.tensor.matmul(pG[o, 192 + c * HW:192 + c * HW + HW], g.ones[:, 0:HW],
                                                        ctx_fix[:, t, h], start=t == 0, stop=t == NT - 1)
                    last.then_inc(s.gram, 1)
                    pe.wait_ge(s.ctxT, i + 1)
                    pe.wait_ge(s.m, i + 1)
                    for c in range(NC):
                        last = nc.tensor.transpose(pM[:, c * P:(c + 1) * P], Mbd[:, c, :], g.ident[:])
                    last.then_inc(s.mT, 1)
                    pe.wait_ge(s.mTc, i + 1)
                    pe.wait_ge(s.ctxTc, i + 1)
                    for t in range(NT):
                        for c in range(NC):
                            o = pY[:, t, c * P:(c + 1) * P]
                            nc.tensor.matmul(o, ctxT[:, c, t * P:(t + 1) * P], MT[:, c, :], start=True, stop=False)
                            last = nc.tensor.matmul(o, g.ones[:], Dg[:, c, :], start=False, stop=True)
                    last.then_inc(s.y, 1)

            @block.scalar
            def _(act):
                with act.Fori(0, B) as i:
                    act.wait_ge(s.ctxT, i + 1)
                    act.wait_ge(s.kept, i * 16 + 16)
                    nc.scalar.copy(ctxT[:], pT[:]).then_inc(s.ctxTc, 1)
                    act.wait_ge(s.exp_in, i + 1)
                    nc.scalar.activation(T[:], T[:], ACT.Exp, scale=float(D) ** -0.5).then_inc(s.exp, 1)
                    act.wait_ge(s.mT, i + 1)
                    nc.scalar.copy(MT[:], pM[:, 0:NC * P].rearrange("p (c n) -> p c n", c=NC)).then_inc(s.mTc, 1)
                act.wait_ge(s.mTc, B)

            @block.vector
            def _(dve):
                dve.wait_ge(s.load, 16 * NLOAD)
                dve.wait_ge(s.const, 1)
                first = Steps(dve, s.const, 1)
                first(nc.vector.tensor_scalar(wp2[:], wp[:], g.tg[:, 0, 0:1], 2.0, ALU.mult, ALU.mult))
                first(nc.vector.tensor_scalar(bp[:], bp[:], g.tg[:, 0, 0:1], None, ALU.mult))
                four = [P, 2, NC, HW]
                with dve.Fori(0, B) as i:
                    step = Steps(dve, s.dve, i * K)
                    layernorm(nc, step, w, xn, batch(g.x, i)).then_inc(s.xn, 1)
                    dve.wait_ge(s.gram, i + 1)
                    step(nc.vector.tensor_copy(gs[:, 0:130], pG[:, 0:130]))
                    step(nc.vector.tensor_copy(gs[:, 192:320], pG[:, 192:320]))
                    nc.vector.tensor_tensor(A[:], col["wq"][:], sx.unsqueeze(1).broadcast_to([P, 2, NC]), ALU.mult)
                    step(nc.vector.tensor_tensor(T[:], G.unsqueeze(1).broadcast_to(four),
                                                 col["wq"][:].unsqueeze(3).broadcast_to(four), ALU.mult))
                    step(nc.vector.scalar_tensor_tensor(out=A[:], in0=col["bq"][:], scalar=float(S), in1=A[:],
                                                        op0=ALU.mult, op1=ALU.add))
                    nc.vector.tensor_tensor(T[:], T[:], row["wk"][:], ALU.mult)
                    step(nc.vector.tensor_tensor(U[:], row["bk"][:], A[:].unsqueeze(3).broadcast_to(four), ALU.mult))
                    step(nc.vector.tensor_tensor(T[:], T[:], U[:], ALU.add))
                    step(nc.vector.tensor_tensor(U[:], row["wk"][:], sc.unsqueeze(1).broadcast_to(four), ALU.mult))
                    step(nc.vector.tensor_tensor(U[:], U[:], col["bq"][:].unsqueeze(3).broadcast_to(four), ALU.mult))
                    step(nc.vector.tensor_tensor(T[:], T[:], U[:], ALU.add))
                    step(nc.vector.tensor_reduce(mx[:], T[:], AX.X, ALU.max))
                    nc.vector.tensor_tensor(T[:], T[:], mx[:].unsqueeze(3).broadcast_to(four), ALU.subtract
                                            ).then_inc(s.exp_in, 1)
                    dve.wait_ge(s.exp, i + 1)
                    step(nc.vector.tensor_reduce(sm[:], T[:], AX.X, ALU.add))
                    step(nc.vector.reciprocal(rc[:], sm[:]))
                    step(nc.vector.tensor_tensor(rc[:], rc[:], wp2[:].unsqueeze(1).broadcast_to([P, 2, NC]), ALU.mult))
                    step(nc.vector.tensor_tensor(T[:], T[:], rc[:].unsqueeze(3).broadcast_to(four), ALU.mult))
                    step(nc.vector.tensor_tensor(U[:], T[:], row["bv"][:], ALU.mult))
                    nc.vector.tensor_tensor(T[:], T[:], row["wv"][:], ALU.mult)
                    step(nc.vector.tensor_reduce(cs[:], U[:], AX.X, ALU.add))
                    nc.vector.tensor_tensor(cst[:], cs[:, 0, :], bp[:], ALU.add)
                    for j in range(2):
                        q = slice(HW * j, HW * j + HW)
                        last = nc.vector.tensor_tensor(Mbd[q, :, HW * j:HW * j + HW], T[q, 0], T[q, 1], ALU.add)
                    step(last)
                    step(nc.vector.tensor_tensor(cst[:], cst[:], cs[:, 1, :], ALU.add))
                    for c in range(NC):
                        last = nc.vector.tensor_scalar(Dg[:, c, :], g.ident[:], cst[:, c:c + 1], None, ALU.mult)
                    last.then_inc(s.m, 1)
                    assert step.n == K, step.n
                    dve.wait_ge(s.y, i + 1)
                    x = batch(g.x, i)
                    nc.vector.tensor_tensor(x, pY[:], x, ALU.add).then_inc(s.x, 1)
                    dve.sem_inc(s.free, 1)
                dve.wait_ge(s.x, B)


PAIRS = ((0, 0), (0, 1), (1, 0), (1, 1), (0, 2), (2, 0))
KS = DH * len(PAIRS)
KM = KS + 3


def load_transposed(nc, g, sb, ps, sem, tag, weights):
    s_in, s_t, s_c = sem(tag + "_w_in"), sem(tag + "_w_t"), sem(tag + "_w_c")
    turned = [sb(f"{tag}_wT{n}", [P, NC, D]) for n in range(len(weights))]
    with ExitStack() as ctx:
        sb2, ps2 = allocators(nc, ctx)
        raw = [sb2(f"{tag}_raw{n}", [P, NC, D]) for n in range(len(weights))]
        pW = ps2(tag + "_pW", [P, 2, NC, D])
        with nc.Block() as block:
            @block.sync
            def _(sp):
                for n, wt in enumerate(weights):
                    sp.dma_start(raw[n][:], wt.rearrange("(c p) k -> p c k", p=P)).then_inc(s_in, 16)

            @block.tensor
            def _(pe):
                pe.wait_ge(s_in, 16 * len(weights))
                for n in range(len(weights)):
                    if n >= 2:
                        pe.wait_ge(s_c, n - 1)
                    for c in range(NC):
                        for k in range(NC):
                            last = nc.tensor.transpose(pW[:, n % 2, k, c * P:(c + 1) * P],
                                                       raw[n][:, c, k * P:(k + 1) * P], g.ident[:])
                    last.then_inc(s_t, 1)

            @block.scalar
            def _(act):
                for n in range(len(weights)):
                    act.wait_ge(s_t, n + 1)
                    nc.scalar.copy(turned[n][:], pW[:, n % 2]).then_inc(s_c, 1)
                act.wait_ge(s_c, len(weights))
    return turned


def head_attention(nc, g, sem, tag, kind, wts, gate):
    self_attn, causal, biased = kind == "self", kind == "causal", kind == "biased"
    names = ("load", "scaled", "const", "dve", "pool", "xn", "xT", "xTc", "kv", "passed", "cT", "cTc", "q", "qsw", "k",
             "ksw", "v", "qf", "kf", "qm", "qr", "km", "kr", "vc", "qp", "kp", "qw", "kw", "qs", "ks", "S", "max",
             "mm", "mT", "mTc", "mw", "mrow", "ST", "exp", "pv", "oev", "ot", "nrm", "ob", "otc", "y", "x", "kept")
    Sems = namedtuple("Sems", names)
    s = Sems(*(sem(f"{tag}_{n}") for n in names))
    HC = 64
    NS = NH * NT
    NW = HG * NT
    MAIN = NW + 1
    FIRST_MAX = 4
    MAX_SLOTS = NW - FIRST_MAX
    cut = [NS * n // MAX_SLOTS for n in range(MAX_SLOTS + 1)]
    NORM_SLOT = 2 * NT + 1

    def max_units(slot):
        n = slot - FIRST_MAX
        return range(cut[n], cut[n + 1]) if 0 <= n < MAX_SLOTS else ()

    def wait(eng, semaphore, value):
        if not isinstance(value, int) or value > 0:
            eng.wait_ge(semaphore, value)

    def run(eng, front, turn):
        front(0, 0)
        turn(0, 0, False, True, True)
        with eng.Fori(1, B - 2, 2) as i:
            turn(i, 1, True, True, True)
            turn(i + 1, 0, True, True, True)
        turn(B - 1, 1, True, True, False)
        turn(B, 0, True, False, False)

    with ExitStack() as ctx:
        sb, ps = allocators(nc, ctx)
        if self_attn:
            Wq, Wqs, Wks = sb(tag + "_Wq", [P, NC, D]), sb(tag + "_Wqs", [P, NC, D]), sb(tag + "_Wks", [HC, D])
            Wc, Wkv = sb(tag + "_Wc", [P, NC, 2, HC]), sb(tag + "_Wkv", [P, D])
            Wk, Wv = Wkv[0:HC], Wkv[HC:P]
            Wo = sb(tag + "_Wo", [P, NC, D])
            kvc = sb(tag + "_kvc", [P, S])
            cos, sin = sb(tag + "_cos", [P, S]), sb(tag + "_sin", [P, S])
            normw = sb(tag + "_normw", [P, D])
        else:
            Wq, Wk, Wv, Wo = load_transposed(nc, g, sb, ps, sem, tag, [wts[n] for n in ("Wq", "Wk", "Wv", "Wo")])
            kvT = sb(tag + "_kvT", [P, NC, S])
        if biased:
            bq, bk = sb(tag + "_bq", [P, NC]), sb(tag + "_bk", [P, NC])
            bv, bo = sb(tag + "_bv", [P, D]), sb(tag + "_bo", [P, D])
        if causal:
            mask_q, mask_k = sb(tag + "_mask_q", [P, P], BF16), sb(tag + "_mask_k", [P, P], BF16)
        xnT, w = sb(tag + "_xnT", [P, NC, S]), norm_scratch(sb, tag)
        rope = sb(tag + "_rope", [P, NC, S])
        xn = rope[:].rearrange("p c n -> p (c n)").rearrange("p (t n) -> p t n", t=NT)
        qf, qp = sb(tag + "_qf", [P, NC, S]), sb(tag + "_qp", [P, 3, NC, S], BF16)
        kf, kp = (qf, qp) if self_attn else (sb(tag + "_kf", [P, NC, S]), sb(tag + "_kp", [P, 3, NC, S], BF16))
        qs, ks = sb(tag + "_qs", [P, 2, NH, S], BF16), sb(tag + "_ks", [P, 2, NH, S], BF16)
        V = sb(tag + "_V", [P, 2, NT, NH, 32])
        nm, nr = sb(tag + "_nm", [P, NT, NH]), sb(tag + "_nr", [P, NT, NH])
        mm, mTb = sb(tag + "_mm", [P, NT, 3, NH], BF16), sb(tag + "_mTb", [3 * NH, S], BF16)
        Pb = sb(tag + "_P", [P, 2, 4, S])
        Osb, rd = sb(tag + "_Osb", [P, HG, S]), sb(tag + "_rd", [P, NT, NH])
        On = Pb[:, 1, 0:2].rearrange("p c n -> p (c n)").rearrange("p (t n) -> p t n", t=NT)
        onT = Pb[:, 1, 2:4]
        pST, pS = ps(tag + "_pST", [P, 2, 2, S]), ps(tag + "_pS", [P, 2, S])
        pO, pM = ps(tag + "_pO", [P, S]), ps(tag + "_pM", [P, S])

        def by_tokens(t):
            return t.rearrange("p a n -> p (a n)").rearrange("p (t n) -> p t n", t=NT)
        half = {n: pST[:, m % 2] for m, n in enumerate(("xT", "C", "Q", "Qs", "K", "Ks", "V") if self_attn else
                                                       ("xT", "Q", "K", "V"))}
        pV, pY = by_tokens(half["V"]), by_tokens(pS[:])
        d_parts = {n: nc.dram_tensor(f"{tag}_d{n}", (3, D, S), BF16, kind="Internal").ap() for n in "qk"}
        d_max = nc.dram_tensor(f"{tag}_dm", (3 * NH, S), BF16, kind="Internal").ap()
        NLOAD = {"self": 9, "causal": 0, "biased": 4}[kind]
        NCONST = {"self": 3 + 4, "causal": 3 + 2, "biased": 3}[kind]
        with nc.Block() as block:
            @block.sync
            def _(sp):
                if self_attn:
                    sp.dma_start(Wq[:], by_rows(wts["Wq"])).then_inc(s.load, 16)
                    sp.dma_start(Wo[:], by_rows(wts["Wo"])).then_inc(s.load, 16)
                    sp.dma_start(Wk, wts["Wk"]).then_inc(s.load, 16)
                    sp.dma_start(Wv, wts["Wv"]).then_inc(s.load, 16)
                    for n, m in enumerate(("Wk_c", "Wv_c")):
                        sp.dma_start(Wc[:, :, n], by_rows(wts[m])).then_inc(s.load, 16)
                    for table, name in ((cos, "cos"), (sin, "sin")):
                        sp.dma_start(table[:], wts[name]).then_inc(s.load, 16)
                    sp.dma_start(normw[:], row_of(wts["norm1_w"])).then_inc(s.load, 16)
                if biased:
                    for t, n in ((bq, "bq"), (bk, "bk")):
                        sp.dma_start(t[:], wts[n].rearrange("(c p) -> p c", p=P),
                                     allow_slow_non_contiguous=True).then_inc(s.load, 16)
                    for t, n in ((bv, "bv"), (bo, "bo")):
                        sp.dma_start(t[:], row_of(wts[n])).then_inc(s.load, 16)

                def load_ctx(n):
                    if not self_attn:
                        wait(sp, s.v, n)
                        sp.sem_inc(s.passed, 1)
                        sp.dma_start(kvT[:], batch_of(g.d_ctxT, n)).then_inc(s.kv, 16)

                def front(n, pn):
                    if isinstance(n, int) and n == 0:
                        load_ctx(n)
                    for src, dram, dst, ready, wrote, there in (
                            (qp, d_parts["q"], qs, s.qp, s.qw, s.qs), (kp, d_parts["k"], ks, s.kp, s.kw, s.ks)):
                        sp.wait_ge(ready, n + 1)
                        for r in range(3):
                            sp.dma_start(dram[r].rearrange("(c p) t -> p c t", p=P), src[:, r]).then_inc(wrote, 16)
                        sp.wait_ge(wrote, n * 48 + 48)
                        for m, pair in enumerate(PAIRS):
                            r = pair[0] if dst is qs else pair[1]
                            sp.dma_start(dst[DH * m:DH * m + DH, pn], dram[r].rearrange("(h d) t -> d h t", d=DH)
                                         ).then_inc(there, 16)

                def turn(k, pk, before, now, after):
                    if after:
                        load_ctx(k + 1)
                    if now:
                        sp.wait_ge(s.mTc, k + 1)
                        sp.dma_start(d_max, mTb[:]).then_inc(s.mw, 16)
                        sp.wait_ge(s.mw, k * 16 + 16)
                        sp.dma_start(qs[KS:KM, pk], d_max.rearrange("(r h) t -> r h t", h=NH)).then_inc(s.mrow, 16)
                    if after:
                        front(k + 1, 1 - pk)
                run(sp, front, turn)

            @block.gpsimd
            def _(pool):
                pre = Steps(pool, s.pool)
                nc.gpsimd.memset(V[:], 0.0).then_inc(s.const, 1)
                pool.wait_ge(s.const, 1)
                nc.gpsimd.memset(V[:, :, :, :, DH:DH + 1], 1.0).then_inc(s.const, 1)
                pool.wait_ge(s.const, 2)
                nc.gpsimd.memset(ks[KS:P], 1.0).then_inc(s.const, 1)
                pool.wait_ge(s.const, 3)
                if causal:
                    pre(nc.gpsimd.memset(mask_q[:], 0.0))
                    pre(nc.gpsimd.memset(mask_k[:], 0.0))
                    nc.gpsimd.affine_select(out=mask_q[:], in_=mask_q[:], compare_op=ALU.is_ge, fill=MASKED, base=0,
                                            pattern=[[-1, P]], channel_multiplier=1).then_inc(s.const, 1)
                    nc.gpsimd.affine_select(out=mask_k[:], in_=mask_k[:], compare_op=ALU.is_ge, fill=MASKED, base=0,
                                            pattern=[[1, P]], channel_multiplier=-1).then_inc(s.const, 1)
                if self_attn:
                    pool.wait_ge(s.load, 16 * NLOAD)
                    for e in range(2):
                        nc.gpsimd.tensor_copy(Wqs[:].rearrange("p c (n e) -> p c n e", e=2)[:, :, :, e],
                                              Wq[:].rearrange("p c (n e) -> p c n e", e=2)[:, :, :, 1 - e]
                                              ).then_inc(s.const, 1)
                        pool.wait_ge(s.const, 3 + 2 * e + 1)
                        nc.gpsimd.tensor_copy(Wks[:].rearrange("p (n e) -> p n e", e=2)[:, :, e],
                                              Wk.rearrange("p (n e) -> p n e", e=2)[:, :, 1 - e]
                                              ).then_inc(s.const, 1)
                        pool.wait_ge(s.const, 3 + 2 * e + 2)
                npre = pre.n
                one = g.ones[:, 0:1].unsqueeze(2).broadcast_to([P, NC, S])

                def front(n, pn):
                    go = Steps(pool, s.pool, n * 3 + npre)
                    pool.wait_ge(s.kf, n + 1)
                    wait(pool, s.kw, n * 48)
                    go(nc.gpsimd.tensor_tensor(kp[:, 0], kf[:], one, ALU.mult))
                    go(nc.gpsimd.tensor_tensor(kf[:], kf[:], kp[:, 0], ALU.subtract))
                    go(nc.gpsimd.tensor_tensor(kp[:, 1], kf[:], one, ALU.mult))
                    nc.gpsimd.tensor_tensor(kp[:, 2], kf[:], kp[:, 1], ALU.subtract).then_inc(s.kp, 1)

                def turn(k, pk, before, now, after):
                    if after:
                        front(k + 1, 1 - pk)
                if not self_attn:
                    run(pool, front, turn)

            @block.tensor
            def _(pe):
                if NLOAD:
                    pe.wait_ge(s.load, 16 * NLOAD)
                pe.wait_ge(s.const, NCONST)
                pe.wait_ge(s.scaled, 1)

                def project(out, W, src):
                    for m in range(NC):
                        for c in range(len(W)):
                            last = nc.tensor.matmul(out[:, m, :], W[c][:, m * P:(m + 1) * P], src[c],
                                                    start=c == 0, stop=c == len(W) - 1)
                    return last

                def tiles(W):
                    return [W[:, c, :] for c in range(NC)]

                def front_xT(n, b):
                    pe.wait_ge(s.xn, n + 1)
                    if b is None:
                        wait(pe, s.vc, n)
                        if not self_attn:
                            wait(pe, s.kf, n)
                    else:
                        pe.wait_ge(s.exp, (b + 1) * 2 * NW)
                    for c in range(NC):
                        for t in range(NT):
                            last = nc.tensor.transpose(half["xT"][:, c, t * P:(t + 1) * P],
                                                       xn[:, t, c * P:(c + 1) * P], g.ident[:])
                    last.then_inc(s.xT, 1)

                def front_compressed(n):
                    pe.wait_ge(s.xTc, n + 1)
                    wait(pe, s.kf, n)
                    for c in range(NC):
                        last = nc.tensor.matmul(half["C"][:, 0], Wc[:, c].rearrange("p n j -> p (n j)"), xnT[:, c, :],
                                                start=c == 0, stop=c == NC - 1)
                    last.then_inc(s.cT, 1)

                def front_q(n):
                    pe.wait_ge(s.xTc, n + 1)
                    if not self_attn:
                        wait(pe, s.vc, n)
                    project(half["Q"], tiles(Wq), tiles(xnT)).then_inc(s.q, 1)

                def front_q_swapped(n):
                    pe.wait_ge(s.cTc, n + 1)
                    project(half["Qs"], tiles(Wqs), tiles(xnT)).then_inc(s.qsw, 1)

                def front_k(n):
                    if self_attn:
                        pe.wait_ge(s.qm, n + 1)
                        project(half["K"], [Wk], [kvc[0:HC]]).then_inc(s.k, 1)
                    else:
                        pe.wait_ge(s.kv, n * 16 + 16)
                        project(half["K"], tiles(Wk), tiles(kvT)).then_inc(s.k, 1)

                def front_k_swapped(n):
                    pe.wait_ge(s.qr, n + 1)
                    project(half["Ks"], [Wks[:]], [kvc[0:HC]]).then_inc(s.ksw, 1)

                def front_v(n):
                    pe.wait_ge(s.km if self_attn else s.qf, n + 1)
                    for t in range(NT):
                        if self_attn:
                            last = nc.tensor.matmul(pV[:, t, :], kvc[HC:P, t * P:(t + 1) * P], Wv,
                                                    start=True, stop=True)
                        else:
                            for c in range(NC):
                                last = nc.tensor.matmul(pV[:, t, :], kvT[:, c, t * P:(t + 1) * P], Wv[:, c, :],
                                                        start=c == 0, stop=c == NC - 1)
                    last.then_inc(s.v, 1)

                def maxima(units, a, pa):
                    for n in units:
                        if n == 0:
                            pe.wait_ge(s.qs, a * 96 + 96)
                            pe.wait_ge(s.ks, a * 96 + 96)
                            wait(pe, s.x, a)
                        h, t = divmod(n, NT)
                        if n >= 2:
                            pe.wait_ge(s.max, a * NS + n - 1)
                        keys = (t + 1) * P if causal else S
                        last = nc.tensor.matmul(pS[:, n % 2, 0:keys], qs[0:KS, pa, h, t * P:(t + 1) * P],
                                                ks[0:KS, pa, h, 0:keys], start=True, stop=not causal)
                        if causal:
                            last = nc.tensor.matmul(pS[:, n % 2, t * P:keys], g.identb[:], mask_q[:],
                                                    start=False, stop=True)
                        last.then_inc(s.S, 1)

                def turn_maxima(a):
                    pe.wait_ge(s.mm, a + 1)
                    for t in range(NT):
                        last = nc.tensor.matmul(pS[0:3 * NH, 0, t * P:(t + 1) * P],
                                                mm[:, t].rearrange("p r h -> p (r h)"), g.identb[:],
                                                start=True, stop=True)
                    last.then_inc(s.mT, 1)

                def scores(slot, pair, b, pb):
                    hg, kt = divmod(slot, NT)
                    lo = kt * P if causal else 0
                    if slot == 0 and pair == 0:
                        pe.wait_ge(s.mrow, b * 16 + 16)
                        fronts = min(b + 2, B) if isinstance(b, int) else b + 2
                        pe.wait_ge(s.kf, fronts)
                        pe.wait_ge(s.vc, fronts)
                    if slot >= 1:
                        pe.wait_ge(s.exp, b * 2 * NW + 2 * slot + pair - 1)
                    for j in range(2):
                        h = 4 * hg + 2 * pair + j
                        o = pST[:, pair, j]
                        last = nc.tensor.matmul(o[:, lo:S], ks[0:KM, pb, h, kt * P:(kt + 1) * P],
                                                qs[0:KM, pb, h, lo:S], start=True, stop=not causal)
                        if causal:
                            last = nc.tensor.matmul(o[:, lo:lo + P], g.identb[:], mask_k[:],
                                                    start=False, stop=True)
                    last.then_inc(s.ST, 1)

                def values(n, pair, b, pb):
                    hg, kt = divmod(n, NT)
                    lo = kt * P if causal else 0
                    if pair == 0:
                        if kt == 0 and hg >= 1:
                            pe.wait_ge(s.oev, b * HG + hg)
                        pe.wait_ge(s.exp, b * 2 * NW + 2 * n + 2)
                    for j in range(2 * pair, 2 * pair + 2):
                        last = nc.tensor.matmul(pO[32 * j:32 * j + 32, lo:S], V[:, pb, kt, 4 * hg + j, :],
                                                Pb[:, n % 2, j, lo:S], start=kt == 0, stop=kt == NT - 1)
                    if pair == 1:
                        last.then_inc(s.pv, 1)

                def turn_output(b, t):
                    if t == 0:
                        pe.wait_ge(s.oev, b * HG + HG)
                    if t >= 2:
                        pe.wait_ge(s.nrm, b * NT + t - 1)
                    for h in range(HG):
                        last = nc.tensor.transpose((pM, pO)[t % 2][:, h * P:(h + 1) * P],
                                                   Osb[:, h, t * P:(t + 1) * P], g.ident[:])
                    last.then_inc(s.ot, 1)

                def turn_back(b):
                    pe.wait_ge(s.nrm, b * NT + NT)
                    wait(pe, s.mTc, min(b + 2, B) if isinstance(b, int) else b + 2)
                    for c in range(NC):
                        for t in range(NT):
                            last = nc.tensor.transpose(pS[:, c, t * P:(t + 1) * P],
                                                       On[:, t, c * P:(c + 1) * P], g.ident[:])
                    last.then_inc(s.ob, 1)

                def project_output(b):
                    pe.wait_ge(s.otc, b + 1)
                    for t in range(NT):
                        for c in range(NC):
                            last = nc.tensor.matmul(pY[:, t, :], onT[:, c, t * P:(t + 1) * P], Wo[:, c, :],
                                                    start=c == 0, stop=c == NC - 1)
                    last.then_inc(s.y, 1)

                def front(n, pn):
                    front_xT(n, None)
                    if self_attn:
                        front_compressed(n)
                    front_q(n)
                    if self_attn:
                        front_q_swapped(n)
                    front_k(n)
                    if self_attn:
                        front_k_swapped(n)
                    front_v(n)

                def turn(k, pk, before, now, after):
                    for slot in range(MAIN):
                        units = max_units(slot) if now else ()
                        for part in range(4):
                            if before and part < 2 and slot < NW:
                                scores(slot, part, k - 1, 1 - pk)
                            if before and part >= 2 and slot >= 1:
                                values(slot - 1, part - 2, k - 1, 1 - pk)
                            maxima(units[len(units) * part // 4:len(units) * (part + 1) // 4], k, pk)
                    if after:
                        front_xT(k + 1, k - 1 if before else None)
                    if now:
                        turn_maxima(k)
                    for t in range(NT):
                        if after and t == 0 and self_attn:
                            front_compressed(k + 1)
                        if after and t == 2:
                            front_q(k + 1)
                        if before:
                            turn_output(k - 1, t)
                    if after:
                        if self_attn:
                            front_q_swapped(k + 1)
                        front_k(k + 1)
                    if before:
                        turn_back(k - 1)
                    if after:
                        if self_attn:
                            front_k_swapped(k + 1)
                        front_v(k + 1)
                    if before:
                        project_output(k - 1)
                run(pe, front, turn)

            @block.scalar
            def _(act):
                if biased:
                    act.wait_ge(s.load, 16 * NLOAD)
                act.wait_ge(s.const, NCONST)
                def shifted(dst, src, bias):
                    if not biased:
                        return nc.scalar.copy(dst[:], src)
                    for c in range(NC):
                        last = nc.scalar.activation(dst[:, c], src[:, c], ACT.Identity, bias=bias[:, c:c + 1])
                    return last

                def turned_x(n):
                    act.wait_ge(s.xT, n + 1)
                    nc.scalar.copy(xnT[:], half["xT"]).then_inc(s.xTc, 1)

                def front_early(n):
                    if self_attn:
                        act.wait_ge(s.cT, n + 1)
                        nc.scalar.copy(kvc[:], half["C"][:, 0]).then_inc(s.cTc, 1)
                    else:
                        act.wait_ge(s.q, n + 1)
                        wait(act, s.qp, n)
                        shifted(qf, half["Q"], bq if biased else None).then_inc(s.qf, 1)
                        act.wait_ge(s.k, n + 1)
                        wait(act, s.kp, n)
                        shifted(kf, half["K"], bk if biased else None).then_inc(s.kf, 1)

                def front_late(n, pn):
                    if not biased:
                        act.wait_ge(s.v, n + 1)
                        nc.scalar.copy(V[:, pn, :, :, 0:DH], pV.rearrange("p t (h d) -> p t h d", d=DH)
                                       ).then_inc(s.vc, 1)

                def front(n, pn):
                    turned_x(n)
                    front_early(n)
                    front_late(n, pn)

                def turn(k, pk, before, now, after):
                    b = k - 1
                    if before:
                        for slot in range(NW):
                            lo = (slot % NT) * P if causal else 0
                            if slot == 1:
                                wait(act, s.x, k)
                            if slot >= 2:
                                act.wait_ge(s.pv, b * NW + slot - 1)
                            for pair in range(2):
                                act.wait_ge(s.ST, b * 2 * NW + 2 * slot + pair + 1)
                                nc.scalar.activation(Pb[:, slot % 2, 2 * pair:2 * pair + 2, lo:S],
                                                     pST[:, pair, :, lo:S], ACT.Exp, scale=float(DH) ** -0.5
                                                     ).then_inc(s.exp, 1)
                    if after:
                        turned_x(k + 1)
                    if now:
                        act.wait_ge(s.mT, k + 1)
                        nc.scalar.copy(mTb[:], pS[0:3 * NH, 0]).then_inc(s.mTc, 1)
                    if after:
                        front_early(k + 1)
                    if before:
                        act.wait_ge(s.ob, b + 1)
                        nc.scalar.copy(onT, pS[:]).then_inc(s.otc, 1)
                    if after:
                        front_late(k + 1, 1 - pk)
                run(act, front, turn)

            @block.vector
            def _(dve):
                if NLOAD:
                    dve.wait_ge(s.load, 16 * NLOAD)
                dve.wait_ge(s.const, NCONST)
                if self_attn:
                    dve.sem_inc(s.scaled, 1)
                else:
                    if biased:
                        nc.vector.tensor_scalar(bo[:], bo[:], g.tg[:, 0, gate:gate + 1], None, ALU.mult)
                    nc.vector.tensor_scalar(Wo[:], Wo[:], g.tg[:, 0, gate:gate + 1], None, ALU.mult
                                            ).then_inc(s.scaled, 1)
                    dve.wait_ge(s.scaled, 1)

                dve.sem_inc(s.x, 1)
                F = LN_STEPS + (1 + 3 + 3 if self_attn else 3)
                M = 3
                O = NT + {"self": 1 + 5 + RSQRT_STEPS, "causal": 0, "biased": 1}[kind]

                def norm(n, go):
                    wait(dve, s.xT, n)
                    if self_attn:
                        wait(dve, s.kept, n)
                    dve.sem_inc(s.passed, 1)
                    layernorm(nc, go, w, xn, batch(g.x, n)).then_inc(s.xn, 1)

                def keep_x(n):
                    if self_attn:
                        dve.wait_ge(s.xn, n + 1)
                        nc.vector.tensor_scalar(batch(g.x2, n), xn, 1.0, None, ALU.mult).then_inc(s.kept, 1)

                def split(part, rest, go, done):
                    go(nc.vector.tensor_copy(part[:, 0], rest[:]))
                    go(nc.vector.tensor_tensor(rest[:], rest[:], part[:, 0], ALU.subtract))
                    go(nc.vector.tensor_copy(part[:, 1], rest[:]))
                    nc.vector.tensor_tensor(part[:, 2], rest[:], part[:, 1], ALU.subtract).then_inc(done, 1)

                wide = [P, NC, S]

                def turned_by(f, name, table, ready, done, n):
                    dve.wait_ge(ready, n + 1)
                    nc.vector.tensor_tensor(f[:], half[name], table[:].unsqueeze(1).broadcast_to(wide), ALU.mult
                                            ).then_inc(done, 1)

                def front_q(n):
                    if self_attn:
                        wait(dve, s.kp, n)
                        turned_by(qf, "Q", cos, s.q, s.qm, n)

                def front_q_end(n, go):
                    if self_attn:
                        dve.wait_ge(s.kept, n + 1)
                        turned_by(rope, "Qs", sin, s.qsw, s.qr, n)
                        dve.wait_ge(s.qr, n + 1)
                        go(nc.vector.tensor_tensor(qf[:], qf[:], rope[:], ALU.add))
                    else:
                        dve.wait_ge(s.qf, n + 1)
                    wait(dve, s.kw if self_attn else s.qw, n * 48)
                    split(qp, qf, go, s.qp)

                def front_k(n, go):
                    if self_attn:
                        dve.wait_ge(s.qp, n + 1)
                        turned_by(kf, "K", cos, s.k, s.km, n)
                        turned_by(rope, "Ks", sin, s.ksw, s.kr, n)
                        dve.wait_ge(s.kr, n + 1)
                        nc.vector.tensor_tensor(kf[:], kf[:], rope[:], ALU.add).then_inc(s.kf, 1)
                        dve.wait_ge(s.kf, n + 1)
                        dve.wait_ge(s.qw, n * 48 + 48)
                        split(kp, kf, go, s.kp)

                def front_v(n, pn):
                    if biased:
                        dve.wait_ge(s.v, n + 1)
                        for t in range(NT):
                            last = nc.vector.tensor_tensor(V[:, pn, t, :, 0:DH],
                                                           pV[:, t].rearrange("p (h d) -> p h d", d=DH),
                                                           bv[:].rearrange("p (h d) -> p h d", d=DH), ALU.add)
                        last.then_inc(s.vc, 1)

                def maxima(units, a):
                    for n in units:
                        h, t = divmod(n, NT)
                        dve.wait_ge(s.S, a * NS + n + 1)
                        keys = (t + 1) * P if causal else S
                        nc.vector.tensor_reduce(nm[:, t, h:h + 1], pS[:, n % 2, 0:keys], AX.X, ALU.max,
                                                negate=True).then_inc(s.max, 1)

                def split_maxima(a, go):
                    dve.wait_ge(s.max, a * NS + NS)
                    go(nc.vector.tensor_copy(mm[:, :, 0], nm[:]))
                    go(nc.vector.tensor_tensor(nr[:], nm[:], mm[:, :, 0], ALU.subtract))
                    go(nc.vector.tensor_copy(mm[:, :, 1], nr[:]))
                    nc.vector.tensor_tensor(mm[:, :, 2], nr[:], mm[:, :, 1], ALU.subtract).then_inc(s.mm, 1)

                def group_out(b, h):
                    dve.wait_ge(s.pv, b * NW + (h + 1) * NT)
                    nc.vector.tensor_copy(Osb[:, h], pO[:]).then_inc(s.oev, 1)

                def normalise(b, t, go):
                    dve.wait_ge(s.ot, b * NT + t + 1)
                    o = (pM, pO)[t % 2][:].rearrange("p (h m) -> p h m", m=32)
                    go(nc.vector.reciprocal(rd[:, t, :], o[:, :, DH]))
                    nc.vector.tensor_tensor(On[:, t].rearrange("p (h d) -> p h d", d=DH), o[:, :, 0:DH],
                                            rd[:, t, :].unsqueeze(2).broadcast_to([P, NH, DH]), ALU.mult
                                            ).then_inc(s.nrm, 1)

                def add_output(b, go):
                    dve.wait_ge(s.y, b + 1)
                    if self_attn:
                        x2 = batch(g.x2, b)
                        go(nc.vector.tensor_tensor(On, pY, x2, ALU.add))
                        rms_rstd(nc, go, w, On)
                        for t in range(NT):
                            last = nc.vector.scalar_tensor_tensor(out=x2[:, t, :], in0=On[:, t, :],
                                                                  scalar=w.rstd[:, t:t + 1], in1=normw[:],
                                                                  op0=ALU.mult, op1=ALU.mult)
                        last.then_inc(s.x, 1)
                    else:
                        x = batch(g.x, b)
                        if biased:
                            go(nc.vector.tensor_tensor(x, pY, x, ALU.add))
                            nc.vector.tensor_tensor(x, x, bo[:].unsqueeze(1).broadcast_to([P, NT, D]), ALU.add
                                                    ).then_inc(s.x, 1)
                        else:
                            nc.vector.tensor_tensor(x, pY, x, ALU.add).then_inc(s.x, 1)
                    dve.wait_ge(s.x, b + 2)

                def front(n, pn):
                    go = Steps(dve, s.dve, 0)
                    norm(n, go)
                    keep_x(n)
                    front_q(n)
                    front_q_end(n, go)
                    front_k(n, go)
                    front_v(n, pn)
                    assert go.n == F, go.n

                def turn(k, pk, before, now, after):
                    if isinstance(k, int):
                        base = F * min(k + 1, B) + M * k + O * max(k - 1, 0)
                    else:
                        base = F * (k + 1) + M * k + O * (k - 1)
                    go = Steps(dve, s.dve, base)
                    units_now = max_units if now else (lambda slot: ())
                    for slot in range(MAIN):
                        units = list(units_now(slot))
                        if after and slot == NORM_SLOT:
                            units = [n for later in range(slot, slot + NT) for n in units_now(later)]
                            go.between = lambda: maxima([units.pop(0)] if units else [], k)
                            norm(k + 1, go)
                            go.between = None
                        elif after and NORM_SLOT < slot < NORM_SLOT + NT:
                            units = []
                        maxima(units, k)
                        if before and slot > 0 and slot % NT == 0:
                            group_out(k - 1, slot // NT - 1)
                    if now:
                        split_maxima(k, go)
                    if after:
                        keep_x(k + 1)
                    for t in range(NT):
                        if after and t == 2:
                            front_q(k + 1)
                        if before:
                            normalise(k - 1, t, go)
                    if after:
                        front_q_end(k + 1, go)
                        front_k(k + 1, go)
                        front_v(k + 1, 1 - pk)
                    if before:
                        add_output(k - 1, go)
                    assert go.n == F * after + M * now + O * before, go.n
                run(dve, front, turn)


def top_attention(nc, g, sem):
    TOP, ROUND, TAKEN = 32, 8, -3.0e38
    NR = TOP // ROUND
    SCALE = float(D) ** -0.5
    d = {k[9:]: v for k, v in g.dram.items() if k.startswith("L2_xattn_")}
    names = ("load", "bo", "dve", "xn", "kv", "xT", "xTc", "q", "k", "v", "qf", "kf", "vc", "sc", "top", "bias", "exp",
             "read", "p", "pT", "pTc", "o", "oc", "y", "x",
             "passed")
    Sems = namedtuple("Sems", names)
    s = Sems(*(sem("t2_" + n) for n in names))
    with ExitStack() as ctx:
        sb, ps = allocators(nc, ctx)
        WqT, WkT, WvT, WoT = load_transposed(nc, g, sb, ps, sem, "t2", [d["W" + n] for n in "qkvo"])
        bq, bk = sb("t2_bq", [P, NC]), sb("t2_bk", [P, NC])
        bv, bo = sb("t2_bv", [P, D]), sb("t2_bo", [P, D])
        w = norm_scratch(sb, "t2")
        xn, xnT, kvT = sb("t2_xn", [P, NT, D]), sb("t2_xnT", [P, NC, S]), sb("t2_kvT", [P, NC, S])
        qf, kf, V = sb("t2_qf", [P, NC, S]), sb("t2_kf", [P, NC, S]), sb("t2_V", [P, NT, D])
        best, work = sb("t2_best", [P, NR, ROUND]), sb("t2_work", [P, 2, S])
        nb = sb("t2_nb", [P, NT])
        E, Pm = sb("t2_E", [P, 2, S]), sb("t2_Pm", [P, 2, S])
        PT, oT = sb("t2_PT", [P, NT, S]), sb("t2_oT", [P, NC, S])
        rsum, rinv = sb("t2_rsum", [P, NT]), sb("t2_rinv", [P, NT])
        pA, pB = ps("t2_pA", [P, NC, S]), ps("t2_pB", [P, NC, S])
        pS, pT = ps("t2_pS", [P, 2, S]), ps("t2_pT", [P, 2, S])
        pV = pS[:].rearrange("p a n -> p (a n)").rearrange("p (t n) -> p t n", t=NT)
        pY = pA[:].rearrange("p a n -> p (a n)").rearrange("p (t n) -> p t n", t=NT)
        NLOAD = 4
        NDVE = LN_STEPS + 1 + NT * (2 * NR - 1) + 2
        with nc.Block() as block:
            @block.sync
            def _(sp):
                for t, n in ((bq, "bq"), (bk, "bk")):
                    sp.dma_start(t[:], d[n].rearrange("(c p) -> p c", p=P),
                                 allow_slow_non_contiguous=True).then_inc(s.load, 16)
                for t, n in ((bv, "bv"), (bo, "bo")):
                    sp.dma_start(t[:], row_of(d[n])).then_inc(s.load, 16)
                with sp.Fori(0, B) as i:
                    sp.wait_ge(s.xn, i + 1)
                    sp.sem_inc(s.passed, 1)
                    sp.dma_start(kvT[:], batch_of(g.d_ctxT, i)).then_inc(s.kv, 16)

            @block.tensor
            def _(pe):
                def project(out, W, src):
                    for m in range(NC):
                        for c in range(NC):
                            last = nc.tensor.matmul(out[:, m, :], W[:, c, m * P:(m + 1) * P], src[:, c, :],
                                                    start=c == 0, stop=c == NC - 1)
                    return last

                with pe.Fori(0, B) as i:
                    pe.wait_ge(s.xn, i + 1)
                    for c in range(NC):
                        for t in range(NT):
                            last = nc.tensor.transpose(pA[:, c, t * P:(t + 1) * P], xn[:, t, c * P:(c + 1) * P],
                                                       g.ident[:])
                    last.then_inc(s.xT, 1)
                    pe.wait_ge(s.kv, i * 16 + 16)
                    project(pB, WkT, kvT).then_inc(s.k, 1)
                    for t in range(NT):
                        for c in range(NC):
                            last = nc.tensor.matmul(pV[:, t, :], kvT[:, c, t * P:(t + 1) * P], WvT[:, c, :],
                                                    start=c == 0, stop=c == NC - 1)
                    last.then_inc(s.v, 1)
                    pe.wait_ge(s.xTc, i + 1)
                    project(pA, WqT, xnT).then_inc(s.q, 1)
                    pe.wait_ge(s.qf, i + 1)
                    pe.wait_ge(s.kf, i + 1)
                    pe.wait_ge(s.vc, i + 1)
                    for n in range(NT + 1):
                        if n < NT:
                            if n >= 2:
                                pe.wait_ge(s.exp, i * NT + n - 1)
                                pe.wait_ge(s.read, i * NT + n - 1)
                            for c in range(NC):
                                last = nc.tensor.matmul(pS[:, n % 2], qf[:, c, n * P:(n + 1) * P], kf[:, c, :],
                                                        start=c == 0, stop=c == NC - 1)
                            last.then_inc(s.sc, 1)
                        if n >= 1:
                            t = n - 1
                            pe.wait_ge(s.p, i * NT + t + 1)
                            if t >= 2:
                                pe.wait_ge(s.pTc, i * NT + t - 1)
                            for k in range(NT):
                                last = nc.tensor.transpose(pT[:, t % 2, k * P:(k + 1) * P],
                                                           Pm[:, t % 2, k * P:(k + 1) * P], g.ident[:])
                            last.then_inc(s.pT, 1)
                    pe.wait_ge(s.pTc, i * NT + NT)
                    for m in range(NC):
                        for k in range(NT):
                            last = nc.tensor.matmul(pB[:, m, :], V[:, k, m * P:(m + 1) * P], PT[:, k, :],
                                                    start=k == 0, stop=k == NT - 1)
                    last.then_inc(s.o, 1)
                    pe.wait_ge(s.oc, i + 1)
                    for t in range(NT):
                        for c in range(NC):
                            last = nc.tensor.matmul(pY[:, t, :], oT[:, c, t * P:(t + 1) * P], WoT[:, c, :],
                                                    start=c == 0, stop=c == NC - 1)
                    last.then_inc(s.y, 1)

            @block.scalar
            def _(act):
                act.wait_ge(s.load, 16 * NLOAD)
                with act.Fori(0, B) as i:
                    act.wait_ge(s.xT, i + 1)
                    nc.scalar.copy(xnT[:], pA[:]).then_inc(s.xTc, 1)
                    for src, dst, bias, ready, done in ((pB, kf, bk, s.k, s.kf), (pA, qf, bq, s.q, s.qf)):
                        act.wait_ge(ready, i + 1)
                        for c in range(NC):
                            last = nc.scalar.activation(dst[:, c], src[:, c], ACT.Identity, bias=bias[:, c:c + 1])
                        last.then_inc(done, 1)
                    for t in range(NT + 1):
                        if t < NT:
                            act.wait_ge(s.bias, i * NT + t + 1)
                            act.wait_ge(s.read, i * NT + t + 1)
                            if t >= 2:
                                act.wait_ge(s.p, i * NT + t - 1)
                            nc.scalar.activation(E[:, t % 2], pS[:, t % 2], ACT.Exp, bias=nb[:, t:t + 1], scale=SCALE
                                                 ).then_inc(s.exp, 1)
                        if t >= 1:
                            act.wait_ge(s.pT, i * NT + t)
                            nc.scalar.copy(PT[:, :, (t - 1) * P:t * P],
                                           pT[:, (t - 1) % 2].rearrange("p (k n) -> p k n", k=NT)).then_inc(s.pTc, 1)
                    act.wait_ge(s.o, i + 1)
                    nc.scalar.copy(oT[:], pB[:]).then_inc(s.oc, 1)

            @block.vector
            def _(dve):
                dve.wait_ge(s.load, 16 * NLOAD)
                nc.vector.tensor_scalar(bo[:], bo[:], g.tg[:, 0, 2:3], None, ALU.mult).then_inc(s.bo, 1)
                dve.wait_ge(s.bo, 1)

                def pass_wait():
                    dve.sem_inc(s.passed, 1)
                with dve.Fori(0, B) as i:
                    step = Steps(dve, s.dve, i * NDVE)
                    x = batch(g.x, i)
                    layernorm(nc, step, w, xn, x).then_inc(s.xn, 1)
                    dve.wait_ge(s.xn, i + 1)
                    step(nc.vector.tensor_tensor(x, x, bo[:].unsqueeze(1).broadcast_to([P, NT, D]), ALU.add))
                    dve.wait_ge(s.v, i + 1)
                    nc.vector.tensor_tensor(V[:], pV, bv[:].unsqueeze(1).broadcast_to([P, NT, D]), ALU.add
                                            ).then_inc(s.vc, 1)
                    for t in range(NT):
                        dve.wait_ge(s.sc, i * NT + t + 1)
                        if t >= 2:
                            dve.wait_ge(s.pT, i * NT + t - 1)
                        pass_wait()
                        src = pS[:, t % 2]
                        for k in range(NR):
                            step(nc.vector.max(best[:, k], src))
                            if k == 0:
                                nc.vector.tensor_scalar(nb[:, t:t + 1], best[:, 0, 0:1], -SCALE, None, ALU.mult
                                                        ).then_inc(s.bias, 1)
                            else:
                                pass_wait()
                            ins = nc.vector.match_replace(work[:, k % 2], best[:, k], src, TAKEN)
                            if k == 0:
                                ins.then_inc(s.read, 1)
                                dve.wait_ge(s.read, i * NT + t + 1)
                            else:
                                step(ins)
                            if k < NR - 1:
                                pass_wait()
                            src = work[:, k % 2]
                        dve.wait_ge(s.exp, i * NT + t + 1)
                        nc.vector.scalar_tensor_tensor(out=Pm[:, t % 2], in0=src, scalar=TAKEN, in1=E[:, t % 2],
                                                       op0=ALU.is_equal, op1=ALU.mult, accum_out=rsum[:, t:t + 1]
                                                       ).then_inc(s.p, 1)
                    dve.wait_ge(s.p, i * NT + NT)
                    step(nc.vector.reciprocal(rinv[:], rsum[:]))
                    step(nc.vector.tensor_scalar(rinv[:], rinv[:], g.tg[:, 0, 2:3], None, ALU.mult))
                    dve.wait_ge(s.y, i + 1)
                    for t in range(NT):
                        last = nc.vector.scalar_tensor_tensor(out=x[:, t, :], in0=pY[:, t, :], scalar=rinv[:, t:t + 1],
                                                              in1=x[:, t, :], op0=ALU.mult, op1=ALU.add)
                    last.then_inc(s.x, 1)
                    dve.wait_ge(s.x, i + 1)
                    assert step.n == NDVE, (step.n, NDVE)


def top_k(nc, step, k, prob, gt, eq, rank, tri, out):
    _, tiles, E = prob.shape
    four = [P, tiles, E, E]
    other, own = prob.unsqueeze(2).broadcast_to(four), prob.unsqueeze(3).broadcast_to(four)
    nc.vector.tensor_tensor(gt, other, own, ALU.is_gt)
    step(nc.vector.tensor_tensor(eq, other, own, ALU.is_equal))
    step(nc.vector.tensor_tensor(eq, eq, tri.unsqueeze(1).broadcast_to(four), ALU.mult))
    step(nc.vector.tensor_tensor(gt, gt, eq, ALU.add))
    step(nc.vector.tensor_reduce(rank, gt, AX.X, ALU.add))
    step(nc.vector.scalar_tensor_tensor(out=out, in0=rank, scalar=float(k), in1=prob, op0=ALU.is_lt, op1=ALU.mult))


def routing(nc, g, sem, r):
    tag, E, EL = r.tag, r.E, r.EL
    names = ("load", "const", "dve", "stats", "xn", "xT", "xTc", "logit", "ein", "exp", "w", "tp", "tpc", "tb", "sel",
             "mask", "pos", "slot")
    Sems = namedtuple("Sems", names)
    s = Sems(*(sem(f"{tag}r_{n}") for n in names))
    TT = B * NT
    by_choice = r.kind == "expert_choice"
    copies = 1 if by_choice else 2
    with ExitStack() as ctx:
        sb, ps = allocators(nc, ctx)
        w = r.norm if by_choice else norm_scratch(sb, tag + "r", TT)
        xn, xnT = sb(tag + "r_xn", [P, 2, NT, D]), sb(tag + "r_xnT", [P, NC, S])
        Wr = sb(tag + "r_Wr", [P, NC, EL])
        L = sb(tag + "r_L", [P, TT, EL])
        pr = sb(tag + "r_pr", [P, TT, E])
        a, b, c2 = (sb(f"{tag}r_{n}", [P, TT, 4]) for n in "abc")
        tri, bias = sb(tag + "r_tri", [P, E, E]), sb(tag + "r_bias", [P, EL])
        if by_choice:
            R = B * E
            pt, work, best = sb(tag + "r_pt", [R, S]), sb(tag + "r_work", [R, S]), sb(tag + "r_best", [R, 8])
            chosen = sb(tag + "r_chosen", [R, S])
            mask, upto = sb(tag + "r_mask", [P, NT, R]), sb(tag + "r_upto", [P, P])
        else:
            gt, eq = sb(tag + "r_gt", [P, TT, E, E]), sb(tag + "r_eq", [P, TT, E, E])
            rank = sb(tag + "r_rank", [P, TT, E])
        pT, pL, pX = ps(tag + "r_pT", [P, 2, NC, S]), ps(tag + "r_pL", [P, TT, EL]), ps(tag + "r_pX", [P, S])
        NLOAD = len(r.router) + (2 if r.kind == "grouped" else 0)
        tgate = g.tg[:, 1, r.gate:r.gate + 1]
        with nc.Block() as block:
            @block.sync
            def _(sp):
                for dst, src in r.router:
                    sp.dma_start(Wr[:, :, dst], src, allow_slow_non_contiguous=True).then_inc(s.load, 16)
                if r.kind == "grouped":
                    sp.dma_start(bias[:, 0:2], r.biases[0].rearrange("(o n) -> o n", o=1).broadcast_to([P, 2])
                                 ).then_inc(s.load, 16)
                    sp.dma_start(bias[:, 2:10], r.biases[1].rearrange("(o n) -> o n", o=1).broadcast_to([P, 8])
                                 ).then_inc(s.load, 16)
                for dst, src in r.loads:
                    sp.dma_start(dst, src).then_inc(r.s_weights, 16)

            @block.gpsimd
            def _(pool):
                nc.gpsimd.memset(tri[:], 0.0).then_inc(s.const, 1)
                pool.wait_ge(s.const, 1)
                nc.gpsimd.affine_select(out=tri[:], in_=tri[:], compare_op=ALU.is_ge, fill=1.0, base=0,
                                        pattern=[[-1, E], [1, E]], channel_multiplier=0).then_inc(s.const, 1)
                if by_choice:
                    pool.wait_ge(s.const, 2)
                    nc.gpsimd.memset(upto[:], 0.0).then_inc(s.const, 1)
                    pool.wait_ge(s.const, 3)
                    nc.gpsimd.affine_select(out=upto[:], in_=upto[:], compare_op=ALU.is_gt, fill=1.0, base=0,
                                            pattern=[[-1, P]], channel_multiplier=1).then_inc(s.const, 1)

            @block.tensor
            def _(pe):
                pe.wait_ge(s.load, 16 * NLOAD)
                pe.sem_inc(s.xT, 2)
                with pe.Fori(0, B - 1, 2) as i:
                    for u in range(2):
                        j = i + u
                        pe.wait_ge(s.xn, j + 1)
                        pe.wait_ge(s.xTc, copies * (j + 1))
                        for c in range(NC):
                            for t in range(NT):
                                last = nc.tensor.transpose(pT[:, u, c, t * P:(t + 1) * P],
                                                           xn[:, u, t, c * P:(c + 1) * P], g.ident[:])
                        last.then_inc(s.xT, 1)
                        pe.wait_ge(s.xTc, copies * (j + 2) + 1)
                        for t in range(NT):
                            for c in range(NC):
                                last = nc.tensor.matmul(pL[:, bass.ds(j * NT + t, 1), :].rearrange("p o e -> p (o e)"),
                                                        xnT[:, c, t * P:(t + 1) * P], Wr[:, c, :],
                                                        start=c == 0, stop=c == NC - 1)
                        last.then_inc(s.logit, 1)
                if r.kind == "expert_choice":
                    pe.wait_ge(s.w, 1)
                    for t in range(NT):
                        last = nc.tensor.transpose(pX[0:R, t * P:(t + 1) * P], r.weights[:, t, :], g.ident[:])
                    last.then_inc(s.tp, 1)
                    pe.wait_ge(s.sel, 1)
                    for t in range(NT):
                        last = nc.tensor.transpose(pX[:, t * R:(t + 1) * R], chosen[:, t * P:(t + 1) * P],
                                                   g.ident[0:R, 0:R])
                    last.then_inc(s.tb, 1)
                    pe.wait_ge(s.mask, 1)
                    pe.wait_ge(s.const, 4)
                    for t in range(NT):
                        for q in range(t + 1):
                            last = nc.tensor.matmul(pX[:, t * R:(t + 1) * R], (upto if q == t else g.ones)[:],
                                                    mask[:, q, :], start=q == 0, stop=q == t)
                    last.then_inc(s.pos, 1)
                    pe.wait_ge(s.slot, 1)
                    nc.tensor.matmul(pX[:, 0:P], g.ones[:], upto[:], start=True, stop=True).then_inc(s.pos, 1)

            @block.scalar
            def _(act):
                act.sem_inc(s.xTc, 2 * copies)
                act.sem_inc(s.logit, 1)
                with act.Fori(0, B - 1, 2) as i:
                    for u in range(2):
                        j = i + u
                        act.wait_ge(s.xT, j + 3)
                        act.wait_ge(s.logit, j + 1)
                        nc.scalar.copy(xnT[:], pT[:, u]).then_inc(s.xTc, 1)
                        if copies > 1:
                            nc.scalar.copy(g.xT[:, :, bass.ds(j * S, S)], pT[:, u]).then_inc(s.xTc, 1)
                act.wait_ge(s.ein, 1)
                nc.scalar.activation(L[:], L[:], ACT.Exp).then_inc(s.exp, 1)

            @block.vector
            def _(dve):
                dve.wait_ge(s.load, 16 * NLOAD)
                dve.wait_ge(s.const, 2)
                step = Steps(dve, s.dve)

                def wide(x, n=E):
                    return x.unsqueeze(2).broadcast_to([P, TT, n])
                if r.kind != "grouped":
                    with dve.Fori(0, B) as i:
                        for t in range(NT):
                            last = nc.vector.bn_stats(batch(w.stats, i)[:, t, :], batch(g.x, i)[:, t, :])
                        last.then_inc(s.stats, 1)
                    dve.wait_ge(s.stats, B)
                    mean_rstd(nc, step, w)
                with dve.Fori(0, B - 1, 2) as i:
                    for u in range(2):
                        j = i + u
                        dve.wait_ge(s.xT, j + 1)
                        if r.kind == "grouped":
                            nc.vector.tensor_scalar(xn[:, u], batch(g.x2, j), 1.0, None, ALU.mult).then_inc(s.xn, 1)
                            continue
                        for t in range(NT):
                            row = bass.ds(j * NT + t, 1)
                            last = nc.vector.tensor_scalar(xn[:, u, t, :], g.x[:, row, :].rearrange("p o d -> p (o d)"),
                                                           w.mean[:, row], w.rstd[:, row], ALU.subtract, ALU.mult)
                        last.then_inc(s.xn, 1)
                dve.wait_ge(s.logit, B + 1)
                if r.kind == "grouped":
                    eight = [P, TT, 2, 4]
                    Lg, Le = L[:, :, 0:2], L[:, :, 2:10].rearrange("p t (g e) -> p t g e", g=2)
                    step(nc.vector.tensor_tensor(L[:], pL[:], bias[:].unsqueeze(1).broadcast_to([P, TT, EL]), ALU.add))
                    nc.vector.tensor_reduce(a[:, :, 0:1], Lg, AX.X, ALU.max)
                    step(nc.vector.tensor_reduce(b[:, :, 0:2], Le, AX.X, ALU.max))
                    nc.vector.tensor_tensor(Lg, Lg, a[:, :, 0:1].broadcast_to([P, TT, 2]), ALU.subtract)
                    nc.vector.tensor_tensor(Le, Le, b[:, :, 0:2].unsqueeze(3).broadcast_to(eight), ALU.subtract
                                            ).then_inc(s.ein, 1)
                    dve.wait_ge(s.exp, 1)
                    nc.vector.tensor_reduce(a[:, :, 0:1], Lg, AX.X, ALU.add)
                    step(nc.vector.tensor_reduce(a[:, :, 1:3], Le, AX.X, ALU.add))
                    step(nc.vector.reciprocal(b[:, :, 0:3], a[:, :, 0:3]))
                    step(nc.vector.tensor_tensor(Lg, Lg, b[:, :, 0:1].broadcast_to([P, TT, 2]), ALU.mult))
                    nc.vector.tensor_tensor(c2[:, :, 0:1], Lg[:, :, 0:1], Lg[:, :, 1:2], ALU.is_ge)
                    step(nc.vector.tensor_tensor(c2[:, :, 1:2], Lg[:, :, 0:1], Lg[:, :, 1:2], ALU.is_lt))
                    step(nc.vector.tensor_tensor(c2[:, :, 0:2], c2[:, :, 0:2], Lg, ALU.mult))
                    step(nc.vector.tensor_tensor(c2[:, :, 0:2], c2[:, :, 0:2], b[:, :, 1:3], ALU.mult))
                    step(nc.vector.tensor_tensor(pr[:].rearrange("p t (g e) -> p t g e", g=2), Le,
                                                 c2[:, :, 0:2].unsqueeze(3).broadcast_to(eight), ALU.mult))
                else:
                    step(nc.vector.tensor_reduce(a[:, :, 0:1], pL[:, :, 0:E], AX.X, ALU.max))
                    if r.shared_gate:
                        nc.vector.tensor_scalar(L[:, :, E:E + 1], pL[:, :, E:E + 1], -1.0, None, ALU.mult)
                    nc.vector.tensor_tensor(L[:, :, 0:E], pL[:, :, 0:E], wide(a[:, :, 0]), ALU.subtract
                                            ).then_inc(s.ein, 1)
                    dve.wait_ge(s.exp, 1)
                    step(nc.vector.tensor_reduce(a[:, :, 0:1], L[:, :, 0:E], AX.X, ALU.add))
                    step(nc.vector.reciprocal(b[:, :, 0:1], a[:, :, 0:1]))
                    step(nc.vector.tensor_tensor(pr[:], L[:, :, 0:E], wide(b[:, :, 0]), ALU.mult))
                weights = r.weights[:].rearrange("p t (b w) -> p b t w", b=B)

                def by_batch(x):
                    return x.rearrange("p (b t) e -> p b t e", b=B)
                if r.kind == "expert_choice":
                    nc.vector.tensor_scalar(weights, by_batch(pr[:]), 1.0, None, ALU.mult).then_inc(s.w, 1)
                else:
                    top_k(nc, step, r.k, pr[:], gt[:], eq[:], rank[:], tri[:], pr[:])
                    if r.renorm:
                        step(nc.vector.tensor_reduce(a[:, :, 0:1], pr[:], AX.X, ALU.add))
                        step(nc.vector.reciprocal(b[:, :, 0:1], a[:, :, 0:1]))
                        step(nc.vector.tensor_tensor(pr[:], pr[:], wide(b[:, :, 0]), ALU.mult))
                    if r.shared_gate:
                        step(nc.vector.tensor_scalar(a[:, :, 0:1], L[:, :, E:E + 1], 1.0, None, ALU.add))
                        step(nc.vector.reciprocal(b[:, :, 0:1], a[:, :, 0:1]))
                        nc.vector.tensor_scalar(weights[:, :, :, E:E + 1], by_batch(b[:, :, 0:1]), tgate, None, ALU.mult)
                    nc.vector.tensor_scalar(weights[:, :, :, 0:E], by_batch(pr[:]),
                                            1.0 if r.kind == "grouped" else tgate, None, ALU.mult).then_inc(s.w, 1)
                dve.wait_ge(s.w, 1)
                if r.kind == "expert_choice":
                    dve.wait_ge(s.tp, 1)
                    nc.vector.tensor_copy(work[:], pX[0:R, :]).then_inc(s.tpc, 1)
                    nc.vector.tensor_copy(pt[:], pX[0:R, :]).then_inc(s.tpc, 1)
                    dve.wait_ge(s.tpc, 2)
                    for n in range(r.capacity // 8):
                        nc.vector.max(best[:], work[:]).then_inc(s.tpc, 1)
                        dve.wait_ge(s.tpc, 2 * n + 3)
                        nc.vector.match_replace(work[:], best[:], work[:], -1.0).then_inc(s.tpc, 1)
                        dve.wait_ge(s.tpc, 2 * n + 4)
                    nc.vector.scalar_tensor_tensor(out=chosen[:], in0=work[:], scalar=0.0, in1=pt[:],
                                                   op0=ALU.is_lt, op1=ALU.mult).then_inc(s.sel, 1)
                    dve.wait_ge(s.tb, 1)
                    by_tile = pX[:, 0:NT * R].rearrange("p (t r) -> p t r", t=NT)
                    nc.vector.tensor_scalar(r.weights[:], by_tile, tgate, None, ALU.mult)
                    nc.vector.tensor_scalar(mask[:], by_tile, 0.0, None, ALU.is_gt).then_inc(s.mask, 1)
                    dve.wait_ge(s.mask, 1)
                    dve.wait_ge(s.pos, 1)
                    nc.vector.tensor_tensor(r.slot[:], by_tile, mask[:], ALU.mult).then_inc(s.slot, 1)
                    dve.wait_ge(s.pos, 2)
                    nc.vector.tensor_copy(r.iota[:], pX[:, 0:P]).then_inc(s.slot, 1)
                    dve.wait_ge(s.slot, 2)


def experts(nc, g, sem, r):
    tag = r.tag
    names = ("H", "sg", "ha", "hm", "Y", "acc", "fin", "dve", "x")
    Sems = namedtuple("Sems", names)
    s = Sems(*(sem(f"{tag}e_{n}") for n in names))
    units, outs = [], []
    for j, job in enumerate(r.jobs):
        for q in range(job.nf if job.glu else job.nf // 2):
            units.append((j, q))
        outs += [(j, n) for n in range(len(job.outs))]
    NU, NY = len(units), len(outs)
    glu = [r.jobs[j].glu for j, _ in units]
    NG, NA = sum(glu), NU - sum(glu)
    assert NU % 2 == 0
    FMAX = max(job.nf for job in r.jobs)
    with ExitStack() as ctx:
        sb, ps = allocators(nc, ctx)
        hT = sb(tag + "e_hT", [P, 2, FMAX, S])
        sg = sb(tag + "e_sg", [P, 2, S])
        acc = sb(tag + "e_acc", [P, NT, D])
        wf = sb(tag + "e_wf", [P, NT, r.EW])
        if r.final_norm is not None:
            nw, w = sb(tag + "e_nw", [P, D]), norm_scratch(sb, tag + "e")
        pH, pY = ps(tag + "e_pH", [P, 2, 2, S]), ps(tag + "e_pY", [P, 2, NT, D])

        def consumed(eng, u, i):
            ahead = 1 if u >= 0 else 0
            u %= NU
            if glu[u]:
                eng.wait_ge(s.hm, (i + ahead) * NG + sum(glu[:u + 1]))
            else:
                eng.wait_ge(s.ha, (i + ahead) * NA + u + 1 - sum(glu[:u + 1]))

        def hidden_free(eng, j, i):
            ahead = 1 if j >= 2 else 0
            before = j - 2 if j >= 2 else max(k for k in range(len(r.jobs)) if k % 2 == j % 2)
            eng.wait_ge(s.Y, (i + ahead) * NY + r.jobs[before].out0 + len(r.jobs[before].outs))

        def out_free(eng, y, i):
            ahead = 1 if y >= 2 else 0
            before = y - 2 if y >= 2 else max(k for k in range(NY) if k % 2 == y % 2)
            eng.wait_ge(s.acc, (i + ahead) * NY + before + 1)

        with nc.Block() as block:
            if r.final_norm is not None:
                @block.sync
                def _(sp):
                    sp.dma_start(nw[:], r.final_norm.rearrange("(o n) -> o n", o=1).broadcast_to([P, D])
                                 ).then_inc(s.fin, 16)

            @block.tensor
            def _(pe):
                pe.wait_ge(r.s_weights, 16 * len(r.loads))
                pe.sem_inc(s.Y, NY)
                with pe.Fori(0, B) as i:
                    def rhs(c):
                        return g.xT[:, c, bass.ds(i * S, S)]

                    def outputs(j):
                        job = r.jobs[j]
                        consumed(pe, job.last, i)
                        for n, (w2, _) in enumerate(job.outs):
                            y = job.out0 + n
                            out_free(pe, y, i)
                            for t in range(NT):
                                for f in range(job.nf):
                                    last = nc.tensor.matmul(pY[:, y % 2, t, :], hT[:, j % 2, f, t * P:(t + 1) * P],
                                                            w2(f), start=f == 0, stop=f == job.nf - 1)
                            last.then_inc(s.Y, 1)
                    for j, job in enumerate(r.jobs):
                        for u in range(job.first, job.last + 1):
                            q = u - job.first
                            consumed(pe, u - 2, i)
                            for k in range(2):
                                for c in range(NC):
                                    w1 = job.win(k, q, c) if job.glu else job.win(0, 2 * q + k, c)
                                    last = nc.tensor.matmul(pH[:, u % 2, k], w1, rhs(c),
                                                            start=c == 0, stop=c == NC - 1)
                            last.then_inc(s.H, 1)
                        if j >= 1:
                            outputs(j - 1)
                    outputs(len(r.jobs) - 1)

            @block.scalar
            def _(act):
                if NA:
                    act.sem_inc(s.ha, NA)
                with act.Fori(0, B) as i:
                    for u, (j, q) in enumerate(units):
                        if not glu[u] and q == 0:
                            hidden_free(act, j, i)
                        act.wait_ge(s.H, i * NU + u + 1)
                        if glu[u]:
                            nc.scalar.activation(sg[:, u % 2], pH[:, u % 2, 0], ACT.Silu).then_inc(s.sg, 1)
                        else:
                            nc.scalar.activation(hT[:, j % 2, 2 * q:2 * q + 2], pH[:, u % 2], ACT.Silu
                                                 ).then_inc(s.ha, 1)

            @block.vector
            def _(dve):
                if NG:
                    dve.sem_inc(s.hm, NG)
                dve.sem_inc(s.acc, NY)
                if r.final_norm is not None:
                    dve.wait_ge(s.fin, 16)
                with dve.Fori(0, B) as i:
                    x = batch(g.x, i)
                    nc.vector.tensor_scalar(acc[:], batch(g.x2, i) if r.final_norm is not None else x, 1.0, None,
                                            ALU.mult).then_inc(s.x, 1)
                    nc.vector.tensor_scalar(wf[:], r.weights[:, :, bass.ds(i * r.EW, r.EW)], 1.0, None, ALU.mult).then_inc(s.x, 1)
                    NX = 3
                    dve.wait_ge(s.x, i * NX + 2)

                    def add(j):
                        job = r.jobs[j]
                        for n, (_, col) in enumerate(job.outs):
                            y = job.out0 + n
                            dve.wait_ge(s.Y, (i + 1) * NY + y + 1)
                            if y >= 1:
                                dve.wait_ge(s.acc, (i + 1) * NY + y)
                            for t in range(NT):
                                scale = 1.0 if col is None else wf[:, t, col:col + 1]
                                last = nc.vector.scalar_tensor_tensor(out=acc[:, t, :], in0=pY[:, y % 2, t, :],
                                                                      scalar=scale, in1=acc[:, t, :],
                                                                      op0=ALU.mult, op1=ALU.add)
                            last.then_inc(s.acc, 1)
                    for j, job in enumerate(r.jobs):
                        for u in range(job.first, job.last + 1):
                            if glu[u]:
                                if u == job.first:
                                    hidden_free(dve, j, i)
                                dve.wait_ge(s.sg, i * NG + sum(glu[:u + 1]))
                                nc.vector.tensor_tensor(hT[:, j % 2, u - job.first], pH[:, u % 2, 1], sg[:, u % 2],
                                                        ALU.mult).then_inc(s.hm, 1)
                        if j >= 1:
                            add(j - 1)
                    add(len(r.jobs) - 1)
                    dve.wait_ge(s.acc, (i + 2) * NY)
                    if r.final_norm is not None:
                        step = Steps(dve, s.dve, i * (5 + RSQRT_STEPS + 1))
                        rms_rstd(nc, step, w, acc)
                        for t in range(NT):
                            last = nc.vector.scalar_tensor_tensor(out=acc[:, t, :], in0=acc[:, t, :],
                                                                  scalar=w.rstd[:, t:t + 1], in1=nw[:],
                                                                  op0=ALU.mult, op1=ALU.mult)
                        step(last)
                        nc.vector.scalar_tensor_tensor(out=x, in0=acc[:], scalar=g.tg[:, 1, r.gate:r.gate + 1],
                                                       in1=x, op0=ALU.mult, op1=ALU.add).then_inc(s.x, 1)
                        assert step.n == 5 + RSQRT_STEPS + 1, step.n
                    else:
                        nc.vector.tensor_scalar(x, acc[:], 1.0, None, ALU.mult).then_inc(s.x, 1)
                    dve.wait_ge(s.x, i * NX + 3)


def choosing_experts(nc, g, sem, r):
    tag, E, F = r.tag, r.E, r.W2.shape[2]
    GB = 4
    assert r.capacity == P and GB * P == S
    names = ("xn", "wf", "sel", "G", "xg", "H", "h", "T", "selT", "Y", "y", "O", "x")
    Sems = namedtuple("Sems", names)
    s = Sems(*(sem(f"{tag}e_{n}") for n in names))
    NO, NH2 = E * GB, E * (F // 2)
    with ExitStack() as ctx:
        sb, ps = allocators(nc, ctx)
        xn = sb(tag + "e_xn", [P, GB, NT, D])
        wf, slot = sb(tag + "e_wf", [P, NT, GB, E]), sb(tag + "e_slot", [P, NT, GB, E])
        sel = sb(tag + "e_sel", [P, 2, GB, NT, P])
        xg, hT = sb(tag + "e_xg", [P, NC, S]), sb(tag + "e_hT", [P, F, S])
        selT, Ysb = sb(tag + "e_selT", [P, 2, S]), sb(tag + "e_Y", [P, 2, D])
        pG, pH = ps(tag + "e_pG", [P, NC, S]), ps(tag + "e_pH", [P, 2, S])
        pY, pT, pO = ps(tag + "e_pY", [P, 512]), ps(tag + "e_pT", [P, S]), ps(tag + "e_pO", [P, NT, D])
        with nc.Block() as block:
            @block.tensor
            def _(pe):
                pe.wait_ge(r.s_weights, 16 * len(r.loads))
                with pe.Fori(0, B // GB) as i:
                    def gather(e, batches):
                        for b in batches:
                            for c in range(NC):
                                for t in range(NT):
                                    last = nc.tensor.matmul(pG[:, c, b * P:(b + 1) * P],
                                                            xn[:, b, t, c * P:(c + 1) * P], sel[:, e % 2, b, t, :],
                                                            start=t == 0, stop=t == NT - 1)
                        return last

                    def hidden(e, k):
                        for f in range(2):
                            for c in range(NC):
                                q = 2 * k + f
                                last = nc.tensor.matmul(pH[:, f], r.W1[:, e, c, q * P:(q + 1) * P], xg[:, c],
                                                        start=c == 0, stop=c == NC - 1)
                        last.then_inc(s.H, 1)

                    def turn_sel(e, b):
                        pe.wait_ge(s.selT, i * NO + e * GB + b + 1)
                        for t in range(NT):
                            last = nc.tensor.transpose(pT[:, t * P:(t + 1) * P], sel[:, e % 2, b, t, :], g.ident[:])
                        last.then_inc(s.T, 1)

                    def outputs(e, b):
                        pe.wait_ge(s.y, i * NO + e * GB + b + 1)
                        for f in range(F):
                            last = nc.tensor.matmul(pY[:, 0:D], hT[:, f, b * P:(b + 1) * P], r.W2[:, e, f],
                                                    start=f == 0, stop=f == F - 1)
                        last.then_inc(s.Y, 1)

                    def put_back(e, b):
                        n = e * GB + b
                        pe.wait_ge(s.selT, i * NO + n + 2)
                        pe.wait_ge(s.y, i * NO + n + 2)
                        pe.wait_ge(s.x, i * NO + n + 1)
                        for t in range(NT):
                            last = nc.tensor.matmul(pO[:, t], selT[:, n % 2, t * P:(t + 1) * P], Ysb[:, n % 2],
                                                    start=True, stop=True)
                        last.then_inc(s.O, 1)

                    pe.wait_ge(s.xn, i + 1)
                    pe.wait_ge(s.sel, i * E + 1)
                    gather(0, range(GB)).then_inc(s.G, 1)
                    for e in range(E):
                        pe.wait_ge(s.xg, i * E + e + 1)
                        pe.wait_ge(s.h, i * NH2 + (F // 2) * e + 1)
                        hidden(e, 0)
                        turn_sel(e, 0)
                        for k in range(1, F // 2):
                            if e + 1 < E:
                                pe.wait_ge(s.sel, i * E + e + 2)
                                gather(e + 1, range(GB // 2))
                            pe.wait_ge(s.h, i * NH2 + (F // 2) * e + k + 1)
                            hidden(e, k)
                            if e + 1 < E:
                                gather(e + 1, range(GB // 2, GB)).then_inc(s.G, 1)
                        pe.wait_ge(s.h, i * NH2 + (F // 2) * (e + 1) + 1)
                        for b in range(GB):
                            outputs(e, b)
                            if b + 1 < GB:
                                turn_sel(e, b + 1)
                            put_back(e, b)

            @block.scalar
            def _(act):
                act.sem_inc(s.h, 1)
                act.sem_inc(s.selT, 1)
                act.sem_inc(s.y, 1)
                with act.Fori(0, B // GB) as i:
                    def gathered(e):
                        act.wait_ge(s.G, i * E + e + 1)
                        nc.scalar.copy(xg[:], pG[:]).then_inc(s.xg, 1)

                    def turned(e, b):
                        n = e * GB + b
                        act.wait_ge(s.T, i * NO + n + 1)
                        nc.scalar.copy(selT[:, n % 2], pT[:]).then_inc(s.selT, 1)

                    gathered(0)
                    for e in range(E):
                        for k in range(F // 2):
                            act.wait_ge(s.H, i * NH2 + e * (F // 2) + k + 1)
                            nc.scalar.activation(hT[:, 2 * k:2 * k + 2], pH[:], ACT.Silu).then_inc(s.h, 1)
                            if k == 0:
                                turned(e, 0)
                        if e + 1 < E:
                            gathered(e + 1)
                        for b in range(GB):
                            n = e * GB + b
                            act.wait_ge(s.Y, i * NO + n + 1)
                            nc.scalar.copy(Ysb[:, n % 2], pY[:, 0:D]).then_inc(s.y, 1)
                            if b + 1 < GB:
                                turned(e, b + 1)

            @block.vector
            def _(dve):
                dve.sem_inc(s.x, 1)
                with dve.Fori(0, B // GB) as i:
                    def select(e):
                        for b in range(GB):
                            for t in range(NT):
                                last = nc.vector.tensor_scalar(sel[:, e % 2, b, t, :], r.iota[:],
                                                               slot[:, t, b, e:e + 1], None, ALU.is_equal)
                        last.then_inc(s.sel, 1)

                    dve.wait_ge(s.x, i * NO + 1)
                    for b in range(GB):
                        for t in range(NT):
                            row = bass.ds(i * (GB * NT) + b * NT + t, 1)
                            last = nc.vector.tensor_scalar(xn[:, b, t, :], g.x[:, row, :].rearrange("p o d -> p (o d)"),
                                                           r.norm.mean[:, row], r.norm.rstd[:, row],
                                                           ALU.subtract, ALU.mult)
                    last.then_inc(s.xn, 1)
                    own = bass.ds(i * (GB * E), GB * E)
                    for dst, src in ((wf, r.weights), (slot, r.slot)):
                        nc.vector.tensor_scalar(dst[:].rearrange("p t b e -> p t (b e)"), src[:, :, own], 1.0, None,
                                                ALU.mult).then_inc(s.wf, 1)
                    dve.wait_ge(s.wf, 2 * i + 2)
                    select(0)
                    select(1)
                    for e in range(E):
                        for b in range(GB):
                            n = e * GB + b
                            if b == GB - 1 and e + 2 < E:
                                dve.wait_ge(s.T, i * NO + (e + 1) * GB)
                                select(e + 2)
                            dve.wait_ge(s.O, i * NO + n + 1)
                            if e >= 1:
                                dve.wait_ge(s.x, i * NO + n + 2 - GB)
                            x = batch(g.x, i * GB + b)
                            for t in range(NT):
                                last = nc.vector.scalar_tensor_tensor(out=x[:, t, :], in0=pO[:, t, :],
                                                                      scalar=wf[:, t, b, e:e + 1], in1=x[:, t, :],
                                                                      op0=ALU.mult, op1=ALU.add)
                            last.then_inc(s.x, 1)
                dve.wait_ge(s.x, 1 + NO * (B // GB))


def moe_layer(nc, g, sem, layer):
    with ExitStack() as ctx:
        sb, _ = allocators(nc, ctx)
        tag = f"m{layer}"
        d = {k[len(f"L{layer}_ffn_"):]: v for k, v in g.dram.items() if k.startswith(f"L{layer}_ffn_")}
        r = Shared()
        r.tag, r.gate, r.shared_gate, r.renorm, r.final_norm, r.biases = tag, layer, False, False, None, None
        r.s_weights, r.loads, r.jobs = sem(tag + "_weights"), [], []
        if layer != 1:
            g.xT = sb(tag + "_xT", [P, NC, B * S])

        def job(glu, nf, win, outs):
            first = r.jobs[-1].last + 1 if r.jobs else 0
            out0 = r.jobs[-1].out0 + len(r.jobs[-1].outs) if r.jobs else 0
            r.jobs.append(Job(glu, nf, win, outs, first, first + (nf if glu else nf // 2) - 1, out0))

        def chunk(w, off=0):
            return lambda k, f, c: w[:, c, off + f * P:off + (f + 1) * P]
        if layer == 0:
            E, F = d["W2_experts"].shape[0], d["W2_experts"].shape[1]
            r.kind, r.E, r.EL, r.EW, r.k = "grouped", E, E + 2, E, 2
            r.router = [(slice(0, 2), by_rows(d["Wg_gate"])), (slice(2, 10), by_rows(d["We_gate"]))]
            r.biases = (d["group_bias"], d["expert_bias"])
            r.final_norm = d["norm2_w"]
            Wsi, Wso = sb(tag + "_Wsi", [P, NC, 2 * F]), sb(tag + "_Wso", [P, F // P, D])
            W1, W2 = sb(tag + "_W1", [P, NC, 2 * F]), sb(tag + "_W2", [P, E, F // P, D])
            r.loads = [(Wsi[:], by_rows(d["W_shared_in"])), (Wso[:], by_rows(d["W_shared_out"])),
                       (W1[:], by_rows(d["W1_shared"]))]
            r.loads += [(W2[:, e], by_rows(d["W2_experts"][e])) for e in range(E)]
            job(True, F // P, lambda k, f, c: Wsi[:, c, k * F + f * P:k * F + (f + 1) * P],
                [(lambda f: Wso[:, f, :], None)])
            job(True, F // P, lambda k, f, c: W1[:, c, k * F + f * P:k * F + (f + 1) * P],
                [((lambda f, e=e: W2[:, e, f, :]), e) for e in range(E)])
        elif layer == 1:
            E, _, F = d["w1"].shape
            r.kind, r.E, r.EL, r.EW = "expert_choice", E, E, E
            r.capacity = S * 2 // E
            r.router = [(e, d["choice_w"][e].rearrange("(c p) -> p c", p=P)) for e in range(E)]
            r.W1, r.W2 = sb(tag + "_W1", [P, E, NC, F]), sb(tag + "_W2", [P, E, F // P, D])
            r.loads = [(r.W1[:, :, c], d["w1"][:, c * P:(c + 1) * P, :].rearrange("e p f -> p e f")) for c in range(NC)]
            r.loads += [(r.W2[:, :, f], d["w2"][:, f * P:(f + 1) * P, :].rearrange("e p n -> p e n"))
                        for f in range(F // P)]
            r.norm = norm_scratch(sb, tag, B * NT)
            r.slot, r.iota = sb(tag + "_slot", [P, NT, B * E]), sb(tag + "_iota", [P, P])
        elif layer == 2:
            E, _, F = d["w1"].shape
            r.kind, r.E, r.EL, r.EW, r.k, r.shared_gate = "top", E, E + 1, E + 1, 2, True
            r.router = [(slice(0, E), by_rows(d["router_w"])), (slice(E, E + 1), by_rows(d["shared_gate_w"]))]
            W1, W2 = sb(tag + "_W1", [P, E, NC, F]), sb(tag + "_W2", [P, E, F // P, D])
            Wg, Wd = sb(tag + "_Wg", [P, NC, 2 * F]), sb(tag + "_Wd", [P, F // P, D])
            r.loads = [(Wg[:], by_rows(d["shared_gate_up"])), (Wd[:], by_rows(d["shared_down"]))]
            for e in range(E):
                r.loads += [(W1[:, e], by_rows(d["w1"][e])), (W2[:, e], by_rows(d["w2"][e]))]
            job(True, F // P, lambda k, f, c: Wg[:, c, k * F + f * P:k * F + (f + 1) * P],
                [(lambda f: Wd[:, f, :], E)])
            for e in range(E):
                job(False, F // P, (lambda k, f, c, e=e: W1[:, e, c, f * P:(f + 1) * P]),
                    [((lambda f, e=e: W2[:, e, f, :]), e)])
        else:
            E, _, F = d["w1"].shape
            r.kind, r.E, r.EL, r.EW, r.k, r.renorm = "top", E, E, E, 4, True
            r.router = [(e, d["gate_w"][e].rearrange("(c p) -> p c", p=P)) for e in range(E)]
            W1, W3, W2 = (sb(f"{tag}_W{n}", shape) for n, shape in
                          (("1", [P, E, NC, F]), ("3", [P, E, NC, F]), ("2", [P, E, D])))
            for c in range(NC):
                r.loads += [(W[:, :, c], d[n][:, c * P:(c + 1) * P, :].rearrange("e p f -> p e f"))
                            for W, n in ((W1, "w1"), (W3, "w3"))]
            r.loads.append((W2[:], d["w2"].rearrange("e p n -> p e n")))
            for e in range(E):
                job(True, 1, (lambda k, f, c, e=e: (W1, W3)[k][:, e, c, :]), [((lambda f, e=e: W2[:, e, :]), e)])
        r.weights = sb(tag + "_weights", [P, NT, B * r.EW])
        routing(nc, g, sem, r)
        if r.kind == "expert_choice":
            choosing_experts(nc, g, sem, r)
        else:
            experts(nc, g, sem, r)


@contextmanager
def stage(nc):
    with ExitStack() as ctx:
        taken = []

        def sem(name):
            taken.append(ctx.enter_context(nc.semaphore(name)))
            return taken[-1]
        yield sem
        with nc.Block() as block:
            @block.sync
            def _(sp):
                for one in taken:
                    sp.sem_clear(one)


def build(nc, dram, out):
    with ExitStack() as ctx:
        sb, _ = allocators(nc, ctx)

        def sem_kept(name):
            return ctx.enter_context(nc.semaphore(name))

        g = Shared()
        g.dram = dram
        g.x = sb("x_all", [P, B * NT, D])
        g.d_ctxT = nc.dram_tensor("ctx_turned", (B, P, NC, S), F32, kind="Internal").ap()
        g.gates, g.tg = sb("gates", [P, 2, 4]), sb("tanh_gates", [P, 2, 4])
        g.ident, g.ones, g.identb = sb("ident", [P, P]), sb("ones", [P, P]), sb("identb", [P, P], BF16)
        prepare(nc, g, sem_kept)
        with stage(nc) as sem:
            channel_attention(nc, g, sem)
        with ExitStack() as l0:
            g.x2 = l0.enter_context(nc.sbuf_tensor("x2_all", [P, B * NT, D], F32))
            d = {k[7:]: v for k, v in dram.items() if k.startswith("L0_ffn_")}
            d.update(cos=dram["rope_cos"], sin=dram["rope_sin"])
            with stage(nc) as sem:
                head_attention(nc, g, sem, "a0", "self", d, 0)
            with stage(nc) as sem:
                moe_layer(nc, g, sem, 0)
        with stage(nc) as sem:
            head_attention(nc, g, sem, "a1", "causal",
                           {"W" + n: dram["L1_xattn_w" + n] for n in "qkvo"}, 1)
        with stage(nc) as sem:
            moe_layer(nc, g, sem, 1)
        with stage(nc) as sem:
            top_attention(nc, g, sem)
        with stage(nc) as sem:
            moe_layer(nc, g, sem, 2)
        with stage(nc) as sem:
            head_attention(nc, g, sem, "a3", "biased",
                           {k[9:]: v for k, v in dram.items() if k.startswith("L3_xattn_")}, 3)
        with stage(nc) as sem:
            moe_layer(nc, g, sem, 3)
        s_out = sem_kept("out_stored")
        with nc.Block() as block:
            @block.sync
            def _(sp):
                sp.dma_start(out.rearrange("b (t p) d -> p (b t) d", p=P), g.x[:]).then_inc(s_out, 16)
                sp.wait_ge(s_out, 16)


def kernel(**inputs):
    import numpy as _np
    import concourse.bacc as _bacc
    from concourse import mybir as _mybir
    from concourse.bass_utils import run_bass_kernel_spmd as _run
    nc = _bacc.Bacc("TRN2", target_bir_lowering=False, num_devices=1)
    arrays, dram = {}, {}
    for name, a in inputs.items():
        a = _np.ascontiguousarray(a)
        arrays["in_" + name] = a
        dram[name] = nc.dram_tensor("in_" + name, a.shape, _mybir.dt.from_np(a.dtype), kind="ExternalInput").ap()
    freq = (1.0 / 10000.0 ** (_np.arange(0, DH, 2, dtype=_np.float32) / DH)).astype(_np.float32)
    angle = _np.arange(S, dtype=_np.float32)[:, None] * freq[None, :]
    sign = _np.tile(_np.array([-1, 1], _np.float32), DH // 2)
    for name, t in (("rope_cos", _np.repeat(_np.cos(angle), 2, 1)), ("rope_sin", _np.repeat(_np.sin(angle), 2, 1) * sign)):
        arrays["in_" + name] = _np.ascontiguousarray(_np.tile(t.T, (P // DH, 1)), dtype=_np.float32)
        dram[name] = nc.dram_tensor("in_" + name, (P, S), F32, kind="ExternalInput").ap()
    out = nc.dram_tensor("out_0", (B, S, D), F32, kind="ExternalOutput").ap()
    build(nc, dram, out)
    r = _run(nc, [arrays], core_ids=[0])
    return r.results[0]["out_0"]
```

```python
from collections import namedtuple
from contextlib import ExitStack, contextmanager

import concourse.bass as bass
from concourse import mybir

ALU = mybir.AluOpType
ACT = mybir.ActivationFunctionType
AX = mybir.AxisListType
F32 = mybir.dt.float32
BF16 = mybir.dt.bfloat16
I32 = mybir.dt.int32

P = 128
B, S, D = 8, 512, 256
NT = S // P
NC = D // P
NH, DH = 16, 16
HG = NH // 4
RSQRT_SEED = 0x5F3759DF
MASKED = -1.0e30
LN_EPS = 1e-5
RMS_EPS = 1e-6


NormScratch = namedtuple("NormScratch", "stats mean var rstd seed tmp")
Job = namedtuple("Job", "glu nf win outs first last out0")


class Shared:
    pass


class Steps:

    def __init__(self, eng, sem, base=0):
        self.eng, self.sem, self.base, self.n = eng, sem, base, 0
        self.between = None

    def __call__(self, ins):
        self.n += 1
        ins.then_inc(self.sem, 1)
        if self.between:
            self.between()
        self.eng.wait_ge(self.sem, self.base + self.n)


def rsqrt(nc, step, out, seed, tmp, val):
    step(nc.vector.tensor_scalar(seed.bitcast(I32), val.bitcast(I32), 1, None, ALU.logical_shift_right))
    step(nc.vector.tensor_scalar(out.bitcast(I32), seed.bitcast(I32), -1.0, float(RSQRT_SEED), ALU.mult, ALU.add))
    for _ in range(4):
        step(nc.vector.tensor_tensor(tmp, out, out, ALU.mult))
        step(nc.vector.scalar_tensor_tensor(out=seed, in0=tmp, scalar=-0.5, in1=val, op0=ALU.mult, op1=ALU.mult))
        step(nc.vector.scalar_tensor_tensor(out=out, in0=seed, scalar=1.5, in1=out, op0=ALU.add, op1=ALU.mult))


RSQRT_STEPS = 14
LN_STEPS = 4 + RSQRT_STEPS


def layernorm(nc, step, w, xn, x):
    for t in range(NT):
        last = nc.vector.bn_stats(w.stats[:, t, :], x[:, t, :])
    step(last)
    mean_rstd(nc, step, w)
    for t in range(NT):
        last = nc.vector.tensor_scalar(xn[:, t, :], x[:, t, :], w.mean[:, t:t + 1], w.rstd[:, t:t + 1],
                                       ALU.subtract, ALU.mult)
    return last


def mean_rstd(nc, step, w):
    st = w.stats
    nc.vector.tensor_tensor(w.mean[:], st[:, :, 1], st[:, :, 4], ALU.add)
    nc.vector.tensor_tensor(w.tmp[:], st[:, :, 1], st[:, :, 4], ALU.subtract)
    step(nc.vector.tensor_tensor(w.var[:], st[:, :, 2], st[:, :, 5], ALU.add))
    nc.vector.tensor_scalar(w.mean[:], w.mean[:], 0.5, None, ALU.mult)
    nc.vector.tensor_scalar(w.var[:], w.var[:], 1.0 / D, LN_EPS, ALU.mult, ALU.add)
    step(nc.vector.scalar_tensor_tensor(out=w.tmp[:], in0=w.tmp[:], scalar=0.25, in1=w.tmp[:], op0=ALU.mult,
                                        op1=ALU.mult))
    step(nc.vector.tensor_tensor(w.var[:], w.var[:], w.tmp[:], ALU.add))
    rsqrt(nc, step, w.rstd[:], w.seed[:], w.tmp[:], w.var[:])


def norm_scratch(sb, name, tiles=NT):
    return NormScratch(stats=sb(name + "_stats", [P, tiles, 6]),
                       **{n: sb(f"{name}_{n}", [P, tiles]) for n in ("mean", "var", "rstd", "seed", "tmp")})


def rms_rstd(nc, step, w, x):
    for t in range(NT):
        last = nc.vector.bn_stats(w.stats[:, t, :], x[:, t, :])
    step(last)
    st = w.stats
    nc.vector.tensor_tensor(w.mean[:], st[:, :, 1], st[:, :, 4], ALU.add)
    nc.vector.tensor_tensor(w.tmp[:], st[:, :, 1], st[:, :, 4], ALU.subtract)
    step(nc.vector.tensor_tensor(w.var[:], st[:, :, 2], st[:, :, 5], ALU.add))
    nc.vector.scalar_tensor_tensor(out=w.mean[:], in0=w.mean[:], scalar=0.25, in1=w.mean[:], op0=ALU.mult,
                                   op1=ALU.mult)
    nc.vector.tensor_scalar(w.var[:], w.var[:], 1.0 / D, RMS_EPS, ALU.mult, ALU.add)
    step(nc.vector.scalar_tensor_tensor(out=w.tmp[:], in0=w.tmp[:], scalar=0.25, in1=w.tmp[:], op0=ALU.mult,
                                        op1=ALU.mult))
    step(nc.vector.tensor_tensor(w.var[:], w.var[:], w.tmp[:], ALU.add))
    step(nc.vector.tensor_tensor(w.var[:], w.var[:], w.mean[:], ALU.add))
    rsqrt(nc, step, w.rstd[:], w.seed[:], w.tmp[:], w.var[:])


def allocators(nc, ctx):
    def sb(name, shape, dt=F32):
        return ctx.enter_context(nc.sbuf_tensor(name, shape, dt))

    def ps(name, shape, dt=F32):
        return ctx.enter_context(nc.psum_tensor(name, shape, dt))
    return sb, ps


def by_rows(w):
    return w.rearrange("(c p) n -> p c n", p=P)


def row_of(v):
    return v.rearrange("(o n) -> o n", o=1).broadcast_to([P, v.shape[0]])


def batch_of(t, i):
    return t[bass.ds(i, 1)].rearrange("o p c n -> (o p) c n")


def batch(t, i):
    return t[:, bass.ds(i * NT, NT), :]


def prepare(nc, g, sem):
    s_x, s_gate, s_zero, s_one, s_tanh = (sem("prep_" + n) for n in ("x", "gate", "zero", "one", "tanh"))
    with nc.Block() as block:
        @block.sync
        def _(sp):
            for h in range(2):
                b = slice(h * (B // 2) * NT, (h + 1) * (B // 2) * NT)
                r = slice(h * (B // 2), (h + 1) * (B // 2))
                sp.dma_start(g.x[:, b, :], g.dram["x"][r].rearrange("b (t p) d -> p (b t) d", p=P)).then_inc(s_x, 16)
            for k, name in enumerate(("g_xattn", "g_ffn")):
                sp.dma_start(g.gates[:, k, :], g.dram[name].rearrange("(o n) -> o n", o=1).broadcast_to([P, 4])
                             ).then_inc(s_gate, 16)
            sp.wait_ge(s_x, 32)

        @block.gpsimd
        def _(pool):
            nc.gpsimd.memset(g.ident[:], 0.0).then_inc(s_zero, 1)
            nc.gpsimd.memset(g.ones[:], 1.0).then_inc(s_one, 1)
            pool.wait_ge(s_zero, 1)
            nc.gpsimd.affine_select(out=g.ident[:], in_=g.ident[:], compare_op=ALU.not_equal, fill=1.0, base=0,
                                    pattern=[[-1, P]], channel_multiplier=1).then_inc(s_one, 1)

        @block.scalar
        def _(act):
            act.wait_ge(s_gate, 32)
            nc.scalar.activation(g.tg[:], g.gates[:], ACT.Tanh).then_inc(s_tanh, 1)
            act.wait_ge(s_tanh, 1)

        @block.vector
        def _(dve):
            dve.wait_ge(s_one, 2)
            nc.vector.tensor_copy(g.identb[:], g.ident[:]).then_inc(s_zero, 1)
            dve.wait_ge(s_zero, 2)


def channel_attention(nc, g, sem):
    names = ("load", "ctx", "free", "xn", "gram", "ctxT", "ctxTc", "exp_in", "exp", "m", "mT", "mTc", "y", "x",
             "dve", "const", "kept", "passed", "ctx_in", "gs", "stats")
    Sems = namedtuple("Sems", names)
    s = Sems(*(sem("ca_" + n) for n in names))
    HW = 64
    with ExitStack() as ctx:
        sb, ps = allocators(nc, ctx)
        ctx_all = sb("ca_ctx_all", [P, B * NT, D])
        ctx_fix = sb("ca_ctx", [P, NT, D])
        ctxT = sb("ca_ctxT", [P, NC, S])
        xn = sb("ca_xn", [P, NT, D])
        w = norm_scratch(sb, "ca", B * NT)
        col = {n: sb("ca_c" + n, [P, 2, NC]) for n in ("wq", "bq")}
        row = {n: sb("ca_r" + n, [P, 2, NC, HW]) for n in ("wk", "bk", "wv", "bv")}
        wp, bp, wp2 = (sb("ca_" + n, [P, NC]) for n in ("wp", "bp", "wp2"))
        gs = sb("ca_gs", [P, 320])
        T, U = sb("ca_T", [P, 2, NC, HW]), sb("ca_U", [P, 2, NC, HW])
        A, mx, sm, rc, cs = (sb("ca_" + n, [P, 2, NC]) for n in ("A", "mx", "sm", "rc", "cs"))
        cst = sb("ca_cst", [P, NC])
        Mbd, MT, Dg = (sb("ca_" + n, [P, NC, P]) for n in ("Mbd", "MT", "Dg"))
        pG = ps("ca_pG", [P, 512])
        pT = ps("ca_pT", [P, NC, S])
        pM = ps("ca_pM", [P, 512])
        pY = ps("ca_pY", [P, NT, D])
        G = gs[:, 0:128].rearrange("p (c e) -> p c e", c=NC)
        sx = gs[:, 128:130]
        sc = gs[:, 192:320].rearrange("p (c e) -> p c e", c=NC)
        NLOAD = 4 + 2 + 16
        K = 16

        def run(eng, turn):
            turn(0, False, True)
            with eng.Fori(1, B - 1) as i:
                turn(i, True, True)
            turn(B - 1, True, False)
        with nc.Block() as block:
            @block.sync
            def _(sp):
                for h in range(2):
                    b = slice(h * (B // 2) * NT, (h + 1) * (B // 2) * NT)
                    r = slice(h * (B // 2), (h + 1) * (B // 2))
                    sp.dma_start(ctx_all[:, b, :], g.dram["ctx_1024"][r].rearrange("b (t p) d -> p (b t) d", p=P)
                                 ).then_inc(s.ctx_in, 16)
                for k, kind in enumerate("gl"):
                    for n in ("wq", "bq"):
                        sp.dma_start(col[n][:, k, :], g.dram[f"L0_xattn_{n}{kind}"].rearrange("(c p) -> p c", p=P),
                                     allow_slow_non_contiguous=True).then_inc(s.load, 16)
                sp.dma_start(wp[:], g.dram["L0_xattn_wp"].rearrange("(c p) -> p c", p=P),
                             allow_slow_non_contiguous=True).then_inc(s.load, 16)
                sp.dma_start(bp[:], g.dram["L0_xattn_bp"].rearrange("(c p) -> p c", p=P),
                             allow_slow_non_contiguous=True).then_inc(s.load, 16)
                for k, kind in enumerate("gl"):
                    for n in ("wk", "bk", "wv", "bv"):
                        v = g.dram[f"L0_xattn_{n}{kind}"].rearrange("(c j e) -> j c e", j=2, e=HW)
                        for j in range(2):
                            sp.dma_start(row[n][HW * j:HW * j + HW, k, :, :],
                                         v[j:j + 1].broadcast_to([HW, NC, HW])).then_inc(s.load, 16)
                with sp.Fori(0, B) as i:
                    sp.wait_ge(s.ctxTc, i + 1)
                    sp.sem_inc(s.passed, 1)
                    sp.dma_start(batch_of(g.d_ctxT, i), ctxT[:]).then_inc(s.kept, 16)
                sp.wait_ge(s.kept, 16 * B)

            @block.gpsimd
            def _(pool):
                nc.gpsimd.memset(Mbd[:], 0.0).then_inc(s.const, 1)
                pool.wait_ge(s.ctx_in, 32)
                nc.gpsimd.tensor_copy(ctx_fix[:], batch(ctx_all, 0)).then_inc(s.ctx, 1)

                def turn(k, before, after):
                    if after:
                        pool.wait_ge(s.gram, k + 1)
                        nc.gpsimd.tensor_copy(ctx_fix[:], batch(ctx_all, k + 1)).then_inc(s.ctx, 1)
                run(pool, turn)

            @block.tensor
            def _(pe):
                def gram(n, first=False):
                    pe.wait_ge(s.ctx, n + 1)
                    if not first:
                        pe.wait_ge(s.ctxTc, n)
                    for c in range(NC):
                        for t in range(NT):
                            last = nc.tensor.transpose(pT[:, c, t * P:(t + 1) * P], ctx_fix[:, t, c * P:(c + 1) * P],
                                                       g.ident[:])
                    last.then_inc(s.ctxT, 1)
                    pe.wait_ge(s.xn, n + 1)
                    if not first:
                        pe.wait_ge(s.gs, n)
                    for c in range(NC):
                        for j in range(2):
                            h = slice((2 * c + j) * HW, (2 * c + j + 1) * HW)
                            o = slice(HW * j, HW * j + HW)
                            for t in range(NT):
                                nc.tensor.matmul(pG[o, c * HW:c * HW + HW], xn[:, t, h], ctx_fix[:, t, h],
                                                 start=t == 0, stop=t == NT - 1)
                            for t in range(NT):
                                nc.tensor.matmul(pG[o, 128 + c:129 + c], xn[:, t, h], g.ones[:, 0:1],
                                                 start=t == 0, stop=t == NT - 1)
                            for t in range(NT):
                                last = nc.tensor.matmul(pG[o, 192 + c * HW:192 + c * HW + HW], g.ones[:, 0:HW],
                                                        ctx_fix[:, t, h], start=t == 0, stop=t == NT - 1)
                    last.then_inc(s.gram, 1)

                def turn(k, before, after):
                    if after:
                        gram(k + 1)
                    pe.wait_ge(s.m, k + 1)
                    for c in range(NC):
                        last = nc.tensor.transpose(pM[:, c * P:(c + 1) * P], Mbd[:, c, :], g.ident[:])
                    last.then_inc(s.mT, 1)
                    pe.wait_ge(s.mTc, k + 1)
                    pe.wait_ge(s.ctxTc, k + 1)
                    if before:
                        pe.wait_ge(s.x, k)
                    for t in range(NT):
                        for c in range(NC):
                            o = pY[:, t, c * P:(c + 1) * P]
                            nc.tensor.matmul(o, ctxT[:, c, t * P:(t + 1) * P], MT[:, c, :], start=True, stop=False)
                            last = nc.tensor.matmul(o, g.ones[:], Dg[:, c, :], start=False, stop=True)
                    last.then_inc(s.y, 1)
                gram(0, first=True)
                run(pe, turn)

            @block.scalar
            def _(act):
                act.wait_ge(s.ctxT, 1)
                nc.scalar.copy(ctxT[:], pT[:]).then_inc(s.ctxTc, 1)

                def turn(k, before, after):
                    act.wait_ge(s.exp_in, k + 1)
                    nc.scalar.activation(T[:], T[:], ACT.Exp, scale=float(D) ** -0.5).then_inc(s.exp, 1)
                    act.wait_ge(s.mT, k + 1)
                    nc.scalar.copy(MT[:], pM[:, 0:NC * P].rearrange("p (c n) -> p c n", c=NC)).then_inc(s.mTc, 1)
                    if after:
                        act.wait_ge(s.ctxT, k + 2)
                        act.wait_ge(s.y, k + 1)
                        act.wait_ge(s.kept, k * 16 + 16)
                        nc.scalar.copy(ctxT[:], pT[:]).then_inc(s.ctxTc, 1)
                run(act, turn)

            @block.vector
            def _(dve):
                with dve.Fori(0, B) as i:
                    for t in range(NT):
                        last = nc.vector.bn_stats(batch(w.stats, i)[:, t, :], batch(g.x, i)[:, t, :])
                    last.then_inc(s.stats, 1)
                dve.wait_ge(s.stats, B)
                pre = Steps(dve, s.dve)
                mean_rstd(nc, pre, w)

                def norm(n):
                    for t in range(NT):
                        row = bass.ds(n * NT + t, 1)
                        last = nc.vector.tensor_scalar(xn[:, t, :], g.x[:, row, :].rearrange("p o d -> p (o d)"),
                                                       w.mean[:, row], w.rstd[:, row], ALU.subtract, ALU.mult)
                    last.then_inc(s.xn, 1)
                norm(0)
                dve.wait_ge(s.load, 16 * NLOAD)
                dve.wait_ge(s.const, 1)
                pre(nc.vector.tensor_scalar(wp2[:], wp[:], g.tg[:, 0, 0:1], 2.0, ALU.mult, ALU.mult))
                pre(nc.vector.tensor_scalar(bp[:], bp[:], g.tg[:, 0, 0:1], None, ALU.mult))
                four = [P, 2, NC, HW]

                def add_output(b):
                    dve.wait_ge(s.y, b + 1)
                    x = batch(g.x, b)
                    nc.vector.tensor_tensor(x, pY[:], x, ALU.add).then_inc(s.x, 1)

                def turn(k, before, after):
                    step = Steps(dve, s.dve, pre.n + k * K)
                    dve.wait_ge(s.gram, k + 1)
                    nc.vector.tensor_copy(gs[:, 0:130], pG[:, 0:130])
                    nc.vector.tensor_copy(gs[:, 192:320], pG[:, 192:320]).then_inc(s.gs, 1)
                    if after:
                        norm(k + 1)
                    dve.wait_ge(s.gs, k + 1)
                    nc.vector.tensor_tensor(A[:], col["wq"][:], sx.unsqueeze(1).broadcast_to([P, 2, NC]), ALU.mult)
                    step(nc.vector.tensor_tensor(T[:], G.unsqueeze(1).broadcast_to(four),
                                                 col["wq"][:].unsqueeze(3).broadcast_to(four), ALU.mult))
                    step(nc.vector.scalar_tensor_tensor(out=A[:], in0=col["bq"][:], scalar=float(S), in1=A[:],
                                                        op0=ALU.mult, op1=ALU.add))
                    nc.vector.tensor_tensor(T[:], T[:], row["wk"][:], ALU.mult)
                    step(nc.vector.tensor_tensor(U[:], row["bk"][:], A[:].unsqueeze(3).broadcast_to(four), ALU.mult))
                    step(nc.vector.tensor_tensor(T[:], T[:], U[:], ALU.add))
                    step(nc.vector.tensor_tensor(U[:], row["wk"][:], sc.unsqueeze(1).broadcast_to(four), ALU.mult))
                    step(nc.vector.tensor_tensor(U[:], U[:], col["bq"][:].unsqueeze(3).broadcast_to(four), ALU.mult))
                    step(nc.vector.tensor_tensor(T[:], T[:], U[:], ALU.add))
                    step(nc.vector.tensor_reduce(mx[:], T[:], AX.X, ALU.max))
                    nc.vector.tensor_tensor(T[:], T[:], mx[:].unsqueeze(3).broadcast_to(four), ALU.subtract
                                            ).then_inc(s.exp_in, 1)
                    if before:
                        add_output(k - 1)
                    dve.wait_ge(s.exp, k + 1)
                    step(nc.vector.tensor_reduce(sm[:], T[:], AX.X, ALU.add))
                    step(nc.vector.reciprocal(rc[:], sm[:]))
                    step(nc.vector.tensor_tensor(rc[:], rc[:], wp2[:].unsqueeze(1).broadcast_to([P, 2, NC]), ALU.mult))
                    step(nc.vector.tensor_tensor(T[:], T[:], rc[:].unsqueeze(3).broadcast_to(four), ALU.mult))
                    step(nc.vector.tensor_tensor(U[:], T[:], row["bv"][:], ALU.mult))
                    nc.vector.tensor_tensor(T[:], T[:], row["wv"][:], ALU.mult)
                    step(nc.vector.tensor_reduce(cs[:], U[:], AX.X, ALU.add))
                    nc.vector.tensor_tensor(cst[:], cs[:, 0, :], bp[:], ALU.add)
                    for j in range(2):
                        q = slice(HW * j, HW * j + HW)
                        last = nc.vector.tensor_tensor(Mbd[q, :, HW * j:HW * j + HW], T[q, 0], T[q, 1], ALU.add)
                    step(last)
                    step(nc.vector.tensor_tensor(cst[:], cst[:], cs[:, 1, :], ALU.add))
                    for c in range(NC):
                        last = nc.vector.tensor_scalar(Dg[:, c, :], g.ident[:], cst[:, c:c + 1], None, ALU.mult)
                    last.then_inc(s.m, 1)
                    assert step.n == K, step.n
                run(dve, turn)
                add_output(B - 1)
                dve.wait_ge(s.x, B)


PAIRS = ((0, 0), (0, 1), (1, 0), (1, 1), (0, 2), (2, 0))
KS = DH * len(PAIRS)
KM = KS + 3


def load_transposed(nc, g, sb, ps, sem, tag, weights):
    s_in, s_t, s_c = sem(tag + "_w_in"), sem(tag + "_w_t"), sem(tag + "_w_c")
    turned = [sb(f"{tag}_wT{n}", [P, NC, D]) for n in range(len(weights))]
    with ExitStack() as ctx:
        sb2, ps2 = allocators(nc, ctx)
        raw = [sb2(f"{tag}_raw{n}", [P, NC, D]) for n in range(len(weights))]
        pW = ps2(tag + "_pW", [P, 2, NC, D])
        with nc.Block() as block:
            @block.sync
            def _(sp):
                for n, wt in enumerate(weights):
                    sp.dma_start(raw[n][:], wt.rearrange("(c p) k -> p c k", p=P)).then_inc(s_in, 16)

            @block.tensor
            def _(pe):
                pe.wait_ge(s_in, 16 * len(weights))
                for n in range(len(weights)):
                    if n >= 2:
                        pe.wait_ge(s_c, n - 1)
                    for c in range(NC):
                        for k in range(NC):
                            last = nc.tensor.transpose(pW[:, n % 2, k, c * P:(c + 1) * P],
                                                       raw[n][:, c, k * P:(k + 1) * P], g.ident[:])
                    last.then_inc(s_t, 1)

            @block.scalar
            def _(act):
                for n in range(len(weights)):
                    act.wait_ge(s_t, n + 1)
                    nc.scalar.copy(turned[n][:], pW[:, n % 2]).then_inc(s_c, 1)
                act.wait_ge(s_c, len(weights))
    return turned


def head_attention(nc, g, sem, tag, kind, wts, gate):
    self_attn, causal, biased = kind == "self", kind == "causal", kind == "biased"
    names = ("load", "scaled", "const", "dve", "pool", "xn", "xT", "xTc", "kv", "passed", "cT", "cTc", "q", "qsw", "k",
             "ksw", "v", "qf", "kf", "qm", "qr", "km", "kr", "vc", "qp", "kp", "qw", "kw", "qs", "ks", "S", "max",
             "mm", "mT", "mTc", "mw", "mrow", "ST", "exp", "pv", "oev", "ot", "nrm", "ob", "otc", "y", "x", "kept", "added")
    Sems = namedtuple("Sems", names)
    s = Sems(*(sem(f"{tag}_{n}") for n in names))
    HC = 64
    NS = NH * NT
    NW = HG * NT
    MAIN = NW + 1
    FIRST_MAX = 5 if biased else 4
    MAX_SLOTS = NW - FIRST_MAX
    LATE = 6 if biased or self_attn else 18
    cut = [(NS - LATE) * n // MAX_SLOTS for n in range(MAX_SLOTS + 1)]
    late = [range(NS - LATE + LATE * n // 3, NS - LATE + LATE * (n + 1) // 3) for n in range(3)]
    NORM_SLOT = 2 * NT + 1

    def max_units(slot):
        n = slot - FIRST_MAX
        return range(cut[n], cut[n + 1]) if 0 <= n < MAX_SLOTS else ()

    def wait(eng, semaphore, value):
        if not isinstance(value, int) or value > 0:
            eng.wait_ge(semaphore, value)

    def run(eng, front, turn):
        front(0, 0)
        turn(0, 0, False, True, True)
        with eng.Fori(1, B - 2, 2) as i:
            turn(i, 1, True, True, True)
            turn(i + 1, 0, True, True, True)
        turn(B - 1, 1, True, True, False)
        turn(B, 0, True, False, False)

    with ExitStack() as ctx:
        sb, ps = allocators(nc, ctx)
        if self_attn:
            Wq, Wqs, Wks = sb(tag + "_Wq", [P, NC, D]), sb(tag + "_Wqs", [P, NC, D]), sb(tag + "_Wks", [HC, D])
            Wc, Wkv = sb(tag + "_Wc", [P, NC, 2, HC]), sb(tag + "_Wkv", [P, D])
            Wk, Wv = Wkv[0:HC], Wkv[HC:P]
            Wo = sb(tag + "_Wo", [P, NC, D])
            kvc = sb(tag + "_kvc", [P, S])
            cos, sin = sb(tag + "_cos", [P, S]), sb(tag + "_sin", [P, S])
            normw = sb(tag + "_normw", [P, D])
        else:
            Wq, Wk, Wv, Wo = load_transposed(nc, g, sb, ps, sem, tag, [wts[n] for n in ("Wq", "Wk", "Wv", "Wo")])
            kvT = sb(tag + "_kvT", [P, NC, S])
        if biased:
            bq, bk = sb(tag + "_bq", [P, NC]), sb(tag + "_bk", [P, NC])
            bv, bo = sb(tag + "_bv", [P, D]), sb(tag + "_bo", [P, D])
        if causal:
            mask_q, mask_k = sb(tag + "_mask_q", [P, P], BF16), sb(tag + "_mask_k", [P, P], BF16)
        xnT, w = sb(tag + "_xnT", [P, NC, S]), norm_scratch(sb, tag)
        rope = sb(tag + "_rope", [P, NC, S])
        xn = rope[:].rearrange("p c n -> p (c n)").rearrange("p (t n) -> p t n", t=NT)
        qf, qp = sb(tag + "_qf", [P, NC, S]), sb(tag + "_qp", [P, 3, NC, S], BF16)
        kf, kp = (qf, qp) if self_attn else (sb(tag + "_kf", [P, NC, S]), sb(tag + "_kp", [P, 3, NC, S], BF16))
        qs, ks = sb(tag + "_qs", [P, 2, NH, S], BF16), sb(tag + "_ks", [P, 2, NH, S], BF16)
        V = sb(tag + "_V", [P, 2, NT, NH, 32])
        nm, nr = sb(tag + "_nm", [P, NT, NH]), sb(tag + "_nr", [P, NT, NH])
        mm, mTb = sb(tag + "_mm", [P, NT, 3, NH], BF16), sb(tag + "_mTb", [3 * NH, S], BF16)
        Pb = sb(tag + "_P", [P, 2, 4, S])
        Osb, rd = sb(tag + "_Osb", [P, HG, S]), sb(tag + "_rd", [P, NT, NH])
        On = Pb[:, 1, 0:2].rearrange("p c n -> p (c n)").rearrange("p (t n) -> p t n", t=NT)
        onT = Pb[:, 1, 2:4]
        pST, pS = ps(tag + "_pST", [P, 2, 2, S]), ps(tag + "_pS", [P, 2, S])
        pO, pM = ps(tag + "_pO", [P, S]), ps(tag + "_pM", [P, S])

        def by_tokens(t):
            return t.rearrange("p a n -> p (a n)").rearrange("p (t n) -> p t n", t=NT)
        half = {n: pST[:, m % 2] for m, n in enumerate(("xT", "C", "Q", "Qs", "K", "Ks", "V") if self_attn else
                                                       ("xT", "Q", "K", "V"))}
        pV, pY = by_tokens(half["V"]), by_tokens(pS[:])
        d_parts = {n: nc.dram_tensor(f"{tag}_d{n}", (3, D, S), BF16, kind="Internal").ap() for n in "qk"}
        d_max = nc.dram_tensor(f"{tag}_dm", (3 * NH, S), BF16, kind="Internal").ap()
        NLOAD = {"self": 9, "causal": 0, "biased": 4}[kind]
        NCONST = {"self": 3 + 4, "causal": 3 + 2, "biased": 3}[kind]
        with nc.Block() as block:
            @block.sync
            def _(sp):
                if self_attn:
                    sp.dma_start(Wq[:], by_rows(wts["Wq"])).then_inc(s.load, 16)
                    sp.dma_start(Wo[:], by_rows(wts["Wo"])).then_inc(s.load, 16)
                    sp.dma_start(Wk, wts["Wk"]).then_inc(s.load, 16)
                    sp.dma_start(Wv, wts["Wv"]).then_inc(s.load, 16)
                    for n, m in enumerate(("Wk_c", "Wv_c")):
                        sp.dma_start(Wc[:, :, n], by_rows(wts[m])).then_inc(s.load, 16)
                    for table, name in ((cos, "cos"), (sin, "sin")):
                        sp.dma_start(table[:], wts[name]).then_inc(s.load, 16)
                    sp.dma_start(normw[:], row_of(wts["norm1_w"])).then_inc(s.load, 16)
                if biased:
                    for t, n in ((bq, "bq"), (bk, "bk")):
                        sp.dma_start(t[:], wts[n].rearrange("(c p) -> p c", p=P),
                                     allow_slow_non_contiguous=True).then_inc(s.load, 16)
                    for t, n in ((bv, "bv"), (bo, "bo")):
                        sp.dma_start(t[:], row_of(wts[n])).then_inc(s.load, 16)

                def load_ctx(n):
                    if not self_attn:
                        wait(sp, s.v, n)
                        sp.sem_inc(s.passed, 1)
                        sp.dma_start(kvT[:], batch_of(g.d_ctxT, n)).then_inc(s.kv, 16)

                def front(n, pn):
                    if isinstance(n, int) and n == 0:
                        load_ctx(n)
                    for src, dram, dst, ready, wrote, there in (
                            (qp, d_parts["q"], qs, s.qp, s.qw, s.qs), (kp, d_parts["k"], ks, s.kp, s.kw, s.ks)):
                        sp.wait_ge(ready, n + 1)
                        for r in range(3):
                            sp.dma_start(dram[r].rearrange("(c p) t -> p c t", p=P), src[:, r]).then_inc(wrote, 16)
                        sp.wait_ge(wrote, n * 48 + 48)
                        for m, pair in enumerate(PAIRS):
                            r = pair[0] if dst is qs else pair[1]
                            sp.dma_start(dst[DH * m:DH * m + DH, pn], dram[r].rearrange("(h d) t -> d h t", d=DH)
                                         ).then_inc(there, 16)

                def turn(k, pk, before, now, after):
                    if after:
                        load_ctx(k + 1)
                    if now:
                        sp.wait_ge(s.mTc, k + 1)
                        sp.dma_start(d_max, mTb[:]).then_inc(s.mw, 16)
                        sp.wait_ge(s.mw, k * 16 + 16)
                        sp.dma_start(qs[KS:KM, pk], d_max.rearrange("(r h) t -> r h t", h=NH)).then_inc(s.mrow, 16)
                    if after:
                        front(k + 1, 1 - pk)
                run(sp, front, turn)

            @block.gpsimd
            def _(pool):
                pre = Steps(pool, s.pool)
                nc.gpsimd.memset(V[:], 0.0).then_inc(s.const, 1)
                pool.wait_ge(s.const, 1)
                nc.gpsimd.memset(V[:, :, :, :, DH:DH + 1], 1.0).then_inc(s.const, 1)
                pool.wait_ge(s.const, 2)
                nc.gpsimd.memset(ks[KS:P], 1.0).then_inc(s.const, 1)
                pool.wait_ge(s.const, 3)
                if causal:
                    pre(nc.gpsimd.memset(mask_q[:], 0.0))
                    pre(nc.gpsimd.memset(mask_k[:], 0.0))
                    nc.gpsimd.affine_select(out=mask_q[:], in_=mask_q[:], compare_op=ALU.is_ge, fill=MASKED, base=0,
                                            pattern=[[-1, P]], channel_multiplier=1).then_inc(s.const, 1)
                    nc.gpsimd.affine_select(out=mask_k[:], in_=mask_k[:], compare_op=ALU.is_ge, fill=MASKED, base=0,
                                            pattern=[[1, P]], channel_multiplier=-1).then_inc(s.const, 1)
                if self_attn:
                    pool.wait_ge(s.load, 16 * NLOAD)
                    for e in range(2):
                        nc.gpsimd.tensor_copy(Wqs[:].rearrange("p c (n e) -> p c n e", e=2)[:, :, :, e],
                                              Wq[:].rearrange("p c (n e) -> p c n e", e=2)[:, :, :, 1 - e]
                                              ).then_inc(s.const, 1)
                        pool.wait_ge(s.const, 3 + 2 * e + 1)
                        nc.gpsimd.tensor_copy(Wks[:].rearrange("p (n e) -> p n e", e=2)[:, :, e],
                                              Wk.rearrange("p (n e) -> p n e", e=2)[:, :, 1 - e]
                                              ).then_inc(s.const, 1)
                        pool.wait_ge(s.const, 3 + 2 * e + 2)

            @block.tensor
            def _(pe):
                if NLOAD:
                    pe.wait_ge(s.load, 16 * NLOAD)
                pe.wait_ge(s.const, NCONST)
                pe.wait_ge(s.scaled, 1)

                def project(out, W, src):
                    for m in range(NC):
                        for c in range(len(W)):
                            last = nc.tensor.matmul(out[:, m, :], W[c][:, m * P:(m + 1) * P], src[c],
                                                    start=c == 0, stop=c == len(W) - 1)
                    return last

                def tiles(W):
                    return [W[:, c, :] for c in range(NC)]

                def front_xT(n, b):
                    pe.wait_ge(s.xn, n + 1)
                    if b is None:
                        wait(pe, s.vc, n)
                        if not self_attn:
                            wait(pe, s.kf, n)
                    else:
                        pe.wait_ge(s.exp, (b + 1) * 2 * NW)
                    for c in range(NC):
                        for t in range(NT):
                            last = nc.tensor.transpose(half["xT"][:, c, t * P:(t + 1) * P],
                                                       xn[:, t, c * P:(c + 1) * P], g.ident[:])
                    last.then_inc(s.xT, 1)

                def front_compressed(n):
                    pe.wait_ge(s.xTc, n + 1)
                    wait(pe, s.kf, n)
                    for c in range(NC):
                        last = nc.tensor.matmul(half["C"][:, 0], Wc[:, c].rearrange("p n j -> p (n j)"), xnT[:, c, :],
                                                start=c == 0, stop=c == NC - 1)
                    last.then_inc(s.cT, 1)

                def front_q(n):
                    pe.wait_ge(s.xTc, n + 1)
                    if not self_attn:
                        wait(pe, s.vc, n)
                    project(half["Q"], tiles(Wq), tiles(xnT)).then_inc(s.q, 1)

                def front_q_swapped(n):
                    pe.wait_ge(s.cTc, n + 1)
                    project(half["Qs"], tiles(Wqs), tiles(xnT)).then_inc(s.qsw, 1)

                def front_k(n):
                    if self_attn:
                        pe.wait_ge(s.qm, n + 1)
                        project(half["K"], [Wk], [kvc[0:HC]]).then_inc(s.k, 1)
                    else:
                        pe.wait_ge(s.kv, n * 16 + 16)
                        project(half["K"], tiles(Wk), tiles(kvT)).then_inc(s.k, 1)

                def front_k_swapped(n):
                    pe.wait_ge(s.qr, n + 1)
                    project(half["Ks"], [Wks[:]], [kvc[0:HC]]).then_inc(s.ksw, 1)

                def front_v(n):
                    pe.wait_ge(s.km if self_attn else s.qf, n + 1)
                    for t in range(NT):
                        if self_attn:
                            last = nc.tensor.matmul(pV[:, t, :], kvc[HC:P, t * P:(t + 1) * P], Wv,
                                                    start=True, stop=True)
                        else:
                            for c in range(NC):
                                last = nc.tensor.matmul(pV[:, t, :], kvT[:, c, t * P:(t + 1) * P], Wv[:, c, :],
                                                        start=c == 0, stop=c == NC - 1)
                    last.then_inc(s.v, 1)

                def maxima(units, a, pa):
                    for n in units:
                        if n == 0:
                            pe.wait_ge(s.qs, a * 96 + 96)
                            pe.wait_ge(s.ks, a * 96 + 96)
                            wait(pe, s.added, a)
                        h, t = divmod(n, NT)
                        if n >= 2:
                            pe.wait_ge(s.max, a * NS + n - 1)
                        keys = (t + 1) * P if causal else S
                        last = nc.tensor.matmul(pS[:, n % 2, 0:keys], qs[0:KS, pa, h, t * P:(t + 1) * P],
                                                ks[0:KS, pa, h, 0:keys], start=True, stop=not causal)
                        if causal:
                            last = nc.tensor.matmul(pS[:, n % 2, t * P:keys], g.identb[:], mask_q[:],
                                                    start=False, stop=True)
                        last.then_inc(s.S, 1)

                def turn_maxima(a):
                    pe.wait_ge(s.mm, a + 1)
                    for t in range(NT):
                        last = nc.tensor.matmul(pS[0:3 * NH, 0, t * P:(t + 1) * P],
                                                mm[:, t].rearrange("p r h -> p (r h)"), g.identb[:],
                                                start=True, stop=True)
                    last.then_inc(s.mT, 1)

                def scores(slot, pair, b, pb):
                    hg, kt = divmod(slot, NT)
                    lo = kt * P if causal else 0
                    if slot == 0 and pair == 0:
                        pe.wait_ge(s.mrow, b * 16 + 16)
                        fronts = min(b + 2, B) if isinstance(b, int) else b + 2
                        pe.wait_ge(s.kf, fronts)
                        pe.wait_ge(s.vc, fronts)
                    if slot >= 1:
                        pe.wait_ge(s.exp, b * 2 * NW + 2 * slot + pair - 1)
                    for j in range(2):
                        h = 4 * hg + 2 * pair + j
                        o = pST[:, pair, j]
                        last = nc.tensor.matmul(o[:, lo:S], ks[0:KM, pb, h, kt * P:(kt + 1) * P],
                                                qs[0:KM, pb, h, lo:S], start=True, stop=not causal)
                        if causal:
                            last = nc.tensor.matmul(o[:, lo:lo + P], g.identb[:], mask_k[:],
                                                    start=False, stop=True)
                    last.then_inc(s.ST, 1)

                def values(n, pair, b, pb):
                    hg, kt = divmod(n, NT)
                    lo = kt * P if causal else 0
                    if pair == 0:
                        if kt == 0 and hg >= 1:
                            pe.wait_ge(s.oev, b * HG + hg)
                        pe.wait_ge(s.exp, b * 2 * NW + 2 * n + 2)
                    for j in range(2 * pair, 2 * pair + 2):
                        last = nc.tensor.matmul(pO[32 * j:32 * j + 32, lo:S], V[:, pb, kt, 4 * hg + j, :],
                                                Pb[:, n % 2, j, lo:S], start=kt == 0, stop=kt == NT - 1)
                    if pair == 1:
                        last.then_inc(s.pv, 1)

                def turn_output(b, t):
                    if t == 0:
                        pe.wait_ge(s.oev, b * HG + HG)
                    if t >= 2:
                        pe.wait_ge(s.nrm, b * NT + t - 1)
                    for h in range(HG):
                        last = nc.tensor.transpose((pM, pO)[t % 2][:, h * P:(h + 1) * P],
                                                   Osb[:, h, t * P:(t + 1) * P], g.ident[:])
                    last.then_inc(s.ot, 1)

                def turn_back(b):
                    pe.wait_ge(s.nrm, b * NT + NT)
                    wait(pe, s.mTc, min(b + 2, B) if isinstance(b, int) else b + 2)
                    for c in range(NC):
                        for t in range(NT):
                            last = nc.tensor.transpose(pS[:, c, t * P:(t + 1) * P],
                                                       On[:, t, c * P:(c + 1) * P], g.ident[:])
                    last.then_inc(s.ob, 1)

                def project_output(b):
                    pe.wait_ge(s.otc, b + 1)
                    for t in range(NT):
                        for c in range(NC):
                            last = nc.tensor.matmul(pY[:, t, :], onT[:, c, t * P:(t + 1) * P], Wo[:, c, :],
                                                    start=c == 0, stop=c == NC - 1)
                    last.then_inc(s.y, 1)

                def front(n, pn):
                    front_xT(n, None)
                    if self_attn:
                        front_compressed(n)
                    front_q(n)
                    if self_attn:
                        front_q_swapped(n)
                    front_k(n)
                    if self_attn:
                        front_k_swapped(n)
                    front_v(n)

                def turn(k, pk, before, now, after):
                    for slot in range(MAIN):
                        units = max_units(slot) if now else ()
                        for part in range(4):
                            if before and part < 2 and slot < NW:
                                scores(slot, part, k - 1, 1 - pk)
                            if before and part >= 2 and slot >= 1:
                                values(slot - 1, part - 2, k - 1, 1 - pk)
                            maxima(units[len(units) * part // 4:len(units) * (part + 1) // 4], k, pk)
                    if after:
                        front_xT(k + 1, k - 1 if before else None)
                    for t in range(NT):
                        if now and t < len(late):
                            maxima(late[t], k, pk)
                        if after and t == 0 and self_attn:
                            front_compressed(k + 1)
                        if after and t == (2 if self_attn else 1):
                            front_q(k + 1)
                        if now and t == 2:
                            turn_maxima(k)
                        if before:
                            turn_output(k - 1, t)
                    if after:
                        if self_attn:
                            front_q_swapped(k + 1)
                        front_k(k + 1)
                    if before:
                        turn_back(k - 1)
                    if after:
                        if self_attn:
                            front_k_swapped(k + 1)
                        front_v(k + 1)
                    if before:
                        project_output(k - 1)
                run(pe, front, turn)

            @block.scalar
            def _(act):
                if biased:
                    act.wait_ge(s.load, 16 * NLOAD)
                act.wait_ge(s.const, NCONST)
                def shifted(dst, src, bias):
                    if not biased:
                        return nc.scalar.copy(dst[:], src)
                    for c in range(NC):
                        last = nc.scalar.activation(dst[:, c], src[:, c], ACT.Identity, bias=bias[:, c:c + 1])
                    return last

                def turned_x(n):
                    act.wait_ge(s.xT, n + 1)
                    nc.scalar.copy(xnT[:], half["xT"]).then_inc(s.xTc, 1)

                def front_early(n):
                    if self_attn:
                        act.wait_ge(s.cT, n + 1)
                        nc.scalar.copy(kvc[:], half["C"][:, 0]).then_inc(s.cTc, 1)
                    else:
                        act.wait_ge(s.q, n + 1)
                        wait(act, s.qp, n)
                        shifted(qf, half["Q"], bq if biased else None).then_inc(s.qf, 1)

                def front_middle(n):
                    if not self_attn:
                        act.wait_ge(s.k, n + 1)
                        wait(act, s.kp, n)
                        shifted(kf, half["K"], bk if biased else None).then_inc(s.kf, 1)

                def front_late(n, pn):
                    if not biased:
                        act.wait_ge(s.v, n + 1)
                        nc.scalar.copy(V[:, pn, :, :, 0:DH], pV.rearrange("p t (h d) -> p t h d", d=DH)
                                       ).then_inc(s.vc, 1)

                def front(n, pn):
                    turned_x(n)
                    front_early(n)
                    front_middle(n)
                    front_late(n, pn)

                def turn(k, pk, before, now, after):
                    b = k - 1
                    if before:
                        for slot in range(NW):
                            lo = (slot % NT) * P if causal else 0
                            if slot == 1:
                                wait(act, s.added, k)
                            if slot >= 2:
                                act.wait_ge(s.pv, b * NW + slot - 1)
                            for pair in range(2):
                                act.wait_ge(s.ST, b * 2 * NW + 2 * slot + pair + 1)
                                nc.scalar.activation(Pb[:, slot % 2, 2 * pair:2 * pair + 2, lo:S],
                                                     pST[:, pair, :, lo:S], ACT.Exp, scale=float(DH) ** -0.5
                                                     ).then_inc(s.exp, 1)
                    if after:
                        turned_x(k + 1)
                        front_early(k + 1)
                    if now:
                        act.wait_ge(s.mT, k + 1)
                        nc.scalar.copy(mTb[:], pS[0:3 * NH, 0]).then_inc(s.mTc, 1)
                    if after:
                        front_middle(k + 1)
                    if before:
                        act.wait_ge(s.ob, b + 1)
                        nc.scalar.copy(onT, pS[:]).then_inc(s.otc, 1)
                    if after:
                        front_late(k + 1, 1 - pk)
                run(act, front, turn)

            @block.vector
            def _(dve):
                if NLOAD:
                    dve.wait_ge(s.load, 16 * NLOAD)
                dve.wait_ge(s.const, NCONST)
                if self_attn:
                    dve.sem_inc(s.scaled, 1)
                else:
                    if biased:
                        nc.vector.tensor_scalar(bo[:], bo[:], g.tg[:, 0, gate:gate + 1], None, ALU.mult)
                    nc.vector.tensor_scalar(Wo[:], Wo[:], g.tg[:, 0, gate:gate + 1], None, ALU.mult
                                            ).then_inc(s.scaled, 1)
                    dve.wait_ge(s.scaled, 1)

                dve.sem_inc(s.added, 1)
                F = LN_STEPS + 3 + 3 + self_attn
                M = 3
                O = NT + (5 + RSQRT_STEPS if self_attn else 0)

                def norm(n, go):
                    wait(dve, s.xT, n)
                    if self_attn:
                        wait(dve, s.kept, n)
                    dve.sem_inc(s.passed, 1)
                    layernorm(nc, go, w, xn, batch(g.x, n)).then_inc(s.xn, 1)

                def keep_x(n):
                    if self_attn:
                        dve.wait_ge(s.xn, n + 1)
                        nc.vector.tensor_scalar(batch(g.x2, n), xn, 1.0, None, ALU.mult).then_inc(s.kept, 1)

                def split(part, rest, go, done):
                    go(nc.vector.tensor_copy(part[:, 0], rest[:]))
                    go(nc.vector.tensor_tensor(rest[:], rest[:], part[:, 0], ALU.subtract))
                    go(nc.vector.tensor_copy(part[:, 1], rest[:]))
                    nc.vector.tensor_tensor(part[:, 2], rest[:], part[:, 1], ALU.subtract).then_inc(done, 1)

                wide = [P, NC, S]

                def turned_by(f, name, table, ready, done, n):
                    dve.wait_ge(ready, n + 1)
                    nc.vector.tensor_tensor(f[:], half[name], table[:].unsqueeze(1).broadcast_to(wide), ALU.mult
                                            ).then_inc(done, 1)

                def front_q(n):
                    if self_attn:
                        wait(dve, s.kp, n)
                        turned_by(qf, "Q", cos, s.q, s.qm, n)

                def front_q_end(n, go):
                    if self_attn:
                        dve.wait_ge(s.kept, n + 1)
                        turned_by(rope, "Qs", sin, s.qsw, s.qr, n)
                        dve.wait_ge(s.qr, n + 1)
                        go(nc.vector.tensor_tensor(qf[:], qf[:], rope[:], ALU.add))
                    else:
                        dve.wait_ge(s.qf, n + 1)
                    wait(dve, s.kw if self_attn else s.qw, n * 48)
                    split(qp, qf, go, s.qp)

                def front_k(n, go):
                    if self_attn:
                        dve.wait_ge(s.qp, n + 1)
                        turned_by(kf, "K", cos, s.k, s.km, n)
                        turned_by(rope, "Ks", sin, s.ksw, s.kr, n)
                        dve.wait_ge(s.kr, n + 1)
                        nc.vector.tensor_tensor(kf[:], kf[:], rope[:], ALU.add).then_inc(s.kf, 1)
                    dve.wait_ge(s.kf, n + 1)
                    if self_attn:
                        dve.wait_ge(s.qw, n * 48 + 48)
                    else:
                        wait(dve, s.kw, n * 48)
                    split(kp, kf, go, s.kp)

                def front_v(n, pn):
                    if biased:
                        dve.wait_ge(s.v, n + 1)
                        for t in range(NT):
                            last = nc.vector.tensor_tensor(V[:, pn, t, :, 0:DH],
                                                           pV[:, t].rearrange("p (h d) -> p h d", d=DH),
                                                           bv[:].rearrange("p (h d) -> p h d", d=DH), ALU.add)
                        last.then_inc(s.vc, 1)

                def maxima(units, a):
                    for n in units:
                        h, t = divmod(n, NT)
                        dve.wait_ge(s.S, a * NS + n + 1)
                        keys = (t + 1) * P if causal else S
                        nc.vector.tensor_reduce(nm[:, t, h:h + 1], pS[:, n % 2, 0:keys], AX.X, ALU.max,
                                                negate=True).then_inc(s.max, 1)

                def split_maxima(a, go):
                    dve.wait_ge(s.max, a * NS + NS)
                    go(nc.vector.tensor_copy(mm[:, :, 0], nm[:]))
                    go(nc.vector.tensor_tensor(nr[:], nm[:], mm[:, :, 0], ALU.subtract))
                    go(nc.vector.tensor_copy(mm[:, :, 1], nr[:]))
                    nc.vector.tensor_tensor(mm[:, :, 2], nr[:], mm[:, :, 1], ALU.subtract).then_inc(s.mm, 1)

                def group_out(b, h):
                    dve.wait_ge(s.pv, b * NW + (h + 1) * NT)
                    nc.vector.tensor_copy(Osb[:, h], pO[:]).then_inc(s.oev, 1)

                def normalise(b, t, go):
                    dve.wait_ge(s.ot, b * NT + t + 1)
                    o = (pM, pO)[t % 2][:].rearrange("p (h m) -> p h m", m=32)
                    go(nc.vector.reciprocal(rd[:, t, :], o[:, :, DH]))
                    nc.vector.tensor_tensor(On[:, t].rearrange("p (h d) -> p h d", d=DH), o[:, :, 0:DH],
                                            rd[:, t, :].unsqueeze(2).broadcast_to([P, NH, DH]), ALU.mult
                                            ).then_inc(s.nrm, 1)

                def add_output(b, go):
                    dve.wait_ge(s.y, b + 1)
                    x = batch(g.x2 if self_attn else g.x, b)
                    nc.vector.tensor_tensor(x, pY, x, ALU.add).then_inc(s.added, 1)
                    dve.wait_ge(s.added, b + 2)
                    if self_attn:
                        dve.sem_inc(s.passed, 1)
                        rms_rstd(nc, go, w, x)
                        for t in range(NT):
                            last = nc.vector.scalar_tensor_tensor(out=x[:, t, :], in0=x[:, t, :],
                                                                  scalar=w.rstd[:, t:t + 1], in1=normw[:],
                                                                  op0=ALU.mult, op1=ALU.mult)
                        last.then_inc(s.x, 1)
                        dve.wait_ge(s.x, b + 1)
                    if biased:
                        nc.vector.tensor_tensor(x, x, bo[:].unsqueeze(1).broadcast_to([P, NT, D]), ALU.add
                                                ).then_inc(s.x, 1)
                        dve.wait_ge(s.x, b + 1)

                def front(n, pn):
                    go = Steps(dve, s.dve, 0)
                    norm(n, go)
                    keep_x(n)
                    front_q(n)
                    front_q_end(n, go)
                    front_k(n, go)
                    front_v(n, pn)
                    assert go.n == F, go.n

                def turn(k, pk, before, now, after):
                    if isinstance(k, int):
                        base = F * min(k + 1, B) + M * k + O * max(k - 1, 0)
                    else:
                        base = F * (k + 1) + M * k + O * (k - 1)
                    go = Steps(dve, s.dve, base)
                    units_now = max_units if now else (lambda slot: ())
                    for slot in range(MAIN):
                        units = list(units_now(slot))
                        if after and slot == NORM_SLOT:
                            units = [n for later in range(slot, slot + NT) for n in units_now(later)]
                            go.between = lambda: maxima([units.pop(0)] if units else [], k)
                            norm(k + 1, go)
                            go.between = None
                        elif after and NORM_SLOT < slot < NORM_SLOT + NT:
                            units = []
                        maxima(units, k)
                        if before and slot > 0 and slot % NT == 0:
                            group_out(k - 1, slot // NT - 1)
                    if after:
                        keep_x(k + 1)
                    for t in range(NT):
                        if now and t < len(late):
                            maxima(late[t], k)
                        if t == 2:
                            if now:
                                split_maxima(k, go)
                            if after:
                                front_q(k + 1)
                                if not self_attn:
                                    front_q_end(k + 1, go)
                        if before:
                            normalise(k - 1, t, go)
                    if after:
                        if self_attn:
                            front_q_end(k + 1, go)
                        front_k(k + 1, go)
                        front_v(k + 1, 1 - pk)
                    if before:
                        add_output(k - 1, go)
                    assert go.n == F * after + M * now + O * before, go.n
                run(dve, front, turn)


def top_attention(nc, g, sem):
    TOP, ROUND, TAKEN = 32, 8, -3.0e38
    NR = TOP // ROUND
    SCALE = float(D) ** -0.5
    d = {k[9:]: v for k, v in g.dram.items() if k.startswith("L2_xattn_")}
    names = ("load", "bo", "dve", "xn", "kv", "xT", "xTc", "q", "k", "v", "qf", "kf", "vc", "sc", "top", "bias", "exp",
             "read", "p", "pT", "pTc", "o", "oc", "y", "x",
             "passed", "stats")
    Sems = namedtuple("Sems", names)
    s = Sems(*(sem("t2_" + n) for n in names))
    with ExitStack() as ctx:
        sb, ps = allocators(nc, ctx)
        WqT, WkT, WvT, WoT = load_transposed(nc, g, sb, ps, sem, "t2", [d["W" + n] for n in "qkvo"])
        bq, bk = sb("t2_bq", [P, NC]), sb("t2_bk", [P, NC])
        bv, bo = sb("t2_bv", [P, D]), sb("t2_bo", [P, D])
        w = norm_scratch(sb, "t2", B * NT)
        xn, xnT, kvT = sb("t2_xn", [P, NT, D]), sb("t2_xnT", [P, NC, S]), sb("t2_kvT", [P, NC, S])
        qf, kf, V = sb("t2_qf", [P, 2, NC, S]), sb("t2_kf", [P, 2, NC, S]), sb("t2_V", [P, 2, NT, D])
        best, work = sb("t2_best", [P, NR, ROUND]), sb("t2_work", [P, 2, S])
        nb = sb("t2_nb", [P, NT])
        E, Pm = sb("t2_E", [P, 2, S]), sb("t2_Pm", [P, 2, S])
        PT, oT = sb("t2_PT", [P, NT, S]), sb("t2_oT", [P, NC, S])
        rsum, rinv = sb("t2_rsum", [P, NT]), sb("t2_rinv", [P, NT])
        pA, pB = ps("t2_pA", [P, NC, S]), ps("t2_pB", [P, NC, S])
        pS, pT = ps("t2_pS", [P, 2, S]), ps("t2_pT", [P, 2, S])
        pV = pA[:].rearrange("p a n -> p (a n)").rearrange("p (t n) -> p t n", t=NT)
        pY = pB[:].rearrange("p a n -> p (a n)").rearrange("p (t n) -> p t n", t=NT)
        NLOAD = 4

        def wait(eng, semaphore, value):
            if not isinstance(value, int) or value > 0:
                eng.wait_ge(semaphore, value)

        def run(front, turn):
            def loop(eng):
                front()
                turn(0, 0, False, True, True, True)
                with eng.Fori(1, B - 4, 2) as i:
                    turn(i, 1, True, True, True, True)
                    turn(i + 1, 0, True, True, True, True)
                turn(B - 3, 1, True, True, True, True)
                turn(B - 2, 0, True, True, True, False)
                turn(B - 1, 1, True, True, False, False)
                turn(B, 0, True, False, False, False)
            return loop

        with nc.Block() as block:
            @block.sync
            def _(sp):
                for t, n in ((bq, "bq"), (bk, "bk")):
                    sp.dma_start(t[:], d[n].rearrange("(c p) -> p c", p=P),
                                 allow_slow_non_contiguous=True).then_inc(s.load, 16)
                for t, n in ((bv, "bv"), (bo, "bo")):
                    sp.dma_start(t[:], row_of(d[n])).then_inc(s.load, 16)

                def load_ctx(n):
                    wait(sp, s.v, n)
                    sp.sem_inc(s.passed, 1)
                    sp.dma_start(kvT[:], batch_of(g.d_ctxT, n)).then_inc(s.kv, 16)

                def turn(k, pk, before, now, after, later):
                    if after:
                        load_ctx(k + 1)
                run(lambda: load_ctx(0), turn)(sp)

            @block.tensor
            def _(pe):
                def project(out, W, src):
                    for m in range(NC):
                        for c in range(NC):
                            last = nc.tensor.matmul(out[:, m, :], W[:, c, m * P:(m + 1) * P], src[:, c, :],
                                                    start=c == 0, stop=c == NC - 1)
                    return last

                def turn_x(n):
                    pe.wait_ge(s.xn, n + 1)
                    wait(pe, s.oc, n - 1)
                    for c in range(NC):
                        for t in range(NT):
                            last = nc.tensor.transpose(pA[:, c, t * P:(t + 1) * P], xn[:, t, c * P:(c + 1) * P],
                                                       g.ident[:])
                    last.then_inc(s.xT, 1)

                def make_k(n, pn):
                    pe.wait_ge(s.kv, n * 16 + 16)
                    wait(pe, s.x, n - 1)
                    project(pB, WkT, kvT).then_inc(s.k, 1)

                def make_v(n, pn):
                    pe.wait_ge(s.xTc, n + 1)
                    for t in range(NT):
                        for c in range(NC):
                            last = nc.tensor.matmul(pV[:, t, :], kvT[:, c, t * P:(t + 1) * P], WvT[:, c, :],
                                                    start=c == 0, stop=c == NC - 1)
                    last.then_inc(s.v, 1)

                def make_q(n, pn):
                    pe.wait_ge(s.kf, n + 1)
                    project(pB, WqT, xnT).then_inc(s.q, 1)

                def scores(k, pk, t):
                    if t == 0:
                        pe.wait_ge(s.qf, k + 1)
                    wait(pe, s.exp, k * NT + t - 1)
                    wait(pe, s.read, k * NT + t - 1)
                    for c in range(NC):
                        last = nc.tensor.matmul(pS[:, t % 2], qf[:, pk, c, t * P:(t + 1) * P], kf[:, pk, c, :],
                                                start=c == 0, stop=c == NC - 1)
                    last.then_inc(s.sc, 1)

                def turn_probs(k, t):
                    pe.wait_ge(s.p, k * NT + t + 1)
                    wait(pe, s.pTc, k * NT + t - 1)
                    for q in range(NT):
                        last = nc.tensor.transpose(pT[:, t % 2, q * P:(q + 1) * P],
                                                   Pm[:, t % 2, q * P:(q + 1) * P], g.ident[:])
                    last.then_inc(s.pT, 1)

                def output(b, pb):
                    fronts = min(b + 2, B) if isinstance(b, int) else b + 2
                    pe.wait_ge(s.pTc, b * NT + NT)
                    pe.wait_ge(s.vc, fronts)
                    for m in range(NC):
                        for q in range(NT):
                            last = nc.tensor.matmul(pA[:, m, :], V[:, pb, q, m * P:(m + 1) * P], PT[:, q, :],
                                                    start=q == 0, stop=q == NT - 1)
                    last.then_inc(s.o, 1)
                    pe.wait_ge(s.oc, b + 1)
                    pe.wait_ge(s.qf, fronts)
                    for t in range(NT):
                        for c in range(NC):
                            last = nc.tensor.matmul(pY[:, t, :], oT[:, c, t * P:(t + 1) * P], WoT[:, c, :],
                                                    start=c == 0, stop=c == NC - 1)
                    last.then_inc(s.y, 1)

                def front():
                    turn_x(0)
                    for make in (make_k, make_v, make_q):
                        make(0, 0)

                def turn(k, pk, before, now, after, later):
                    if now:
                        scores(k, pk, 0)
                        scores(k, pk, 1)
                    if before:
                        output(k - 1, 1 - pk)
                    if after:
                        turn_x(k + 1)
                    for t in range(NT if now else 0):
                        if after and t > 0:
                            (make_k, make_v, make_q)[t - 1](k + 1, 1 - pk)
                        turn_probs(k, t)
                        if t + 2 < NT:
                            scores(k, pk, t + 2)
                run(front, turn)(pe)

            @block.scalar
            def _(act):
                act.wait_ge(s.load, 16 * NLOAD)
                def turned_x(n):
                    act.wait_ge(s.xT, n + 1)
                    nc.scalar.copy(xnT[:], pA[:]).then_inc(s.xTc, 1)

                def shifted(dst, bias, ready, done, n, pn):
                    act.wait_ge(ready, n + 1)
                    for c in range(NC):
                        last = nc.scalar.activation(dst[:, pn, c], pB[:, c], ACT.Identity, bias=bias[:, c:c + 1])
                    last.then_inc(done, 1)

                def exp(k, t):
                    act.wait_ge(s.bias, k * NT + t + 1)
                    act.wait_ge(s.read, k * NT + t + 1)
                    wait(act, s.p, k * NT + t - 1)
                    nc.scalar.activation(E[:, t % 2], pS[:, t % 2], ACT.Exp, bias=nb[:, t:t + 1], scale=SCALE
                                         ).then_inc(s.exp, 1)

                def turned_probs(k, t):
                    act.wait_ge(s.pT, k * NT + t + 1)
                    nc.scalar.copy(PT[:, :, t * P:(t + 1) * P],
                                   pT[:, t % 2].rearrange("p (k n) -> p k n", k=NT)).then_inc(s.pTc, 1)

                def front():
                    turned_x(0)
                    shifted(kf, bk, s.k, s.kf, 0, 0)
                    shifted(qf, bq, s.q, s.qf, 0, 0)

                def turn(k, pk, before, now, after, later):
                    if now:
                        exp(k, 0)
                    if before:
                        act.wait_ge(s.o, k)
                        nc.scalar.copy(oT[:], pA[:]).then_inc(s.oc, 1)
                    if after:
                        turned_x(k + 1)
                    for t in range(1, NT + 1) if now else ():
                        if t < NT:
                            exp(k, t)
                        if t == NT and after:
                            shifted(qf, bq, s.q, s.qf, k + 1, 1 - pk)
                        turned_probs(k, t - 1)
                        if t == 1 and after:
                            shifted(kf, bk, s.k, s.kf, k + 1, 1 - pk)
                run(front, turn)(act)

            @block.vector
            def _(dve):
                dve.wait_ge(s.load, 16 * NLOAD)
                nc.vector.tensor_scalar(bo[:], bo[:], g.tg[:, 0, 2:3], None, ALU.mult).then_inc(s.bo, 1)
                dve.wait_ge(s.bo, 1)

                def pass_wait():
                    dve.sem_inc(s.passed, 1)
                pre = Steps(dve, s.dve)
                with dve.Fori(0, B) as i:
                    for t in range(NT):
                        last = nc.vector.bn_stats(batch(w.stats, i)[:, t, :], batch(g.x, i)[:, t, :])
                    last.then_inc(s.stats, 1)
                dve.wait_ge(s.stats, B)
                mean_rstd(nc, pre, w)
                K = NT * (2 * NR - 1) + 2

                def norm(n, go):
                    wait(dve, s.xT, n)
                    for t in range(NT):
                        row = bass.ds(n * NT + t, 1)
                        last = nc.vector.tensor_scalar(xn[:, t, :], g.x[:, row, :].rearrange("p o d -> p (o d)"),
                                                       w.mean[:, row], w.rstd[:, row], ALU.subtract, ALU.mult)
                    last.then_inc(s.xn, 1)
                    dve.wait_ge(s.xn, n + 1)
                    x = batch(g.x, n)
                    go(nc.vector.tensor_tensor(x, x, bo[:].unsqueeze(1).broadcast_to([P, NT, D]), ALU.add))

                def shift_v(n, pn):
                    dve.wait_ge(s.v, n + 1)
                    nc.vector.tensor_tensor(V[:, pn], pV, bv[:].unsqueeze(1).broadcast_to([P, NT, D]), ALU.add
                                            ).then_inc(s.vc, 1)

                def choose(k, t, step):
                    dve.wait_ge(s.sc, k * NT + t + 1)
                    wait(dve, s.pT, k * NT + t - 1)
                    pass_wait()
                    src = pS[:, t % 2]
                    for m in range(NR):
                        step(nc.vector.max(best[:, m], src))
                        if m == 0:
                            nc.vector.tensor_scalar(nb[:, t:t + 1], best[:, 0, 0:1], -SCALE, None, ALU.mult
                                                    ).then_inc(s.bias, 1)
                        else:
                            pass_wait()
                        ins = nc.vector.match_replace(work[:, m % 2], best[:, m], src, TAKEN)
                        if m == 0:
                            ins.then_inc(s.read, 1)
                            dve.wait_ge(s.read, k * NT + t + 1)
                        else:
                            step(ins)
                        if m < NR - 1:
                            pass_wait()
                        src = work[:, m % 2]
                    dve.wait_ge(s.exp, k * NT + t + 1)
                    nc.vector.scalar_tensor_tensor(out=Pm[:, t % 2], in0=src, scalar=TAKEN, in1=E[:, t % 2],
                                                   op0=ALU.is_equal, op1=ALU.mult, accum_out=rsum[:, t:t + 1]
                                                   ).then_inc(s.p, 1)

                def add_output(b):
                    dve.wait_ge(s.y, b + 1)
                    x = batch(g.x, b)
                    for t in range(NT):
                        last = nc.vector.scalar_tensor_tensor(out=x[:, t, :], in0=pY[:, t, :], scalar=rinv[:, t:t + 1],
                                                              in1=x[:, t, :], op0=ALU.mult, op1=ALU.add)
                    last.then_inc(s.x, 1)
                    dve.wait_ge(s.x, b + 1)

                def front():
                    norm(0, pre)
                    shift_v(0, 0)
                    norm(1, pre)

                def turn(k, pk, before, now, after, later):
                    step = Steps(dve, s.dve, pre.n + K * k + (min(k, B - 2) if isinstance(k, int) else k))
                    for t in range(NT):
                        if now:
                            choose(k, t, step)
                        if before and t == 1:
                            add_output(k - 1)
                        if after and t == 2:
                            shift_v(k + 1, 1 - pk)
                    if now:
                        dve.wait_ge(s.p, k * NT + NT)
                        step(nc.vector.reciprocal(rinv[:], rsum[:]))
                        step(nc.vector.tensor_scalar(rinv[:], rinv[:], g.tg[:, 0, 2:3], None, ALU.mult))
                    if later:
                        norm(k + 2, step)
                    assert step.n == K * now + later, step.n
                run(front, turn)(dve)


def top_k(nc, step, k, prob, best, work, out):
    for t in range(prob.shape[1]):
        last = nc.vector.max(best[:, t, :], prob[:, t, :])
    step(last)
    step(nc.vector.tensor_scalar(best[:, :, k:8], best[:, :, k:8], 0.0, -2.0, ALU.mult, ALU.add))
    for t in range(prob.shape[1]):
        last = nc.vector.match_replace(work[:, t, :], best[:, t, :], prob[:, t, :], -1.0)
    step(last)
    step(nc.vector.scalar_tensor_tensor(out=out, in0=work, scalar=0.0, in1=prob, op0=ALU.is_lt, op1=ALU.mult))


def routing(nc, g, sem, r):
    tag, E, EL = r.tag, r.E, r.EL
    names = ("load", "const", "dve", "stats", "xn", "xT", "xTc", "logit", "ein", "exp", "w", "tp", "tpc", "tb", "sel",
             "mask", "pos", "slot", "Lc")
    Sems = namedtuple("Sems", names)
    s = Sems(*(sem(f"{tag}r_{n}") for n in names))
    TT = B * NT
    by_choice = r.kind == "expert_choice"
    copies = 1 if by_choice else 2
    with ExitStack() as ctx:
        sb, ps = allocators(nc, ctx)
        w = r.norm if by_choice else norm_scratch(sb, tag + "r", TT)
        xn, xnT = sb(tag + "r_xn", [P, 2, NT, D]), sb(tag + "r_xnT", [P, 2, NC, S])
        Wr = sb(tag + "r_Wr", [P, NC, EL])
        L = sb(tag + "r_L", [P, TT, EL])
        pr = sb(tag + "r_pr", [P, TT, E])
        a, b, c2 = (sb(f"{tag}r_{n}", [P, TT, 4]) for n in "abc")
        bias = sb(tag + "r_bias", [P, EL])
        if by_choice:
            R = B * E
            pt, work, best = sb(tag + "r_pt", [R, S]), sb(tag + "r_work", [R, S]), sb(tag + "r_best", [R, 8])
            chosen = sb(tag + "r_chosen", [R, S])
            mask, upto = sb(tag + "r_mask", [P, NT, R]), sb(tag + "r_upto", [P, P])
        else:
            best, work = sb(tag + "r_best", [P, TT, 8]), sb(tag + "r_work", [P, TT, E])
        pT, pL, pX = ps(tag + "r_pT", [P, 2, NC, S]), ps(tag + "r_pL", [P, 2, 512]), ps(tag + "r_pX", [P, S])
        NLOAD = len(r.router) + (2 if r.kind == "grouped" else 0)
        tgate = g.tg[:, 1, r.gate:r.gate + 1]
        with nc.Block() as block:
            @block.sync
            def _(sp):
                for dst, src in r.router:
                    sp.dma_start(Wr[:, :, dst], src, allow_slow_non_contiguous=True).then_inc(s.load, 16)
                if r.kind == "grouped":
                    sp.dma_start(bias[:, 0:2], r.biases[0].rearrange("(o n) -> o n", o=1).broadcast_to([P, 2])
                                 ).then_inc(s.load, 16)
                    sp.dma_start(bias[:, 2:10], r.biases[1].rearrange("(o n) -> o n", o=1).broadcast_to([P, 8])
                                 ).then_inc(s.load, 16)
                for dst, src in r.loads:
                    sp.dma_start(dst, src).then_inc(r.s_weights, 16)

            if by_choice:
                @block.gpsimd
                def _(pool):
                    nc.gpsimd.memset(upto[:], 0.0).then_inc(s.const, 1)
                    pool.wait_ge(s.const, 1)
                    nc.gpsimd.affine_select(out=upto[:], in_=upto[:], compare_op=ALU.is_gt, fill=1.0, base=0,
                                            pattern=[[-1, P]], channel_multiplier=1).then_inc(s.const, 1)

            @block.tensor
            def _(pe):
                pe.wait_ge(s.load, 16 * NLOAD)
                pe.sem_inc(s.xT, 2)

                def turn_x(j, u):
                    pe.wait_ge(s.xn, j + 1)
                    pe.wait_ge(s.xTc, copies * (j + 1))
                    for c in range(NC):
                        for t in range(NT):
                            last = nc.tensor.transpose(pT[:, u, c, t * P:(t + 1) * P],
                                                       xn[:, u, t, c * P:(c + 1) * P], g.ident[:])
                    last.then_inc(s.xT, 1)

                def logits(j, u):
                    pe.wait_ge(s.xTc, copies * (j + 2) + 1)
                    pe.wait_ge(s.Lc, j + 1)
                    for t in range(NT):
                        for c in range(NC):
                            last = nc.tensor.matmul(pL[:, u, t * EL:(t + 1) * EL],
                                                    xnT[:, u, c, t * P:(t + 1) * P], Wr[:, c, :],
                                                    start=c == 0, stop=c == NC - 1)
                    last.then_inc(s.logit, 1)

                turn_x(0, 0)
                with pe.Fori(0, B - 3, 2) as i:
                    for u in range(2):
                        turn_x(i + u + 1, 1 - u)
                        logits(i + u, u)
                turn_x(B - 1, 1)
                for u in range(2):
                    logits(B - 2 + u, u)
                if r.kind == "expert_choice":
                    pe.wait_ge(s.w, 1)
                    for t in range(NT):
                        last = nc.tensor.transpose(pX[0:R, t * P:(t + 1) * P], r.weights[:, t, :], g.ident[:])
                    last.then_inc(s.tp, 1)
                    pe.wait_ge(s.sel, 1)
                    for t in range(NT):
                        last = nc.tensor.transpose(pX[:, t * R:(t + 1) * R], chosen[:, t * P:(t + 1) * P],
                                                   g.ident[0:R, 0:R])
                    last.then_inc(s.tb, 1)
                    pe.wait_ge(s.mask, 1)
                    pe.wait_ge(s.const, 2)
                    for t in range(NT):
                        for q in range(t + 1):
                            last = nc.tensor.matmul(pX[:, t * R:(t + 1) * R], (upto if q == t else g.ones)[:],
                                                    mask[:, q, :], start=q == 0, stop=q == t)
                    last.then_inc(s.pos, 1)
                    pe.wait_ge(s.slot, 1)
                    nc.tensor.matmul(pX[:, 0:P], g.ones[:], upto[:], start=True, stop=True).then_inc(s.pos, 1)

            @block.scalar
            def _(act):
                act.sem_inc(s.xTc, 2 * copies)
                act.sem_inc(s.Lc, 2)
                act.sem_inc(s.logit, 2)

                def copy_x(j, u):
                    act.wait_ge(s.xT, j + 3)
                    act.wait_ge(s.logit, j + 1)
                    nc.scalar.copy(xnT[:, u], pT[:, u]).then_inc(s.xTc, 1)
                    if copies > 1:
                        nc.scalar.copy(g.xT[:, :, bass.ds(j * S, S)], pT[:, u]).then_inc(s.xTc, 1)

                def copy_logits(j, u):
                    act.wait_ge(s.logit, j + 3)
                    nc.scalar.copy(batch(L, j), pL[:, u, 0:NT * EL].rearrange("p (t e) -> p t e", t=NT)
                                   ).then_inc(s.Lc, 1)

                copy_x(0, 0)
                with act.Fori(0, B - 3, 2) as i:
                    for u in range(2):
                        copy_x(i + u + 1, 1 - u)
                        copy_logits(i + u, u)
                copy_x(B - 1, 1)
                for u in range(2):
                    copy_logits(B - 2 + u, u)
                act.wait_ge(s.ein, 1)
                nc.scalar.activation(L[:], L[:], ACT.Exp).then_inc(s.exp, 1)

            @block.vector
            def _(dve):
                dve.wait_ge(s.load, 16 * NLOAD)
                step = Steps(dve, s.dve)

                def wide(x, n=E):
                    return x.unsqueeze(2).broadcast_to([P, TT, n])
                if r.kind != "grouped":
                    with dve.Fori(0, B) as i:
                        for t in range(NT):
                            last = nc.vector.bn_stats(batch(w.stats, i)[:, t, :], batch(g.x, i)[:, t, :])
                        last.then_inc(s.stats, 1)
                    dve.wait_ge(s.stats, B)
                    mean_rstd(nc, step, w)
                with dve.Fori(0, B - 1, 2) as i:
                    for u in range(2):
                        j = i + u
                        dve.wait_ge(s.xT, j + 1)
                        if r.kind == "grouped":
                            nc.vector.tensor_scalar(xn[:, u], batch(g.x2, j), 1.0, None, ALU.mult).then_inc(s.xn, 1)
                            continue
                        for t in range(NT):
                            row = bass.ds(j * NT + t, 1)
                            last = nc.vector.tensor_scalar(xn[:, u, t, :], g.x[:, row, :].rearrange("p o d -> p (o d)"),
                                                           w.mean[:, row], w.rstd[:, row], ALU.subtract, ALU.mult)
                        last.then_inc(s.xn, 1)
                dve.wait_ge(s.Lc, B + 2)
                if r.kind == "grouped":
                    eight = [P, TT, 2, 4]
                    Lg, Le = L[:, :, 0:2], L[:, :, 2:10].rearrange("p t (g e) -> p t g e", g=2)
                    step(nc.vector.tensor_tensor(L[:], L[:], bias[:].unsqueeze(1).broadcast_to([P, TT, EL]), ALU.add))
                    nc.vector.tensor_reduce(a[:, :, 0:1], Lg, AX.X, ALU.max)
                    step(nc.vector.tensor_reduce(b[:, :, 0:2], Le, AX.X, ALU.max))
                    nc.vector.tensor_tensor(Lg, Lg, a[:, :, 0:1].broadcast_to([P, TT, 2]), ALU.subtract)
                    nc.vector.tensor_tensor(Le, Le, b[:, :, 0:2].unsqueeze(3).broadcast_to(eight), ALU.subtract
                                            ).then_inc(s.ein, 1)
                    dve.wait_ge(s.exp, 1)
                    nc.vector.tensor_reduce(a[:, :, 0:1], Lg, AX.X, ALU.add)
                    step(nc.vector.tensor_reduce(a[:, :, 1:3], Le, AX.X, ALU.add))
                    step(nc.vector.reciprocal(b[:, :, 0:3], a[:, :, 0:3]))
                    step(nc.vector.tensor_tensor(Lg, Lg, b[:, :, 0:1].broadcast_to([P, TT, 2]), ALU.mult))
                    nc.vector.tensor_tensor(c2[:, :, 0:1], Lg[:, :, 0:1], Lg[:, :, 1:2], ALU.is_ge)
                    step(nc.vector.tensor_tensor(c2[:, :, 1:2], Lg[:, :, 0:1], Lg[:, :, 1:2], ALU.is_lt))
                    step(nc.vector.tensor_tensor(c2[:, :, 0:2], c2[:, :, 0:2], Lg, ALU.mult))
                    step(nc.vector.tensor_tensor(c2[:, :, 0:2], c2[:, :, 0:2], b[:, :, 1:3], ALU.mult))
                    step(nc.vector.tensor_tensor(pr[:].rearrange("p t (g e) -> p t g e", g=2), Le,
                                                 c2[:, :, 0:2].unsqueeze(3).broadcast_to(eight), ALU.mult))
                else:
                    step(nc.vector.tensor_reduce(a[:, :, 0:1], L[:, :, 0:E], AX.X, ALU.max))
                    if r.shared_gate:
                        nc.vector.tensor_scalar(L[:, :, E:E + 1], L[:, :, E:E + 1], -1.0, None, ALU.mult)
                    nc.vector.tensor_tensor(L[:, :, 0:E], L[:, :, 0:E], wide(a[:, :, 0]), ALU.subtract
                                            ).then_inc(s.ein, 1)
                    dve.wait_ge(s.exp, 1)
                    step(nc.vector.tensor_reduce(a[:, :, 0:1], L[:, :, 0:E], AX.X, ALU.add))
                    step(nc.vector.reciprocal(b[:, :, 0:1], a[:, :, 0:1]))
                    step(nc.vector.tensor_tensor(pr[:], L[:, :, 0:E], wide(b[:, :, 0]), ALU.mult))
                weights = r.weights[:].rearrange("p t (b w) -> p b t w", b=B)

                def by_batch(x):
                    return x.rearrange("p (b t) e -> p b t e", b=B)
                if r.kind == "expert_choice":
                    nc.vector.tensor_scalar(weights, by_batch(pr[:]), 1.0, None, ALU.mult).then_inc(s.w, 1)
                else:
                    top_k(nc, step, r.k, pr[:], best[:], work[:], pr[:])
                    if r.renorm:
                        step(nc.vector.tensor_reduce(a[:, :, 0:1], pr[:], AX.X, ALU.add))
                        step(nc.vector.reciprocal(b[:, :, 0:1], a[:, :, 0:1]))
                        step(nc.vector.tensor_tensor(pr[:], pr[:], wide(b[:, :, 0]), ALU.mult))
                    if r.shared_gate:
                        step(nc.vector.tensor_scalar(a[:, :, 0:1], L[:, :, E:E + 1], 1.0, None, ALU.add))
                        step(nc.vector.reciprocal(b[:, :, 0:1], a[:, :, 0:1]))
                        nc.vector.tensor_scalar(weights[:, :, :, E:E + 1], by_batch(b[:, :, 0:1]), tgate, None, ALU.mult)
                    nc.vector.tensor_scalar(weights[:, :, :, 0:E], by_batch(pr[:]),
                                            1.0 if r.kind == "grouped" else tgate, None, ALU.mult).then_inc(s.w, 1)
                dve.wait_ge(s.w, 1)
                if r.kind == "expert_choice":
                    dve.wait_ge(s.tp, 1)
                    nc.vector.tensor_copy(work[:], pX[0:R, :]).then_inc(s.tpc, 1)
                    nc.vector.tensor_copy(pt[:], pX[0:R, :]).then_inc(s.tpc, 1)
                    dve.wait_ge(s.tpc, 2)
                    for n in range(r.capacity // 8):
                        nc.vector.max(best[:], work[:]).then_inc(s.tpc, 1)
                        dve.wait_ge(s.tpc, 2 * n + 3)
                        nc.vector.match_replace(work[:], best[:], work[:], -1.0).then_inc(s.tpc, 1)
                        dve.wait_ge(s.tpc, 2 * n + 4)
                    nc.vector.scalar_tensor_tensor(out=chosen[:], in0=work[:], scalar=0.0, in1=pt[:],
                                                   op0=ALU.is_lt, op1=ALU.mult).then_inc(s.sel, 1)
                    dve.wait_ge(s.tb, 1)
                    by_tile = pX[:, 0:NT * R].rearrange("p (t r) -> p t r", t=NT)
                    nc.vector.tensor_scalar(r.weights[:], by_tile, tgate, None, ALU.mult)
                    nc.vector.tensor_scalar(mask[:], by_tile, 0.0, None, ALU.is_gt).then_inc(s.mask, 1)
                    dve.wait_ge(s.mask, 1)
                    dve.wait_ge(s.pos, 1)
                    nc.vector.tensor_tensor(r.slot[:], by_tile, mask[:], ALU.mult).then_inc(s.slot, 1)
                    dve.wait_ge(s.pos, 2)
                    nc.vector.tensor_copy(r.iota[:], pX[:, 0:P]).then_inc(s.slot, 1)
                    dve.wait_ge(s.slot, 2)


def experts(nc, g, sem, r):
    tag = r.tag
    names = ("H", "sg", "ha", "hm", "Y", "acc", "fin", "dve", "x")
    Sems = namedtuple("Sems", names)
    s = Sems(*(sem(f"{tag}e_{n}") for n in names))
    units, outs = [], []
    for j, job in enumerate(r.jobs):
        for q in range(job.nf if job.glu else job.nf // 2):
            units.append((j, q))
        outs += [(j, n) for n in range(len(job.outs))]
    NU, NY = len(units), len(outs)
    glu = [r.jobs[j].glu for j, _ in units]
    NG, NA = sum(glu), NU - sum(glu)
    assert NU % 2 == 0
    FMAX = max(job.nf for job in r.jobs)
    with ExitStack() as ctx:
        sb, ps = allocators(nc, ctx)
        hT = sb(tag + "e_hT", [P, 2, FMAX, S])
        sg = sb(tag + "e_sg", [P, 2, S])
        acc = sb(tag + "e_acc", [P, NT, D])
        wf = sb(tag + "e_wf", [P, NT, r.EW])
        if r.final_norm is not None:
            nw, w = sb(tag + "e_nw", [P, D]), norm_scratch(sb, tag + "e")
        pH, pY = ps(tag + "e_pH", [P, 2, 2, S]), ps(tag + "e_pY", [P, 2, NT, D])

        def consumed(eng, u, i):
            ahead = 1 if u >= 0 else 0
            u %= NU
            if glu[u]:
                eng.wait_ge(s.hm, (i + ahead) * NG + sum(glu[:u + 1]))
            else:
                eng.wait_ge(s.ha, (i + ahead) * NA + u + 1 - sum(glu[:u + 1]))

        def hidden_free(eng, j, i):
            ahead = 1 if j >= 2 else 0
            before = j - 2 if j >= 2 else max(k for k in range(len(r.jobs)) if k % 2 == j % 2)
            eng.wait_ge(s.Y, (i + ahead) * NY + r.jobs[before].out0 + len(r.jobs[before].outs))

        def out_free(eng, y, i):
            ahead = 1 if y >= 2 else 0
            before = y - 2 if y >= 2 else max(k for k in range(NY) if k % 2 == y % 2)
            eng.wait_ge(s.acc, (i + ahead) * NY + before + 1)

        with nc.Block() as block:
            if r.final_norm is not None:
                @block.sync
                def _(sp):
                    sp.dma_start(nw[:], r.final_norm.rearrange("(o n) -> o n", o=1).broadcast_to([P, D])
                                 ).then_inc(s.fin, 16)

            @block.tensor
            def _(pe):
                pe.wait_ge(r.s_weights, 16 * len(r.loads))
                pe.sem_inc(s.Y, NY)
                with pe.Fori(0, B) as i:
                    def rhs(c):
                        return g.xT[:, c, bass.ds(i * S, S)]

                    def outputs(j):
                        job = r.jobs[j]
                        consumed(pe, job.last, i)
                        for n, (w2, _) in enumerate(job.outs):
                            y = job.out0 + n
                            out_free(pe, y, i)
                            for t in range(NT):
                                for f in range(job.nf):
                                    last = nc.tensor.matmul(pY[:, y % 2, t, :], hT[:, j % 2, f, t * P:(t + 1) * P],
                                                            w2(f), start=f == 0, stop=f == job.nf - 1)
                            last.then_inc(s.Y, 1)
                    for j, job in enumerate(r.jobs):
                        for u in range(job.first, job.last + 1):
                            q = u - job.first
                            consumed(pe, u - 2, i)
                            for k in range(2):
                                for c in range(NC):
                                    w1 = job.win(k, q, c) if job.glu else job.win(0, 2 * q + k, c)
                                    last = nc.tensor.matmul(pH[:, u % 2, k], w1, rhs(c),
                                                            start=c == 0, stop=c == NC - 1)
                            last.then_inc(s.H, 1)
                        if j >= 1:
                            outputs(j - 1)
                    outputs(len(r.jobs) - 1)

            @block.scalar
            def _(act):
                if NA:
                    act.sem_inc(s.ha, NA)
                with act.Fori(0, B) as i:
                    for u, (j, q) in enumerate(units):
                        if not glu[u] and q == 0:
                            hidden_free(act, j, i)
                        act.wait_ge(s.H, i * NU + u + 1)
                        if glu[u]:
                            nc.scalar.activation(sg[:, u % 2], pH[:, u % 2, 0], ACT.Silu).then_inc(s.sg, 1)
                        else:
                            nc.scalar.activation(hT[:, j % 2, 2 * q:2 * q + 2], pH[:, u % 2], ACT.Silu
                                                 ).then_inc(s.ha, 1)

            @block.vector
            def _(dve):
                if NG:
                    dve.sem_inc(s.hm, NG)
                dve.sem_inc(s.acc, NY)
                if r.final_norm is not None:
                    dve.wait_ge(s.fin, 16)
                NX = 3

                def begin(i):
                    nc.vector.tensor_scalar(acc[:], batch(g.x if r.final_norm is None else g.x2, i), 1.0, None, ALU.mult
                                            ).then_inc(s.x, 1)
                    nc.vector.tensor_scalar(wf[:], r.weights[:, :, bass.ds(i * r.EW, r.EW)], 1.0, None, ALU.mult
                                            ).then_inc(s.x, 1)
                    dve.wait_ge(s.x, i * NX + 2)

                K = 5 + RSQRT_STEPS + 1

                def mean_square(i):
                    dve.wait_ge(s.acc, (i + 2) * NY)
                    step = Steps(dve, s.dve, i * K)
                    rms_rstd(nc, step, w, acc)
                    assert step.n == K - 1, step.n

                def end(i):
                    x = batch(g.x, i)
                    dve.wait_ge(s.acc, (i + 2) * NY)
                    if r.final_norm is not None:
                        step = Steps(dve, s.dve, i * K + K - 1)
                        for t in range(NT):
                            last = nc.vector.scalar_tensor_tensor(out=acc[:, t, :], in0=acc[:, t, :],
                                                                  scalar=w.rstd[:, t:t + 1], in1=nw[:],
                                                                  op0=ALU.mult, op1=ALU.mult)
                        step(last)
                        nc.vector.scalar_tensor_tensor(out=x, in0=acc[:], scalar=g.tg[:, 1, r.gate:r.gate + 1],
                                                       in1=x, op0=ALU.mult, op1=ALU.add).then_inc(s.x, 1)
                    else:
                        nc.vector.tensor_scalar(x, acc[:], 1.0, None, ALU.mult).then_inc(s.x, 1)
                    dve.wait_ge(s.x, i * NX + 3)

                def add(i, j):
                    for n, (_, col) in enumerate(r.jobs[j].outs):
                        y = r.jobs[j].out0 + n
                        dve.wait_ge(s.Y, (i + 1) * NY + y + 1)
                        if y >= 1:
                            dve.wait_ge(s.acc, (i + 1) * NY + y)
                        for t in range(NT):
                            scale = 1.0 if col is None else wf[:, t, col:col + 1]
                            last = nc.vector.scalar_tensor_tensor(out=acc[:, t, :], in0=pY[:, y % 2, t, :],
                                                                  scalar=scale, in1=acc[:, t, :],
                                                                  op0=ALU.mult, op1=ALU.add)
                        last.then_inc(s.acc, 1)

                def one_batch(i, before):
                    for j, job in enumerate(r.jobs):
                        for u in range(job.first, job.last + 1):
                            if glu[u]:
                                if u == job.first:
                                    hidden_free(dve, j, i)
                                dve.wait_ge(s.sg, i * NG + sum(glu[:u + 1]))
                                nc.vector.tensor_tensor(hT[:, j % 2, u - job.first], pH[:, u % 2, 1], sg[:, u % 2],
                                                        ALU.mult).then_inc(s.hm, 1)
                            if u == 1 and before and r.final_norm is not None:
                                mean_square(i - 1)
                            if u == (1 if r.final_norm is None else 3):
                                if before:
                                    end(i - 1)
                                begin(i)
                        if j >= 1:
                            add(i, j - 1)
                    add(i, len(r.jobs) - 1)

                one_batch(0, False)
                with dve.Fori(1, B) as i:
                    one_batch(i, True)
                if r.final_norm is not None:
                    mean_square(B - 1)
                end(B - 1)


def choosing_experts(nc, g, sem, r):
    tag, E, F = r.tag, r.E, r.W2.shape[2]
    GB = 4
    assert r.capacity == P and GB * P == S
    names = ("xn", "wf", "sel", "selb", "G", "xg", "H", "h", "T", "selT", "Y", "y", "O", "x")
    Sems = namedtuple("Sems", names)
    s = Sems(*(sem(f"{tag}e_{n}") for n in names))
    NO, NH2 = E * GB, E * (F // 2)
    with ExitStack() as ctx:
        sb, ps = allocators(nc, ctx)
        xn = sb(tag + "e_xn", [P, GB, NT, D])
        wf, slot = sb(tag + "e_wf", [P, NT, GB, E]), sb(tag + "e_slot", [P, NT, GB, E])
        sel, selb = sb(tag + "e_sel", [P, 3, GB, NT, P]), sb(tag + "e_selb", [P, 3, GB, NT, P], BF16)
        xg, hT = sb(tag + "e_xg", [P, NC, S]), sb(tag + "e_hT", [P, F, S])
        selT, Ysb = sb(tag + "e_selT", [P, 2, S]), sb(tag + "e_Y", [P, 2, D])
        pG, pH = ps(tag + "e_pG", [P, NC, S]), ps(tag + "e_pH", [P, 2, S])
        pY, pT, pO = ps(tag + "e_pY", [P, 512]), ps(tag + "e_pT", [P, S]), ps(tag + "e_pO", [P, NT, D])
        with nc.Block() as block:
            @block.tensor
            def _(pe):
                pe.wait_ge(r.s_weights, 16 * len(r.loads))
                with pe.Fori(0, B // GB) as i:
                    def gather(e, batches):
                        for b in batches:
                            for c in range(NC):
                                for t in range(NT):
                                    last = nc.tensor.matmul(pG[:, c, b * P:(b + 1) * P],
                                                            xn[:, b, t, c * P:(c + 1) * P], sel[:, e % 3, b, t, :],
                                                            start=t == 0, stop=t == NT - 1)
                        return last

                    def hidden(e, k):
                        for f in range(2):
                            for c in range(NC):
                                q = 2 * k + f
                                last = nc.tensor.matmul(pH[:, f], r.W1[:, e, c, q * P:(q + 1) * P], xg[:, c],
                                                        start=c == 0, stop=c == NC - 1)
                        last.then_inc(s.H, 1)

                    def turn_sel(e, b):
                        pe.wait_ge(s.selT, i * NO + e * GB + b + 1)
                        pe.wait_ge(s.selb, i * E + e + 1)
                        for t in range(NT):
                            last = nc.tensor.matmul(pT[:, t * P:(t + 1) * P], selb[:, e % 3, b, t, :], g.identb[:],
                                                    start=True, stop=True)
                        last.then_inc(s.T, 1)

                    def outputs(e, b):
                        pe.wait_ge(s.y, i * NO + e * GB + b + 1)
                        for f in range(F):
                            last = nc.tensor.matmul(pY[:, 0:D], hT[:, f, b * P:(b + 1) * P], r.W2[:, e, f],
                                                    start=f == 0, stop=f == F - 1)
                        last.then_inc(s.Y, 1)

                    def put_back(e, b):
                        n = e * GB + b
                        pe.wait_ge(s.selT, i * NO + n + 2)
                        pe.wait_ge(s.y, i * NO + n + 2)
                        pe.wait_ge(s.x, i * NO + n + 1)
                        for t in range(NT):
                            last = nc.tensor.matmul(pO[:, t], selT[:, n % 2, t * P:(t + 1) * P], Ysb[:, n % 2],
                                                    start=True, stop=True)
                        last.then_inc(s.O, 1)

                    pe.wait_ge(s.xn, i + 1)
                    pe.wait_ge(s.sel, i * E + 1)
                    gather(0, range(GB)).then_inc(s.G, 1)
                    for e in range(E):
                        pe.wait_ge(s.xg, i * E + e + 1)
                        pe.wait_ge(s.h, i * NH2 + (F // 2) * e + 1)
                        hidden(e, 0)
                        turn_sel(e, 0)
                        for k in range(1, F // 2):
                            if e + 1 < E:
                                pe.wait_ge(s.sel, i * E + e + 2)
                                gather(e + 1, range(GB // 2))
                            pe.wait_ge(s.h, i * NH2 + (F // 2) * e + k + 1)
                            hidden(e, k)
                            if e + 1 < E:
                                gather(e + 1, range(GB // 2, GB)).then_inc(s.G, 1)
                        pe.wait_ge(s.h, i * NH2 + (F // 2) * (e + 1) + 1)
                        for b in range(GB):
                            outputs(e, b)
                            if b + 1 < GB:
                                turn_sel(e, b + 1)
                            put_back(e, b)

            @block.scalar
            def _(act):
                act.sem_inc(s.h, 1)
                act.sem_inc(s.selT, 1)
                act.sem_inc(s.y, 1)
                with act.Fori(0, B // GB) as i:
                    def gathered(e):
                        act.wait_ge(s.G, i * E + e + 1)
                        nc.scalar.copy(xg[:], pG[:]).then_inc(s.xg, 1)

                    def turned(e, b):
                        n = e * GB + b
                        act.wait_ge(s.T, i * NO + n + 1)
                        nc.scalar.copy(selT[:, n % 2], pT[:]).then_inc(s.selT, 1)

                    gathered(0)
                    for e in range(E):
                        for k in range(F // 2):
                            act.wait_ge(s.H, i * NH2 + e * (F // 2) + k + 1)
                            nc.scalar.activation(hT[:, 2 * k:2 * k + 2], pH[:], ACT.Silu).then_inc(s.h, 1)
                            if k == 0:
                                turned(e, 0)
                        if e + 1 < E:
                            gathered(e + 1)
                        for b in range(GB):
                            n = e * GB + b
                            act.wait_ge(s.Y, i * NO + n + 1)
                            nc.scalar.copy(Ysb[:, n % 2], pY[:, 0:D]).then_inc(s.y, 1)
                            if b + 1 < GB:
                                turned(e, b + 1)

            @block.vector
            def _(dve):
                dve.sem_inc(s.x, 1)
                with dve.Fori(0, B // GB) as i:
                    def select(e):
                        for b in range(GB):
                            for t in range(NT):
                                last = nc.vector.tensor_scalar(sel[:, e % 3, b, t, :], r.iota[:],
                                                               slot[:, t, b, e:e + 1], None, ALU.is_equal)
                        last.then_inc(s.sel, 1)
                        dve.wait_ge(s.sel, i * E + e + 1)
                        nc.vector.tensor_copy(selb[:, e % 3], sel[:, e % 3]).then_inc(s.selb, 1)

                    dve.wait_ge(s.x, i * NO + 1)
                    for b in range(GB):
                        for t in range(NT):
                            row = bass.ds(i * (GB * NT) + b * NT + t, 1)
                            last = nc.vector.tensor_scalar(xn[:, b, t, :], g.x[:, row, :].rearrange("p o d -> p (o d)"),
                                                           r.norm.mean[:, row], r.norm.rstd[:, row],
                                                           ALU.subtract, ALU.mult)
                    last.then_inc(s.xn, 1)
                    own = bass.ds(i * (GB * E), GB * E)
                    for dst, src in ((wf, r.weights), (slot, r.slot)):
                        nc.vector.tensor_scalar(dst[:].rearrange("p t b e -> p t (b e)"), src[:, :, own], 1.0, None,
                                                ALU.mult).then_inc(s.wf, 1)
                    dve.wait_ge(s.wf, 2 * i + 2)
                    select(0)
                    select(1)
                    for e in range(E):
                        if e + 2 < E:
                            if e >= 1:
                                dve.wait_ge(s.T, i * NO + e * GB)
                            select(e + 2)
                        for b in range(GB):
                            n = e * GB + b
                            dve.wait_ge(s.O, i * NO + n + 1)
                            if e >= 1:
                                dve.wait_ge(s.x, i * NO + n + 2 - GB)
                            x = batch(g.x, i * GB + b)
                            for t in range(NT):
                                last = nc.vector.scalar_tensor_tensor(out=x[:, t, :], in0=pO[:, t, :],
                                                                      scalar=wf[:, t, b, e:e + 1], in1=x[:, t, :],
                                                                      op0=ALU.mult, op1=ALU.add)
                            last.then_inc(s.x, 1)
                dve.wait_ge(s.x, 1 + NO * (B // GB))


def moe_layer(nc, g, sem, layer):
    with ExitStack() as ctx:
        sb, _ = allocators(nc, ctx)
        tag = f"m{layer}"
        d = {k[len(f"L{layer}_ffn_"):]: v for k, v in g.dram.items() if k.startswith(f"L{layer}_ffn_")}
        r = Shared()
        r.tag, r.gate, r.shared_gate, r.renorm, r.final_norm, r.biases = tag, layer, False, False, None, None
        r.s_weights, r.loads, r.jobs = sem(tag + "_weights"), [], []
        if layer != 1:
            g.xT = sb(tag + "_xT", [P, NC, B * S])

        def job(glu, nf, win, outs):
            first = r.jobs[-1].last + 1 if r.jobs else 0
            out0 = r.jobs[-1].out0 + len(r.jobs[-1].outs) if r.jobs else 0
            r.jobs.append(Job(glu, nf, win, outs, first, first + (nf if glu else nf // 2) - 1, out0))

        def chunk(w, off=0):
            return lambda k, f, c: w[:, c, off + f * P:off + (f + 1) * P]
        if layer == 0:
            E, F = d["W2_experts"].shape[0], d["W2_experts"].shape[1]
            r.kind, r.E, r.EL, r.EW, r.k = "grouped", E, E + 2, E, 2
            r.router = [(slice(0, 2), by_rows(d["Wg_gate"])), (slice(2, 10), by_rows(d["We_gate"]))]
            r.biases = (d["group_bias"], d["expert_bias"])
            r.final_norm = d["norm2_w"]
            Wsi, Wso = sb(tag + "_Wsi", [P, NC, 2 * F]), sb(tag + "_Wso", [P, F // P, D])
            W1, W2 = sb(tag + "_W1", [P, NC, 2 * F]), sb(tag + "_W2", [P, E, F // P, D])
            r.loads = [(Wsi[:], by_rows(d["W_shared_in"])), (Wso[:], by_rows(d["W_shared_out"])),
                       (W1[:], by_rows(d["W1_shared"]))]
            r.loads += [(W2[:, e], by_rows(d["W2_experts"][e])) for e in range(E)]
            job(True, F // P, lambda k, f, c: Wsi[:, c, k * F + f * P:k * F + (f + 1) * P],
                [(lambda f: Wso[:, f, :], None)])
            job(True, F // P, lambda k, f, c: W1[:, c, k * F + f * P:k * F + (f + 1) * P],
                [((lambda f, e=e: W2[:, e, f, :]), e) for e in range(E)])
        elif layer == 1:
            E, _, F = d["w1"].shape
            r.kind, r.E, r.EL, r.EW = "expert_choice", E, E, E
            r.capacity = S * 2 // E
            r.router = [(e, d["choice_w"][e].rearrange("(c p) -> p c", p=P)) for e in range(E)]
            r.W1, r.W2 = sb(tag + "_W1", [P, E, NC, F]), sb(tag + "_W2", [P, E, F // P, D])
            r.loads = [(r.W1[:, :, c], d["w1"][:, c * P:(c + 1) * P, :].rearrange("e p f -> p e f")) for c in range(NC)]
            r.loads += [(r.W2[:, :, f], d["w2"][:, f * P:(f + 1) * P, :].rearrange("e p n -> p e n"))
                        for f in range(F // P)]
            r.norm = norm_scratch(sb, tag, B * NT)
            r.slot, r.iota = sb(tag + "_slot", [P, NT, B * E]), sb(tag + "_iota", [P, P])
        elif layer == 2:
            E, _, F = d["w1"].shape
            r.kind, r.E, r.EL, r.EW, r.k, r.shared_gate = "top", E, E + 1, E + 1, 2, True
            r.router = [(slice(0, E), by_rows(d["router_w"])), (slice(E, E + 1), by_rows(d["shared_gate_w"]))]
            W1, W2 = sb(tag + "_W1", [P, E, NC, F]), sb(tag + "_W2", [P, E, F // P, D])
            Wg, Wd = sb(tag + "_Wg", [P, NC, 2 * F]), sb(tag + "_Wd", [P, F // P, D])
            r.loads = [(Wg[:], by_rows(d["shared_gate_up"])), (Wd[:], by_rows(d["shared_down"]))]
            for e in range(E):
                r.loads += [(W1[:, e], by_rows(d["w1"][e])), (W2[:, e], by_rows(d["w2"][e]))]
            job(True, F // P, lambda k, f, c: Wg[:, c, k * F + f * P:k * F + (f + 1) * P],
                [(lambda f: Wd[:, f, :], E)])
            for e in range(E):
                job(False, F // P, (lambda k, f, c, e=e: W1[:, e, c, f * P:(f + 1) * P]),
                    [((lambda f, e=e: W2[:, e, f, :]), e)])
        else:
            E, _, F = d["w1"].shape
            r.kind, r.E, r.EL, r.EW, r.k, r.renorm = "top", E, E, E, 4, True
            r.router = [(e, d["gate_w"][e].rearrange("(c p) -> p c", p=P)) for e in range(E)]
            W1, W3, W2 = (sb(f"{tag}_W{n}", shape) for n, shape in
                          (("1", [P, E, NC, F]), ("3", [P, E, NC, F]), ("2", [P, E, D])))
            for c in range(NC):
                r.loads += [(W[:, :, c], d[n][:, c * P:(c + 1) * P, :].rearrange("e p f -> p e f"))
                            for W, n in ((W1, "w1"), (W3, "w3"))]
            r.loads.append((W2[:], d["w2"].rearrange("e p n -> p e n")))
            for e in range(E):
                job(True, 1, (lambda k, f, c, e=e: (W1, W3)[k][:, e, c, :]), [((lambda f, e=e: W2[:, e, :]), e)])
        r.weights = sb(tag + "_weights", [P, NT, B * r.EW])
        routing(nc, g, sem, r)
        if r.kind == "expert_choice":
            choosing_experts(nc, g, sem, r)
        else:
            experts(nc, g, sem, r)


@contextmanager
def stage(nc):
    with ExitStack() as ctx:
        taken = []

        def sem(name):
            taken.append(ctx.enter_context(nc.semaphore(name)))
            return taken[-1]
        yield sem
        with nc.Block() as block:
            @block.sync
            def _(sp):
                for one in taken:
                    sp.sem_clear(one)


def build(nc, dram, out):
    with ExitStack() as ctx:
        sb, _ = allocators(nc, ctx)

        def sem_kept(name):
            return ctx.enter_context(nc.semaphore(name))

        g = Shared()
        g.dram = dram
        g.x = sb("x_all", [P, B * NT, D])
        g.d_ctxT = nc.dram_tensor("ctx_turned", (B, P, NC, S), F32, kind="Internal").ap()
        g.gates, g.tg = sb("gates", [P, 2, 4]), sb("tanh_gates", [P, 2, 4])
        g.ident, g.ones, g.identb = sb("ident", [P, P]), sb("ones", [P, P]), sb("identb", [P, P], BF16)
        prepare(nc, g, sem_kept)
        with stage(nc) as sem:
            channel_attention(nc, g, sem)
        with ExitStack() as l0:
            g.x2 = l0.enter_context(nc.sbuf_tensor("x2_all", [P, B * NT, D], F32))
            d = {k[7:]: v for k, v in dram.items() if k.startswith("L0_ffn_")}
            d.update(cos=dram["rope_cos"], sin=dram["rope_sin"])
            with stage(nc) as sem:
                head_attention(nc, g, sem, "a0", "self", d, 0)
            with stage(nc) as sem:
                moe_layer(nc, g, sem, 0)
        with stage(nc) as sem:
            head_attention(nc, g, sem, "a1", "causal",
                           {"W" + n: dram["L1_xattn_w" + n] for n in "qkvo"}, 1)
        with stage(nc) as sem:
            moe_layer(nc, g, sem, 1)
        with stage(nc) as sem:
            top_attention(nc, g, sem)
        with stage(nc) as sem:
            moe_layer(nc, g, sem, 2)
        with stage(nc) as sem:
            head_attention(nc, g, sem, "a3", "biased",
                           {k[9:]: v for k, v in dram.items() if k.startswith("L3_xattn_")}, 3)
        with stage(nc) as sem:
            moe_layer(nc, g, sem, 3)
        s_out = sem_kept("out_stored")
        with nc.Block() as block:
            @block.sync
            def _(sp):
                sp.dma_start(out.rearrange("b (t p) d -> p (b t) d", p=P), g.x[:]).then_inc(s_out, 16)
                sp.wait_ge(s_out, 16)


def kernel(**inputs):
    import numpy as _np
    import concourse.bacc as _bacc
    from concourse import mybir as _mybir
    from concourse.bass_utils import run_bass_kernel_spmd as _run
    nc = _bacc.Bacc("TRN2", target_bir_lowering=False, num_devices=1)
    arrays, dram = {}, {}
    for name, a in inputs.items():
        a = _np.ascontiguousarray(a)
        arrays["in_" + name] = a
        dram[name] = nc.dram_tensor("in_" + name, a.shape, _mybir.dt.from_np(a.dtype), kind="ExternalInput").ap()
    freq = (1.0 / 10000.0 ** (_np.arange(0, DH, 2, dtype=_np.float32) / DH)).astype(_np.float32)
    angle = _np.arange(S, dtype=_np.float32)[:, None] * freq[None, :]
    sign = _np.tile(_np.array([-1, 1], _np.float32), DH // 2)
    for name, t in (("rope_cos", _np.repeat(_np.cos(angle), 2, 1)), ("rope_sin", _np.repeat(_np.sin(angle), 2, 1) * sign)):
        arrays["in_" + name] = _np.ascontiguousarray(_np.tile(t.T, (P // DH, 1)), dtype=_np.float32)
        dram[name] = nc.dram_tensor("in_" + name, (P, S), F32, kind="ExternalInput").ap()
    out = nc.dram_tensor("out_0", (B, S, D), F32, kind="ExternalOutput").ap()
    build(nc, dram, out)
    r = _run(nc, [arrays], core_ids=[0])
    return r.results[0]["out_0"]
```
